# Optimizing a Trainium2 kernel written in Bass

```python
import numpy as np
import jax
import jax.numpy as jnp

def _softmax(x, axis=-1):
    return jax.nn.softmax(x, axis=axis)

def _gelu(x):
    return jax.nn.gelu(x, approximate=True)

def _silu(x):
    return jax.nn.silu(x)

def _sigmoid(x):
    return jax.nn.sigmoid(x)

def _layernorm(x, axis=-1, eps=1e-05):
    m = jnp.mean(x, axis=axis, keepdims=True)
    v = jnp.var(x, axis=axis, keepdims=True)
    return (x - m) / jnp.sqrt(v + eps)

def _scatter_add(tgt, idx, src, axis=0):
    return tgt.at[idx].add(src)

def _segment_sum(src, seg, n):
    return jax.ops.segment_sum(src, seg, n)
kernel_name = 'mk_gnn_preln_d4_gnn_r64_d9b090'

def setup_inputs(seed: int=0):
    np.random.seed(seed)
    _w = jnp.asarray

    def _rec_inputs():
        import jax
        import jax.numpy as jnp
        _gk = jax.random.key(seed)
        x = -0.0003713 + 1 * jax.random.normal(jax.random.fold_in(_gk, 1), (100000, 128), jnp.float32)
        src = jax.random.randint(jax.random.fold_in(_gk, 2), (25000,), 0, 100000, jnp.int32)
        dst = jax.random.randint(jax.random.fold_in(_gk, 3), (25000,), 0, 100000, jnp.int32)
        _o = jnp.argsort(dst, stable=True)
        src = src[_o]
        dst = dst[_o]
        edge_attr_64 = 0.000155561 + 1.00019 * jax.random.normal(jax.random.fold_in(_gk, 11), (25000, 64), jnp.float32)
        edge_type_8 = jax.random.randint(jax.random.fold_in(_gk, 13), (25000,), 0, 8, jnp.int32)
        return (x, src, dst, edge_attr_64, edge_type_8)
    x, src, dst, edge_attr_64, edge_type_8 = _rec_inputs()

    def _L0_gnn_setup():
        import jax, jax.numpy as jnp
        import numpy as np
        N = 100000
        E = 25000
        F_IN = 128
        C = 32
        H = 4
        NEG_SLOPE = 0.2
        key = jax.random.key(seed)
        ks = jax.random.split(key, 6)
        x = jax.random.normal(ks[0], (N, F_IN), dtype=jnp.float32)
        edge_index = jax.random.randint(ks[1], (2, E), 0, N, dtype=jnp.int32)
        W = jax.random.normal(ks[2], (F_IN, H * C), dtype=jnp.float32) * (1.0 / np.sqrt(F_IN))
        att_src = jax.random.normal(ks[3], (H, C), dtype=jnp.float32) * 0.1
        att_dst = jax.random.normal(ks[4], (H, C), dtype=jnp.float32) * 0.1
        bias = jnp.zeros((H * C,), dtype=jnp.float32)
        return {'x': x, 'edge_index': edge_index, 'W': W, 'att_src': att_src, 'att_dst': att_dst, 'bias': bias}
    _L0_gnn_all = _L0_gnn_setup()
    _L0_gnn_in = {k: v for k, v in _L0_gnn_all.items() if k in ('W', 'att_src', 'att_dst', 'bias')}
    del _L0_gnn_all

    def _L1_gnn_setup():
        import jax, jax.numpy as jnp
        import numpy as np
        N_NODES, N_EDGES = (50000, 9375)
        NODE_DIM, EDGE_DIM = (128, 64)
        H, HD = (4, 32)
        key = jax.random.key(seed)
        k = jax.random.split(key, 6)
        node_features = jax.random.normal(k[0], (N_NODES, NODE_DIM), jnp.float32)
        edge_indices = jax.random.randint(k[1], (2, N_EDGES), 0, N_NODES, jnp.int32)
        edge_features = jax.random.normal(k[2], (N_EDGES, EDGE_DIM), jnp.float32)
        W_node = jax.random.normal(k[3], (H * HD, NODE_DIM), jnp.float32) / np.sqrt(NODE_DIM).astype(np.float32)
        W_edge = jax.random.normal(k[4], (H * HD, EDGE_DIM), jnp.float32) / np.sqrt(EDGE_DIM).astype(np.float32)
        a = jax.random.normal(k[5], (H, 3 * HD), jnp.float32)
        return {'node_features': node_features, 'edge_indices': edge_indices, 'edge_features': edge_features, 'W_node': W_node, 'W_edge': W_edge, 'a': a}
    _L1_gnn_all = _L1_gnn_setup()
    _L1_gnn_in = {k: v for k, v in _L1_gnn_all.items() if k in ('W_node', 'W_edge', 'a')}
    del _L1_gnn_all

    def _L2_gnn_setup():
        import jax, jax.numpy as jnp
        import numpy as np
        LN_EPS = 1e-05
        key = jax.random.key(seed)
        k1, k2, k3, k4, k5 = jax.random.split(key, 5)
        N, E, D, R = (100000, 9375, 128, 8)
        entity_emb = jax.random.normal(k1, (N, D), dtype=jnp.float32)
        edge_index = jax.random.randint(k2, (2, E), 0, N)
        edge_type = jax.random.randint(k3, (E,), 0, R)
        W = jax.random.normal(k4, (R, D, D), dtype=jnp.float32) * (1.0 / np.sqrt(D))
        b = jax.random.normal(k5, (R, D), dtype=jnp.float32) * 0.01
        gamma = jnp.ones((D,), dtype=jnp.float32)
        beta = jnp.zeros((D,), dtype=jnp.float32)
        return {'entity_emb': entity_emb, 'edge_index': edge_index, 'edge_type': edge_type, 'W': W, 'b': b, 'gamma': gamma, 'beta': beta}
    _L2_gnn_all = _L2_gnn_setup()
    _L2_gnn_in = {k: v for k, v in _L2_gnn_all.items() if k in ('W', 'b', 'gamma', 'beta')}
    del _L2_gnn_all

    def _L3_gnn_setup():
        import jax, jax.numpy as jnp
        import numpy as np
        N_NODES = 50000
        N_EDGES = 6250
        D_MODEL = 128
        HEADS = 4
        NEG_SLOPE = 0.2
        LN_EPS = 1e-05

        def _gat_forward(x, edge_index, W, att_src, att_dst, bias):
            N = x.shape[0]
            h = (x @ W).reshape(N, HEADS, D_MODEL)
            a_src = jnp.einsum('nhc,hc->nh', h, att_src)
            a_dst = jnp.einsum('nhc,hc->nh', h, att_dst)
            loop = jnp.arange(N, dtype=edge_index.dtype)
            src = jnp.concatenate([edge_index[0], loop])
            dst = jnp.concatenate([edge_index[1], loop])
            e = jax.nn.leaky_relu(a_src[src] + a_dst[dst], NEG_SLOPE)
            m = jax.ops.segment_max(e, dst, num_segments=N)
            w = jnp.exp(e - m[dst])
            z = jax.ops.segment_sum(w, dst, num_segments=N)
            alpha = w / z[dst]
            msg = h[src] * alpha[:, :, None]
            out = jax.ops.segment_sum(msg, dst, num_segments=N)
            return out.mean(axis=1) + bias
        key = jax.random.key(seed)
        ks = jax.random.split(key, 6)
        x = jax.random.normal(ks[0], (N_NODES, D_MODEL), dtype=jnp.float32)
        edge_index = jax.random.randint(ks[1], (2, N_EDGES), 0, N_NODES, dtype=jnp.int64)
        sc = 1.0 / np.sqrt(D_MODEL)
        W = jax.random.normal(ks[2], (D_MODEL, HEADS * D_MODEL), dtype=jnp.float32) * sc
        att_src = jax.random.normal(ks[3], (HEADS, D_MODEL), dtype=jnp.float32) * sc
        att_dst = jax.random.normal(ks[4], (HEADS, D_MODEL), dtype=jnp.float32) * sc
        bias = jnp.zeros((D_MODEL,), dtype=jnp.float32)
        ln_gamma = jnp.ones((D_MODEL,), dtype=jnp.float32)
        ln_beta = jnp.zeros((D_MODEL,), dtype=jnp.float32)
        return {'x': x, 'edge_index': edge_index, 'W': W, 'att_src': att_src, 'att_dst': att_dst, 'bias': bias, 'ln_gamma': ln_gamma, 'ln_beta': ln_beta}
    _L3_gnn_all = _L3_gnn_setup()
    _L3_gnn_in = {k: v for k, v in _L3_gnn_all.items() if k in ('W', 'att_src', 'att_dst', 'bias', 'ln_gamma', 'ln_beta')}
    del _L3_gnn_all
    return {'x': x, 'src': src, 'dst': dst, 'edge_attr_64': edge_attr_64, 'edge_type_8': edge_type_8, 'L0_gnn_W': _L0_gnn_in['W'], 'L0_gnn_att_src': _L0_gnn_in['att_src'], 'L0_gnn_att_dst': _L0_gnn_in['att_dst'], 'L0_gnn_bias': _L0_gnn_in['bias'], 'L1_gnn_W_node': _L1_gnn_in['W_node'], 'L1_gnn_W_edge': _L1_gnn_in['W_edge'], 'L1_gnn_a': _L1_gnn_in['a'], 'L2_gnn_W': _L2_gnn_in['W'], 'L2_gnn_b': _L2_gnn_in['b'], 'L2_gnn_gamma': _L2_gnn_in['gamma'], 'L2_gnn_beta': _L2_gnn_in['beta'], 'L3_gnn_W': _L3_gnn_in['W'], 'L3_gnn_att_src': _L3_gnn_in['att_src'], 'L3_gnn_att_dst': _L3_gnn_in['att_dst'], 'L3_gnn_bias': _L3_gnn_in['bias'], 'L3_gnn_ln_gamma': _L3_gnn_in['ln_gamma'], 'L3_gnn_ln_beta': _L3_gnn_in['ln_beta']}

def reference(x, src, dst, edge_attr_64, edge_type_8, L0_gnn_W, L0_gnn_att_src, L0_gnn_att_dst, L0_gnn_bias, L1_gnn_W_node, L1_gnn_W_edge, L1_gnn_a, L2_gnn_W, L2_gnn_b, L2_gnn_gamma, L2_gnn_beta, L3_gnn_W, L3_gnn_att_src, L3_gnn_att_dst, L3_gnn_bias, L3_gnn_ln_gamma, L3_gnn_ln_beta):
    import jax
    import jax.numpy as jnp

    def _L0_gnn_ref(x, edge_index, W, att_src, att_dst, bias):
        import jax, jax.numpy as jnp
        import numpy as np
        N = 100000
        E = 25000
        F_IN = 128
        C = 32
        H = 4
        NEG_SLOPE = 0.2
        h = (x @ W).reshape(N, H, C)
        a_src = jnp.einsum('nhc,hc->nh', h, att_src)
        a_dst = jnp.einsum('nhc,hc->nh', h, att_dst)
        src, dst = (edge_index[0], edge_index[1])
        alpha = jax.nn.leaky_relu(a_src[src] + a_dst[dst], NEG_SLOPE)
        amax = jax.ops.segment_max(alpha, dst, num_segments=N)
        amax = jnp.where(jnp.isfinite(amax), amax, 0.0)
        ex = jnp.exp(alpha - amax[dst])
        denom = jax.ops.segment_sum(ex, dst, num_segments=N)
        alpha = ex / (denom[dst] + 1e-16)
        msg = h[src] * alpha[:, :, None]
        out = jax.ops.segment_sum(msg, dst, num_segments=N)
        out = out.reshape(N, H * C) + bias
        return jax.nn.elu(out)

    def _L1_gnn_ref(node_features, edge_indices, edge_features, W_node, W_edge, a):
        import jax, jax.numpy as jnp
        import numpy as np
        N_NODES, N_EDGES = (50000, 9375)
        NODE_DIM, EDGE_DIM = (128, 64)
        H, HD = (4, 32)
        num_nodes = node_features.shape[0]
        num_edges = edge_indices.shape[1]
        h = (node_features @ W_node.T).reshape(num_nodes, H, HD)
        e = (edge_features @ W_edge.T).reshape(num_edges, H, HD)
        src, tgt = (edge_indices[0], edge_indices[1])
        h_src = h[src]
        h_tgt = h[tgt]
        att_in = jnp.concatenate([h_src, h_tgt, e], axis=-1)
        att = jnp.sum(att_in * a, axis=-1)
        att = jnp.where(att > 0, att, 0.2 * att)
        m = jnp.maximum(jax.ops.segment_max(att, tgt, num_segments=num_nodes), 0.0)
        ex = jnp.exp(att - m[tgt])
        ones = jnp.ones((num_edges,), node_features.dtype)
        deg = jax.ops.segment_sum(ones, tgt, num_segments=num_nodes)
        denom = jax.ops.segment_sum(ex, tgt, num_segments=num_nodes) + (num_edges - deg)[:, None] * jnp.exp(-m)
        w = ex / denom[tgt]
        h_prime = jax.ops.segment_sum(w[:, :, None] * h_src, tgt, num_segments=num_nodes)
        return h_prime.reshape(num_nodes, H * HD)

    def _L2_gnn_ref(entity_emb, edge_index, edge_type, W, b, gamma, beta):
        import jax, jax.numpy as jnp
        import numpy as np
        LN_EPS = 1e-05
        src = edge_index[0]
        dst = edge_index[1]
        H = jnp.einsum('nd,rhd->nrh', entity_emb, W)
        msg = H[src, edge_type] + b[edge_type]
        out = jnp.zeros_like(entity_emb).at[dst].add(msg)
        x = out + entity_emb
        mu = jnp.mean(x, axis=-1, keepdims=True)
        var = jnp.mean(jnp.square(x - mu), axis=-1, keepdims=True)
        return (x - mu) * jax.lax.rsqrt(var + LN_EPS) * gamma + beta

    def _L3_gnn_ref(x, edge_index, W, att_src, att_dst, bias, ln_gamma, ln_beta):
        import jax, jax.numpy as jnp
        import numpy as np
        N_NODES = 50000
        N_EDGES = 6250
        D_MODEL = 128
        HEADS = 4
        NEG_SLOPE = 0.2
        LN_EPS = 1e-05

        def _gat_forward(x, edge_index, W, att_src, att_dst, bias):
            N = x.shape[0]
            h = (x @ W).reshape(N, HEADS, D_MODEL)
            a_src = jnp.einsum('nhc,hc->nh', h, att_src)
            a_dst = jnp.einsum('nhc,hc->nh', h, att_dst)
            loop = jnp.arange(N, dtype=edge_index.dtype)
            src = jnp.concatenate([edge_index[0], loop])
            dst = jnp.concatenate([edge_index[1], loop])
            e = jax.nn.leaky_relu(a_src[src] + a_dst[dst], NEG_SLOPE)
            m = jax.ops.segment_max(e, dst, num_segments=N)
            w = jnp.exp(e - m[dst])
            z = jax.ops.segment_sum(w, dst, num_segments=N)
            alpha = w / z[dst]
            msg = h[src] * alpha[:, :, None]
            out = jax.ops.segment_sum(msg, dst, num_segments=N)
            return out.mean(axis=1) + bias
        out = _gat_forward(x, edge_index, W, att_src, att_dst, bias)
        mu = out.mean(axis=-1, keepdims=True)
        var = ((out - mu) ** 2).mean(axis=-1, keepdims=True)
        ln = ln_gamma * (out - mu) * jax.lax.rsqrt(var + LN_EPS) + ln_beta
        return jax.nn.relu(ln) + x
    edge_index = jnp.stack([src, dst])
    h = jnp.maximum(_layernorm(x, axis=-1), 0.0)
    x = x + _L0_gnn_ref(h, edge_index, L0_gnn_W, L0_gnn_att_src, L0_gnn_att_dst, L0_gnn_bias)
    h = jnp.maximum(_layernorm(x, axis=-1), 0.0)
    x = x + _L1_gnn_ref(h, edge_index, edge_attr_64, L1_gnn_W_node, L1_gnn_W_edge, L1_gnn_a)
    h = jnp.maximum(_layernorm(x, axis=-1), 0.0)
    x = x + _L2_gnn_ref(h, edge_index, edge_type_8, L2_gnn_W, L2_gnn_b, L2_gnn_gamma, L2_gnn_beta)
    h = jnp.maximum(_layernorm(x, axis=-1), 0.0)
    x = x + _L3_gnn_ref(h, edge_index, L3_gnn_W, L3_gnn_att_src, L3_gnn_att_dst, L3_gnn_bias, L3_gnn_ln_gamma, L3_gnn_ln_beta)
    return x

_drawn_inputs = setup_inputs


def setup_inputs(seed=0):
    import zlib

    import numpy as np

    out = dict(_drawn_inputs(seed))
    spreads = {'L0_gnn_bias': (0.0, 0.1),
     'L2_gnn_gamma': (1.0, 0.2),
     'L2_gnn_beta': (0.0, 0.1),
     'L3_gnn_bias': (0.0, 0.1),
     'L3_gnn_ln_gamma': (1.0, 0.2),
     'L3_gnn_ln_beta': (0.0, 0.322)}
    factors = {'L0_gnn_att_src': 6.161,
     'L0_gnn_att_dst': 64.0,
     'L2_gnn_b': 23.244,
     'L3_gnn_att_src': 2.695,
     'L3_gnn_att_dst': 21.953}
    for name, (base, spread) in spreads.items():
        noise = np.random.default_rng([zlib.crc32(name.encode()), seed]).standard_normal(out[name].shape)
        drawn = base * np.exp(spread * noise) if base else spread * noise
        out[name] = jnp.asarray(drawn.astype(out[name].dtype))
    for name, factor in factors.items():
        out[name] = (out[name] * factor).astype(out[name].dtype)
    return out
```

```python
import numpy as np
import concourse.bass as bass
from concourse import mybir

F32, I32, BF16 = mybir.dt.float32, mybir.dt.int32, mybir.dt.bfloat16
ALU, ACT = mybir.AluOpType, mybir.ActivationFunctionType

N, E, F = 100000, 25000, 128
P = 128
H, HC = 4, 32
EF = 64
R = 8
EPS = 1e-5
CH = 512
G = CH // P
NCH = -(-E // CH)
EP = NCH * CH
NT = EP // P
PARTS = 32
PL = EP // PARTS
FAR = 200000
BIG = 1.0e30
NDC = -(-N // CH)
LASTROW = (NDC - 1) * CH
TAILP = (LASTROW - (N - CH)) // G
U = 4
LAG = 6


def at_least(eng, sem, value):
    if isinstance(value, int) and value <= 0:
        return
    eng.wait_ge(sem, value)


def settle(eng, turns):
    eng.sem_inc(turns, 1)


def program(nc, x, src, dst, eattr, etype, W0, as0, ad0, b0, W1n, W1e, a1, W2, b2, g2, be2,
            W3, as3, ad3, b3, g3, be3, out, stop=99):
    def dram(name, shape, dt=F32):
        return nc.dram_tensor(name, shape, dt, kind="Internal").ap()

    D0 = dram("D0", (EP, F))
    T2 = dram("T2", (EP + NDC * CH, F + 1))
    T3 = dram("T3", (EP + NDC * CH, F))
    LG = dram("LG", (16, EP))
    AL = dram("AL", (8, EP))
    RSR = dram("RSR", (2, EP))
    CUB = dram("CUB", (1, EP), BF16)
    CUR = dram("CUR", (1, EP))
    CNR = dram("CNR", (1, EP))
    TYR = dram("TYR", (1, EP))
    HDT = dram("HDT", (NCH * P, CH))
    BM = dram("BM", (7 * P, PL))

    sb = nc.alloc_sbuf_tensor
    pb = nc.alloc_psum_tensor

    phase_sems = []

    def lasting(name):
        return nc.alloc_semaphore(name)

    def sem(name):
        phase_sems.append(nc.alloc_semaphore(name))
        return phase_sems[-1]

    def end_phase():
        nc.clear_and_free_semaphores(list(phase_sems))
        phase_sems.clear()
        nc.all_engine_barrier()

    turns = {name: lasting(f"turns_{name}") for name in ("pool", "sync", "vector", "tensor")}

    HT = sb("HT", [P, EP], F32)
    ARENA = sb("ARENA", [P, 10240], F32)
    X = [sb(f"X{i}", [P, G, F + 1], F32) for i in range(4)]
    UU = [sb(f"UU{i}", [P, G, F], F32) for i in range(4)]
    X3 = [sb(f"X3_{i}", [P, G, F], F32) for i in range(4)]
    U3 = [sb(f"U3_{i}", [P, G, F], F32) for i in range(2)]
    U3T = [sb(f"U3T{i}", [P, CH], F32) for i in range(2)]
    O = [sb(f"O{i}", [P, G, F], F32) for i in range(2)]

    ident = sb("ident", [P, P], F32)
    CC = sb("CC", [P, 2 * F], F32)
    CEN = CC[:, 0:F]
    W0s = sb("W0s", [P, F], F32)
    W1T = sb("W1T", [P, F], F32)
    W2T = sb("W2T", [P, R, F], F32)
    W3s = sb("W3s", [P, H, F], F32)
    WW3 = sb("WW3", [P, 2 * F], F32)
    LS = sb("LS", [P, 4, 12], F32)
    LD = sb("LD", [P, 4, 12], F32)
    LE = sb("LE", [EF, 12], F32)
    b2s = sb("b2s", [R, F], F32)
    b0c = sb("b0c", [P, 1], F32)
    b3c = sb("b3c", [P, 1], F32)
    bc3 = sb("bc3", [3, 4 * F], BF16)
    ones3 = sb("ones3", [3, P], BF16)
    onesr = sb("onesr", [1, P], F32)
    c0b = sb("c0b", [P, F], F32)
    g2b = sb("g2b", [P, F], F32)
    be2b = sb("be2b", [P, F], F32)
    be3b = sb("be3b", [P, F], F32)
    epsc = sb("epsc", [P, 2], F32)
    ridx = sb("ridx", [P, 1], F32)
    STS = [sb(f"STS{i}", [P, NT * 6], F32) for i in range(2)]
    MEAN = sb("MEAN", [P, NT], F32)
    RSD = sb("RSD", [P, NT], F32)
    NMR = sb("NMR", [P, NT], F32)
    SRC = sb("SRC", [P, NT], I32)
    SRCF = sb("SRCF", [P, NT], F32)
    GDST = sb("GDST", [P, NT], I32)
    ENDN = sb("ENDN", [P, NT], I32)
    ENDO = sb("ENDO", [P, NT], I32)
    SLOTF = sb("SLOTF", [P, NT], F32)
    IDX2 = sb("IDX2", [P, NT], I32)
    IC = [sb(f"IC{i}", [P, 8], I32) for i in range(2)]
    IT = sb("IT", [P, 8], F32)
    MV = {n: sb(f"MV{n}", [P, 4, G, 2], F32) for n in "xu3z"}
    BN = {n: sb(f"BN{n}", [P, 2, G, 6], F32) for n in "xu3z"}
    SM = {n: sb(f"SM{n}", [P, 4, G], F32) for n in ("nm1", "s2", "sd2", "r2", "nm3", "sg", "r3", "sd5", "r5", "ss5")}
    ERT = sb("ERT", [P, 64], F32)

    BK = [pb(f"BK{i}", [P, CH], F32) for i in range(6)]
    Q = pb("Q", [P, G, 2 * F], F32)

    AR = ARENA[:, :]
    D_flat = AR[0:98, 0:256].bitcast(I32)
    Dn_flat = AR[0:98, 256:512].bitcast(I32)
    Dp_flat = AR[0:98, 512:768].bitcast(I32)
    S_flat = AR[0:98, 768:1024].bitcast(I32)
    Ty_flat = AR[0:98, 1024:1280].bitcast(I32)
    fD, fDn, fDp = AR[0:98, 1280:1536], AR[0:98, 1536:1792], AR[0:98, 1792:2048]
    fS, fTy, cU, cN = (AR[0:98, 2048 + 256 * i:2304 + 256 * i] for i in range(4))
    fG, fO = AR[0:98, 3072:3328], AR[0:98, 3328:3584]
    cUb = AR[0:98, 3584:3712].bitcast(BF16)
    W1ns, W1es = AR[:, 3712:3840], AR[:, 3840:3904]
    W2s = AR[:, 4096:4096 + R * F].rearrange("p (r f) -> p r f", r=R)
    W3T = AR[:, 5120:5120 + H * F].rearrange("p (h f) -> p h f", h=H)
    BK0 = AR[:, 5632:5640]
    BK1 = AR[:, 5640:5652]
    A3c = AR[:, 5652:5660]
    W0T = AR[:, 5660:5788]
    Wm = AR[:, 5788:5916]
    WmT = AR[:, 5916:6044]
    g3b = AR[:, 6044:6172]
    b3m = AR[:, 6172:6300]
    tA, tB = AR[:, 6300:6428], AR[:, 6428:6556]
    SLI = AR[:, 6556:6556 + NT].bitcast(I32)
    FT = AR[:, 6800:6800 + NT]
    RI = AR[:, 7000:7001].bitcast(I32)
    brow, bback = AR[0:1, 7168:7680], AR[0:1, 7680:8192]
    bparts = [AR[0:1, 8192 + 256 * i:8448 + 256 * i].bitcast(BF16) for i in range(3)]

    loads, mem, v, pe, ac, pl, st0 = (sem(n) for n in
        ("set_loads", "set_memset", "set_dve", "set_pe", "set_act", "set_pool", "set_stores"))
    FULLQ = E // 256
    REST = E - FULLQ * 256
    with nc.Block() as block:
        nload = [0]

        @block.sync
        def _(sp):
            def load(dst_ap, src_ap, **kw):
                sp.dma_start(dst_ap, src_ap, **kw).then_inc(loads, 16)
                nload[0] += 16

            sp.wait_ge(mem, 1)
            load(D_flat[0:FULLQ, :], dst[0:FULLQ * 256].rearrange("(q j) -> q j", j=256))
            load(D_flat[FULLQ:FULLQ + 1, 0:REST], dst[FULLQ * 256:E].rearrange("(q j) -> q j", q=1))
            load(S_flat[0:FULLQ, :], src[0:FULLQ * 256].rearrange("(q j) -> q j", j=256))
            load(S_flat[FULLQ:FULLQ + 1, 0:REST], src[FULLQ * 256:E].rearrange("(q j) -> q j", q=1))
            load(Ty_flat[0:FULLQ, :], etype[0:FULLQ * 256].rearrange("(q j) -> q j", j=256))
            load(Ty_flat[FULLQ:FULLQ + 1, 0:REST], etype[FULLQ * 256:E].rearrange("(q j) -> q j", q=1))
            load(Dn_flat[0:FULLQ, :], dst[1:1 + FULLQ * 256].rearrange("(q j) -> q j", j=256))
            load(Dn_flat[FULLQ:FULLQ + 1, 0:REST - 1], dst[FULLQ * 256 + 1:E].rearrange("(q j) -> q j", q=1))
            load(Dp_flat[0:1, 1:256], dst[0:255].rearrange("(q j) -> q j", q=1))
            load(Dp_flat[1:FULLQ, :], dst[255:FULLQ * 256 - 1].rearrange("(q j) -> q j", j=256))
            load(Dp_flat[FULLQ:FULLQ + 1, 0:REST + 1], dst[FULLQ * 256 - 1:E].rearrange("(q j) -> q j", q=1))
            load(W0s[:, :], W0)
            load(W1ns, W1n)
            load(W1es, W1e)
            load(W2s, W2.rearrange("r h d -> h r d"))
            load(W3s[:, :, :], W3.rearrange("f (h c) -> f h c", h=H))
            load(b2s[:, :], b2)
            for h in range(H):
                hp = slice(h * HC, (h + 1) * HC)
                load(BK0[hp, h:h + 1], as0[h, :].rearrange("(c a) -> c a", a=1))
                load(BK0[hp, 4 + h:5 + h], ad0[h, :].rearrange("(c a) -> c a", a=1))
                for part in range(3):
                    load(BK1[hp, 4 * part + h:4 * part + h + 1],
                         a1[h, part * HC:(part + 1) * HC].rearrange("(c a) -> c a", a=1))
                load(A3c[:, h:h + 1], as3[h, :].rearrange("(c a) -> c a", a=1))
                load(A3c[:, 4 + h:5 + h], ad3[h, :].rearrange("(c a) -> c a", a=1))
            for col, row in ((b0c, b0), (b3c, b3)):
                load(col[:, :], row.rearrange("(c a) -> c a", a=1))
            for wide, row in ((c0b[:, :], b0), (g2b[:, :], g2), (be2b[:, :], be2), (be3b[:, :], be3), (g3b, g3)):
                load(wide, row.rearrange("(a c) -> a c", a=1).broadcast_to([P, F]))
            nload.append(nload[0])
            sp.wait_ge(v, 1)
            for row, tile in ((CUB, cUb), (CUR, cU), (CNR, cN), (TYR, fTy)):
                sp.dma_start(row.rearrange("a (q j) -> (a q) j", j=256), tile).then_inc(st0, 16)
            sp.wait_ge(v, 8)
            for part in range(3):
                sp.dma_start(bc3[part:part + 1, :], bparts[part]).then_inc(st0, 16)
            sp.wait_ge(st0, 112)

        @block.gpsimd
        def _(pool):
            pool.memset(ident[:, :], 0.0).then_inc(pl, 1)
            pool.wait_ge(pl, 1)
            pool.affine_select(out=ident[:, :], in_=ident[:, :], compare_op=ALU.not_equal, fill=1.0,
                               base=0, pattern=[[-1, P]], channel_multiplier=1).then_inc(pl, 1)
            pool.iota(SLI, pattern=[[P, NT]], base=0, channel_multiplier=1).then_inc(pl, 1)
            pool.iota(RI, pattern=[[0, 1]], base=0, channel_multiplier=1).then_inc(pl, 1)

        total_loads = 16 * (11 + 6 + H * 7 + 2 + 5)

        @block.vector
        def _(dve):
            n = [0]

            def link(ins):
                n[0] += 1
                ins.then_inc(chain, 1)
                dve.wait_ge(chain, n[0])

            chain = sem("set_chain")
            for tile, value in ((D_flat, N), (Dn_flat, N), (Dp_flat, N), (S_flat, 0), (Ty_flat, 0)):
                link(dve.memset(tile, value))
            link(dve.memset(AR[0:1, 512:513].bitcast(I32), -1))
            link(dve.memset(Dn_flat[96:98, 255:256], -1))
            link(dve.memset(AR[:, 5632:5660], 0.0))
            link(dve.memset(LS[:, :, :], 0.0))
            link(dve.memset(LD[:, :, :], 0.0))
            link(dve.memset(LE[:, :], 0.0))
            link(dve.memset(onesr[:, :], 1.0))
            link(dve.memset(ones3[:, :], 1.0))
            link(dve.memset(epsc[:, 0:1], EPS))
            link(dve.memset(epsc[:, 1:2], EPS * EPS))
            for i in range(4):
                link(dve.memset(X[i][:, :, F:F + 1], -1.0))
            dve.nop().then_inc(mem, 1)
            dve.wait_ge(loads, total_loads)
            for f, i in ((fD, D_flat), (fDn, Dn_flat), (fDp, Dp_flat), (fS, S_flat), (fTy, Ty_flat)):
                link(dve.tensor_copy(f, i))
            link(dve.tensor_tensor(cU, fD, fDp, ALU.is_equal))
            link(dve.tensor_tensor(cN, fD, fDn, ALU.is_equal))
            link(dve.tensor_copy(cUb, cU))
            dve.nop().then_inc(v, 1)
            link(dve.tensor_scalar(fG, fD, float(N - 1), None, ALU.min))
            link(dve.scalar_tensor_tensor(fO, cN, float(FAR), fD, ALU.mult, ALU.add))
            link(dve.tensor_scalar(tA, c0b[:, :], 0.0, None, ALU.min))
            dve.nop().then_inc(v, 1)
            link(dve.tensor_scalar(tB, c0b[:, :], 0.0, -1.0, ALU.max, ALU.add))
            dve.wait_ge(ac, 1)
            link(dve.tensor_tensor(c0b[:, :], tA, tB, ALU.add))
            dve.wait_ge(pl, 4)
            link(dve.tensor_scalar(CEN, ident[:, :], -1.0 / F, None, ALU.add))
            link(dve.tensor_tensor(CC[:, F:2 * F], CEN, g3b, ALU.mult))
            link(dve.tensor_copy(SLOTF[:, :], SLI))
            link(dve.tensor_copy(ridx[:, :], RI))
            link(dve.tensor_tensor(Wm, W3s[:, 0, :], W3s[:, 1, :], ALU.add))
            link(dve.tensor_tensor(Wm, Wm, W3s[:, 2, :], ALU.add))
            link(dve.tensor_tensor(Wm, Wm, W3s[:, 3, :], ALU.add))
            link(dve.tensor_scalar(Wm, Wm, 1.0 / H, None, ALU.mult))
            dve.nop().then_inc(v, 1)
            dve.wait_ge(pe, 1)
            link(dve.tensor_copy(W0T, BK[0][:, 0:P]))
            link(dve.tensor_copy(W1T[:, :], BK[0][:, P:2 * P]))
            link(dve.tensor_copy(WmT, BK[0][:, 2 * P:3 * P]))
            link(dve.tensor_copy(W3T, BK[1][:, :].rearrange("p (h f) -> p h f", h=H)))
            link(dve.tensor_copy(W2T[:, 0:4, :], BK[2][:, :].rearrange("p (h f) -> p h f", h=4)))
            link(dve.tensor_copy(W2T[:, 4:8, :], BK[3][:, :].rearrange("p (h f) -> p h f", h=4)))
            dve.nop().then_inc(v, 1)
            for k, (f, ints, shift) in enumerate(((fS, SRC, 0), (fG, GDST, 0), (fO, ENDO, 0))):
                dve.wait_ge(pe, 2 + k)
                link(dve.tensor_copy(FT.rearrange("p (q two) -> p two q", two=2),
                                     BK[4][:, 0:NT].rearrange("p (two q) -> p two q", two=2)))
                link(dve.tensor_copy(ints[:, :], FT))
                if k == 0:
                    link(dve.tensor_scalar(SRCF[:, :], FT, float(EP + 1), None, ALU.add))
                if k == 2:
                    link(dve.tensor_scalar(FT, FT, float(EP), None, ALU.add))
                    link(dve.tensor_copy(ENDN[:, :], FT))
                dve.nop().then_inc(v, 1)
            dve.wait_ge(pe, 5)
            ps = BK[5]
            link(dve.tensor_copy(LS[:, 0, 0:4], ps[:, 0:4]))
            link(dve.tensor_copy(LD[:, 0, 4:8], ps[:, 4:8]))
            link(dve.tensor_copy(LS[:, 1, 0:4], ps[:, 8:12]))
            link(dve.tensor_copy(LD[:, 1, 4:8], ps[:, 12:16]))
            link(dve.tensor_copy(LE[:, 8:12], ps[0:EF, 16:20]))
            link(dve.tensor_copy(LS[:, 3, 0:4], ps[:, 24:28]))
            link(dve.tensor_copy(LD[:, 3, 8:12], ps[:, 24:28]))
            link(dve.tensor_copy(LD[:, 3, 4:8], ps[:, 28:32]))
            link(dve.tensor_copy(WW3[:, 0:F], ps[:, P:2 * P]))
            link(dve.tensor_tensor(WW3[:, F:2 * F], WW3[:, 0:F], g3b, ALU.mult))
            for i in (0, 2):
                link(dve.tensor_copy(brow[:, i * F:(i + 1) * F], ps[0:1, 2 * P:3 * P]))
                link(dve.tensor_tensor(brow[:, (i + 1) * F:(i + 2) * F], brow[:, i * F:(i + 1) * F], g3b[0:1, :], ALU.mult))
            for part in range(3):
                link(dve.tensor_copy(bparts[part], brow))
                if part < 2:
                    link(dve.tensor_copy(bback, bparts[part]))
                    link(dve.tensor_tensor(brow, brow, bback, ALU.subtract))
            dve.nop().then_inc(v, 1)

        @block.scalar
        def _(act):
            act.wait_ge(v, 2)
            act.activation(tA, tA, ACT.Exp).then_inc(ac, 1)

        @block.tensor
        def _(te):
            te.wait_ge(v, 3)
            te.transpose(BK[0][:, 0:P], W0s[:, :], ident[:, :])
            te.transpose(BK[0][:, P:2 * P], W1ns, ident[:, :])
            te.transpose(BK[0][:, 2 * P:3 * P], Wm, ident[:, :])
            for h in range(H):
                te.transpose(BK[1][:, h * P:(h + 1) * P], W3s[:, h, :], ident[:, :])
            for r in range(R):
                last = te.transpose(BK[2 + r // 4][:, (r % 4) * P:(r % 4 + 1) * P], W2s[:, r, :], ident[:, :])
            last.then_inc(pe, 1)
            te.wait_ge(v, 4)
            for k, f in enumerate((fS, fG, fO)):
                if k:
                    te.wait_ge(v, 4 + k)
                te.transpose(BK[4][:, 0:98], f[:, 0:128], ident[0:98, 0:98])
                te.transpose(BK[4][:, 98:196], f[:, 128:256], ident[0:98, 0:98]).then_inc(pe, 1)
            ps = BK[5]
            te.matmul(ps[:, 0:8], W0T, BK0, start=True, stop=True)
            te.matmul(ps[:, 8:16], W1ns, BK1[:, 0:8], start=True, stop=True)
            te.matmul(ps[0:EF, 16:20], W1es, BK1[:, 8:12], start=True, stop=True)
            for h in range(H):
                te.matmul(ps[:, 24 + h:25 + h], W3T[:, h, :], A3c[:, h:h + 1], start=True, stop=True)
                te.matmul(ps[:, 28 + h:29 + h], W3T[:, h, :], A3c[:, 4 + h:5 + h], start=True, stop=True)
            te.matmul(ps[:, P:2 * P], WmT, CEN, start=True, stop=True)
            te.matmul(ps[0:1, 2 * P:3 * P], b3c[:, :], CEN, start=True, stop=True).then_inc(pe, 1)

    assert nload[1] == total_loads
    end_phase()
    if stop <= 0:
        return

    def chunks(eng, body, peel=1):
        for k in range(peel):
            for j in range(U):
                body(k, j)
        with eng.Fori(peel, NCH // U - 1) as k:
            for j in range(U):
                body(k, j)
        for j in range(U):
            body(NCH // U - 1, j)
        body(NCH // U, 0)

    def sync_wait(sp, sem, value):
        at_least(sp, sem, value)
        if not isinstance(value, int):
            settle(sp, turns["sync"])

    def gate(eng, name, count):
        if not isinstance(count, int):
            settle(eng, turns[name])

    def half(n, k):
        return n % 2, k * 2 + n // 2

    def known(n, k):
        return 4 * k + n if isinstance(k, int) else None

    d_ld = [lasting(f"dense_x_loaded{i}") for i in range(4)]
    (d_bn, d_sq, d_qe, d_agx, d_agu, d_ag3, d_nm1, d_u, d_s2, d_sd2, d_r2, d_t, d_xb, d_x3,
     d_nm3, d_u3, d_sg, d_pt, d_ut, d_q, d_r3, d_xh, d_sd5, d_r5, d_o, d_out) = (lasting(f"dense_{n}") for n in
        ("stats", "q_squares", "q_evacuated", "x_moments", "u_moments", "x3_moments",
         "neg_mean1", "u", "var2", "std2", "rstd2", "t", "xb", "x3", "neg_mean3", "u3", "std3", "transposed",
         "evacuated", "q", "rstd3", "x3_plus_h", "std5", "rstd5", "o", "out"))
    d_x3st = [lasting(f"dense_x3_stored{i}") for i in range(4)]
    d_ost = [lasting(f"dense_out_stored{i}") for i in range(2)]

    def at(ph, j, lag, k):
        n = NCH * ph + j - lag
        if isinstance(k, int):
            d = 4 * k + n
            return 0 <= d < NDC, d, d % 4, d // 4
        return True, k * 4 + n, n % 4, k + n // 4

    def dense_sp(sp, ph, j, k):
        ok, d, s, q = at(ph, j, LAG + 1, k)
        if ok:
            sync_wait(sp, d_out, d + 1)
            if isinstance(d, int) and d == NDC - 1:
                rows = N - d * CH
                sp.dma_start(out[d * CH:N, :].rearrange("(p g) f -> p g f", g=G),
                             O[s % 2][0:rows // G, :, :]).then_inc(d_ost[s % 2], 16)
            else:
                sp.dma_start(out[bass.ds(d * CH, CH), :].rearrange("(p g) f -> p g f", g=G),
                             O[s % 2][:, :, :]).then_inc(d_ost[s % 2], 16)
        ok, d, s, q = at(ph, j, 3, k)
        if ok:
            sync_wait(sp, d_x3, d + 1)
            sp.dma_start(T3[bass.ds(d * CH + EP, CH), :].rearrange("(p g) f -> p g f", g=G), X3[s][:, :, :]).then_inc(d_x3st[s], 16)
        first = isinstance(k, int) and 4 * k + NCH * ph + j == 0
        for lag in ((0, -1) if first else (-1,)):
            ok, d, s, q = at(ph, j, lag, k)
            if ok:
                sync_wait(sp, d_x3, d - 3)
                sp.dma_start(X[s][:, :, :].rearrange("p g f -> p (g f)"),
                             T2[bass.ds(d * CH + EP, CH), :].rearrange("(p g) f -> p (g f)", g=G)).then_inc(d_ld[s], 16)

    def dense_dve(dve, ph, j, k):
        ok6, d6, s6, q6 = at(ph, j, LAG, k)
        ok0, d0, s0, q0 = at(ph, j, 0, k)
        ok1, d1, s1, q1 = at(ph, j, 1, k)
        ok2, d2, s2, q2 = at(ph, j, 2, k)
        ok3, d3, s3, q3 = at(ph, j, 3, k)
        ok4, d4, s4, q4 = at(ph, j, 4, k)
        if ok4:
            dve.wait_ge(d_sg, d4 + 1)
            dve.reciprocal(SM["r3"][:, s4, :], SM["sg"][:, s4, :]).then_inc(d_r3, 1)
        if ok1:
            dve.wait_ge(d_u, d1 + 1)
            for g in range(G):
                last = dve.bn_stats(BN["u"][:, s1 % 2, g, :], UU[s1][:, g, :])
        if ok0:
            dve.wait_ge(d_ld[s0], q0 * 16 + 16)
            for g in range(G):
                last = dve.bn_stats(BN["x"][:, s0 % 2, g, :], X[s0][:, g, 0:F])
        if ok4:
            dve.wait_ge(d_r3, d4 + 1)
            dve.scalar_tensor_tensor(SM["nm3"][:, s4, :], MV["3"][:, s4, :, 0], -1.0, SM["r3"][:, s4, :],
                                     ALU.mult, ALU.mult).then_inc(d_nm3, 1)
        if ok3:
            dve.wait_ge(d_x3, d3 + 1)
            for g in range(G):
                last = dve.bn_stats(BN["3"][:, s3 % 2, g, :], X3[s3][:, g, :])
        if ok0 or ok1 or ok3:
            last.then_inc(d_bn, 1)
        if ok2:
            for g in range(G):
                last = dve.scalar_tensor_tensor(UU[s2][:, g, :], UU[s2][:, g, :], MV["u"][:, s2, g, 0:1],
                                                g2b[:, :], ALU.subtract, ALU.mult)
            last.then_inc(d_t, 1)
        if ok0 or ok1 or ok3:
            dve.wait_ge(d_bn, d0 + 1)
            gate(dve, "vector", d0)
        if ok0:
            for g in range(G):
                last = dve.bn_aggr(MV["x"][:, s0, g, :], BN["x"][:, s0 % 2, g, :])
            last.then_inc(d_agx, 1)
        if ok1:
            for g in range(G):
                last = dve.bn_aggr(MV["u"][:, s1, g, :], BN["u"][:, s1 % 2, g, :])
            last.then_inc(d_agu, 1)
        if ok3:
            for g in range(G):
                last = dve.bn_aggr(MV["3"][:, s3, g, :], BN["3"][:, s3 % 2, g, :])
            last.then_inc(d_ag3, 1)
        if ok0:
            dve.wait_ge(d_agx, d0 + 1)
            dve.tensor_scalar(SM["nm1"][:, s0, :], MV["x"][:, s0, :, 0], -1.0, None, ALU.mult).then_inc(d_nm1, 1)
        if ok2:
            dve.wait_ge(d_sd2, d2 + 1)
            dve.reciprocal(SM["r2"][:, s2, :], SM["sd2"][:, s2, :]).then_inc(d_r2, 1)
        if ok6:
            dve.wait_ge(d_sd5, d6 + 1)
            dve.reciprocal(SM["r5"][:, s6, :], SM["sd5"][:, s6, :]).then_inc(d_r5, 1)
        if ok1:
            dve.wait_ge(d_agu, d1 + 1)
            dve.scalar_tensor_tensor(SM["s2"][:, s1, :], MV["x"][:, s1, :, 1], EPS, MV["u"][:, s1, :, 1],
                                     ALU.mult, ALU.add).then_inc(d_s2, 1)
        if ok6:
            o = O[s6 % 2]
            dve.wait_ge(d_r5, d6 + 1)
            for g in range(G):
                last = dve.scalar_tensor_tensor(o[:, g, :], o[:, g, :], SM["r5"][:, s6, g:g + 1],
                                                be3b[:, :], ALU.mult, ALU.add)
            last.then_inc(d_o, 1)
            dve.wait_ge(d_o, d6 + 1)
            dve.wait_ge(d_xh, d6 + 1)
            dve.scalar_tensor_tensor(o[:, :, :], o[:, :, :], 0.0, X3[s6][:, :, :], ALU.max, ALU.add).then_inc(d_out, 1)
        if ok2:
            at_least(dve, d_x3st[s2], q2 * 16)
            at_least(dve, d_out, d2 - 3)
            dve.wait_ge(d_t, d2 + 1)
            dve.wait_ge(d_r2, d2 + 1)
            dve.wait_ge(d_xb, d2 + 1)
            for g in range(G):
                last = dve.scalar_tensor_tensor(X3[s2][:, g, :], UU[s2][:, g, :], SM["r2"][:, s2, g:g + 1],
                                                X[s2][:, g, 0:F], ALU.mult, ALU.add)
            last.then_inc(d_x3, 1)

    def dense_pool(pool, ph, j, k):
        ok1, d1, s1, q1 = at(ph, j, 1, k)
        ok5, d5, s5, q5 = at(ph, j, 5, k)
        if ok1:
            pool.wait_ge(d_u, d1 + 1)
            x = X[s1][:, :, 0:F]
            pool.tensor_tensor(x, x, be2b[:, :].unsqueeze(1).broadcast_to([P, G, F]), ALU.add).then_inc(d_xb, 1)
        if ok5:
            pool.wait_ge(d_x3st[s5], q5 * 16 + 16)
            pool.wait_ge(d_u3, d5 + 1)
            x3 = X3[s5][:, :, :]
            pool.tensor_tensor(x3, x3, U3[s5 % 2][:, :, :], ALU.add).then_inc(d_xh, 1)

    def dense_act(act, ph, j, k):
        ok5, d5, s5, q5 = at(ph, j, 5, k)
        ok4, d4, s4, q4 = at(ph, j, 4, k)
        ok0, d0, s0, q0 = at(ph, j, 0, k)
        ok1, d1, s1, q1 = at(ph, j, 1, k)
        ok3, d3, s3, q3 = at(ph, j, 3, k)
        if ok5:
            at_least(act, d_q, d5 - 1)
            act.wait_ge(d_pt, d5 + 1)
            act.activation(U3T[s5 % 2][:, :], BK[5][:, :], ACT.Copy).then_inc(d_ut, 1)
        if ok4:
            act.wait_ge(d_nm3, d4 + 1)
            at_least(act, d_xh, d4 - 1)
            for g in range(G):
                last = act.activation(U3[s4 % 2][:, g, :], X3[s4][:, g, :], ACT.Relu, bias=SM["nm3"][:, s4, g:g + 1],
                                      scale=SM["r3"][:, s4, g:g + 1])
            last.then_inc(d_u3, 1)
        if ok0:
            act.wait_ge(d_nm1, d0 + 1)
            at_least(act, d_x3, d0 - 3)
            for g in range(G):
                last = act.activation(UU[s0][:, g, :], X[s0][:, g, 0:F], ACT.Relu, bias=SM["nm1"][:, s0, g:g + 1])
            last.then_inc(d_u, 1)
        if ok3:
            act.wait_ge(d_ag3, d3 + 1)
            act.activation(SM["sg"][:, s3, :], MV["3"][:, s3, :, 1], ACT.Sqrt, bias=epsc[:, 0:1]).then_inc(d_sg, 1)
        if ok5:
            act.wait_ge(d_q, d5 + 1)
            for g in range(G):
                last = act.activation(Q[:, g, 0:F], Q[:, g, 0:F], ACT.Square, accum_out=SM["ss5"][:, s5, g:g + 1])
            last.then_inc(d_sq, 1)
            at_least(act, d_ost[s5 % 2], ((d5 // 2) if isinstance(d5, int) else q5 * 2 + s5 // 2) * 16)
            act.activation(O[s5 % 2][:, :, :], Q[:, :, F:2 * F], ACT.Copy).then_inc(d_qe, 1)
        if ok1:
            act.wait_ge(d_s2, d1 + 1)
            act.activation(SM["sd2"][:, s1, :], SM["s2"][:, s1, :], ACT.Sqrt, bias=epsc[:, 1:2]).then_inc(d_sd2, 1)
        if ok5:
            act.wait_ge(d_sq, d5 + 1)
            act.activation(SM["sd5"][:, s5, :], SM["ss5"][:, s5, :], ACT.Sqrt, bias=epsc[:, 0:1],
                           scale=1.0 / F).then_inc(d_sd5, 1)

    def bias_rows(te, q):
        for half_q in range(2):
            te.matmul(q[:, 2 * half_q:2 * half_q + 2, :], ones3[:, :], bc3[:, :], start=True, stop=False)

    def dense_pe_q(te, ph, j, k):
        ok5, d5, s5, q5 = at(ph, j, 5, k)
        if ok5:
            te.wait_ge(d_ut, d5 + 1)
            at_least(te, d_qe, d5)
            bias_rows(te, Q)
            for g in range(G):
                last = te.matmul(Q[:, g, :], U3T[s5 % 2][:, g * P:(g + 1) * P], WW3[:, :], start=False, stop=g % 2 == 1)
            last.then_inc(d_q, 1)

    def dense_pe_t(te, ph, j, k):
        ok4, d4, s4, q4 = at(ph, j, 4, k)
        if ok4:
            te.wait_ge(d_u3, d4 + 1)
            at_least(te, d_ut, d4)
            for g in range(G):
                last = te.transpose(BK[5][:, g * P:(g + 1) * P], U3[s4 % 2][:, g, :], ident[:, :])
            last.then_inc(d_pt, 1)

    def phase_a(l, ph):
        W = F + 1 if l in (1, 2) else F
        a = [0]

        def take(cols, parts=P):
            v = ARENA[0:parts, a[0]:a[0] + cols]
            a[0] += cols
            return v

        SW = F + 1 if l in (1, 2) else F
        SR = [take(G * SW).rearrange("p (g f) -> p g f", f=SW) for _ in range(2)]
        DR = [take(G * SW).rearrange("p (g f) -> p g f", f=SW) for _ in range(2)]
        XTS, XTD = take(CH), take(CH)
        UDT = [take(CH) for _ in range(2)]
        LGS = [take(CH, 12) for _ in range(2)]
        if l == 1:
            EA = [take(G * EF).rearrange("p (g f) -> p g f", f=EF) for _ in range(2)]
            EAT = take(CH, EF)
        assert a[0] <= 10240
        logits = l != 2

        def pair(name):
            return [sem(f"a{l}_{name}{i}") for i in range(2)]

        s_ld, d_ldr, st_d0, st_lg, st_hd, e_ld = (pair(n) for n in
            ("s_rows", "d_rows", "d0_stored", "logits_stored", "ud_stored", "edges_loaded"))
        (s_tr, d_tr, e_tr, s_xt, d_xt, e_xt, s_cen, d_cen, s_u, d_u_, lg_pe, lg_ev, s_st, d_st, ic, fl) = (
            sem(f"a{l}_{n}") for n in ("s_transposed", "d_transposed", "e_transposed", "s_evacuated", "d_evacuated",
                "e_evacuated", "s_centred", "d_centred", "s_u", "d_u", "logits", "logits_evacuated", "s_stats",
                "d_stats", "index_columns", "flag_bias"))
        x_ld = [sem(f"a{l}_x_loaded{i}") for i in range(4)]
        x_st = [sem(f"a{l}_x_stored{i}") for i in range(4)]
        x_add = sem(f"a{l}_x_added")
        source = {0: x, 1: T2, 2: T2, 3: T3}[l]
        index = {0: SRC, 1: SRC, 2: IDX2, 3: IDX2}[l]
        dsrc = {1: T2, 2: T2, 3: T3}.get(l)

        with nc.Block() as block:
            @block.gpsimd
            def _(pool):
                def body(k, j):
                    b, q = half(j, k)
                    c = k * 4 + j
                    at_least(pool, s_tr, c - 1)
                    at_least(pool, s_st, c - 1)
                    if l == 0:
                        at_least(pool, d_tr, c - 1)
                        at_least(pool, d_st, c - 1)
                        at_least(pool, st_d0[b], q * 16)
                    pool.tensor_copy(IC[b][:, 0:4], index[:, bass.ds(c * G, G)]).then_inc(ic, 1)
                    if l == 0:
                        pool.tensor_copy(IC[b][:, 4:8], GDST[:, bass.ds(c * G, G)]).then_inc(ic, 1)
                    pool.wait_ge(ic, (c + 1) * (2 if l == 0 else 1))
                    settle(pool, turns["pool"])
                    for g in range(G):
                        pool.indirect_dma_start(
                            out=SR[b][:, g, :], out_offset=None, in_=source,
                            in_offset=bass.IndirectOffsetOnAxis(ap=IC[b][:, g:g + 1], axis=0),
                            element_offset=0).then_inc(s_ld[b], 16)
                    if l == 0:
                        for g in range(G):
                            pool.indirect_dma_start(
                                out=DR[b][:, g, :], out_offset=None, in_=source,
                                in_offset=bass.IndirectOffsetOnAxis(ap=IC[b][:, 4 + g:5 + g], axis=0)).then_inc(d_ldr[b], 16)
                    if ph is not None:
                        dense_pool(pool, ph, j, k)

                chunks(pool, body, 2 if ph == 0 else 1)

            @block.sync
            def _(sp):
                def loads(n, k):
                    b, q = half(n, k)
                    c = k * 4 + n
                    if l:
                        if logits:
                            sync_wait(sp, d_tr, c - 1)
                        sync_wait(sp, d_st, c - 1)
                        sp.dma_start(DR[b][:, :, :], dsrc[bass.ds(c * CH, CH), :].rearrange("(g p) f -> p g f", p=P)).then_inc(d_ldr[b], 16)
                    if l == 1:
                        sync_wait(sp, e_tr, c - 1)
                        if isinstance(c, int) and c == NCH - 1:
                            rest = E - c * CH
                            full = rest // P
                            sp.dma_start(EA[b][:, 0:full, :], eattr[c * CH:c * CH + full * P, :].rearrange("(g p) f -> p g f", p=P)).then_inc(e_ld[b], 16)
                            sp.dma_start(EA[b][:, full:G, :], eattr[0:(G - full) * P, :].rearrange("(g p) f -> p g f", p=P)).then_inc(e_ld[b], 16)
                            sync_wait(sp, e_ld[b], q * 16 + 32)
                            sp.dma_start(EA[b][0:rest - full * P, full, :], eattr[c * CH + full * P:E, :]).then_inc(e_ld[b], 16)
                        else:
                            sp.dma_start(EA[b][:, :, :], eattr[bass.ds(c * CH, CH), :].rearrange("(g p) f -> p g f", p=P)).then_inc(e_ld[b], 16)

                def body(k, j):
                    b, q = half(j, k)
                    c = k * 4 + j
                    first = isinstance(c, int) and c == 0
                    last = isinstance(c, int) and c == NCH - 1
                    if first:
                        loads(0, 0)
                    if not last:
                        loads(j + 1, k)
                    if l == 0:
                        if first:
                            for i in range(3):
                                sp.dma_start(X[i][:, :, 0:F], x[i * CH:(i + 1) * CH, :].rearrange("(p g) f -> p g f", g=G)).then_inc(x_ld[i], 16)
                        sync_wait(sp, x_st[3], c * 16)
                        if last:
                            row = (NDC - 1) * CH
                            sp.dma_start(X[3][0:(N - row) // G, :, 0:F], x[row:N, :].rearrange("(p g) f -> p g f", g=G)).then_inc(x_ld[3], 16)
                        else:
                            sp.dma_start(X[3][:, :, 0:F], x[bass.ds((c * 4 + 3) * CH, CH), :].rearrange("(p g) f -> p g f", g=G)).then_inc(x_ld[3], 16)
                        for i in range(4):
                            sync_wait(sp, x_add, c * 4 + (i + 1))
                            sp.dma_start(T2[bass.ds((c * 4 + i) * CH + EP, CH), :].rearrange("(p g) f -> p (g f)", g=G),
                                         X[i][:, :, :].rearrange("p g f -> p (g f)")).then_inc(x_st[i], 16)
                        sync_wait(sp, d_ldr[b], (q + 1) * 64)
                        sp.dma_start(D0[bass.ds(c * CH, CH), :].rearrange("(g p) f -> p g f", p=P), DR[b][:, :, :]).then_inc(st_d0[b], 16)
                        if not last:
                            for i in range(3):
                                sync_wait(sp, x_st[i], c * 16 + 16)
                                sp.dma_start(X[i][:, :, 0:F], x[bass.ds((c * 4 + 4 + i) * CH, CH), :].rearrange("(p g) f -> p g f", g=G)).then_inc(x_ld[i], 16)
                    if ph is not None:
                        dense_sp(sp, ph, j, k)
                    if not first:
                        store(j - 1, k)

                def store(n, k):
                    b, q = half(n, k)
                    c = k * 4 + n
                    if logits:
                        sync_wait(sp, lg_ev, c + 1)
                        sp.dma_start(LG[0:12, bass.ds(c * CH, CH)], LGS[b][:, :]).then_inc(st_lg[b], 16)
                    if l == 3:
                        sync_wait(sp, d_u_, c + 1)
                        sp.dma_start(HDT[bass.ds(c * P, P), :], UDT[b][:, :]).then_inc(st_hd[b], 16)

                chunks(sp, body, 2 if ph == 0 else 1)
                store(0, NCH // U)
                n0, n1 = (NCH + 1) // 2, NCH // 2
                for sems, used in ((st_d0, l == 0), (st_lg, logits), (st_hd, l == 3)):
                    if used:
                        sync_wait(sp, sems[0], 16 * n0)
                        sync_wait(sp, sems[1], 16 * n1)
                if l == 0:
                    for i in range(4):
                        sync_wait(sp, x_st[i], 16 * NCH)

            @block.vector
            def _(dve):
                def body(k, j):
                    b, q = half(j, k)
                    c = k * 4 + j
                    if l == 0:
                        for i in range(4):
                            dve.wait_ge(x_ld[i], c * 16 + 16)
                            dve.tensor_tensor(X[i][:, :, 0:F], X[i][:, :, 0:F],
                                              c0b[:, :].unsqueeze(1).broadcast_to([P, G, F]), ALU.add).then_inc(x_add, 1)
                    dve.wait_ge(d_ldr[b], (q + 1) * (64 if l == 0 else 16))
                    for g in range(G):
                        last = dve.bn_stats(STS[1][:, bass.ds(c * (G * 6) + g * 6, 6)], DR[b][:, g, 0:F])
                    last.then_inc(d_st, 1)
                    if ph is not None:
                        dense_dve(dve, ph, j, k)
                    dve.wait_ge(s_ld[b], (q + 1) * 64)
                    if l == 1:
                        dve.scalar_tensor_tensor(IT[:, 0:4], SR[b][:, :, F], 0.0, SRCF[:, bass.ds(c * G, G)],
                                                 ALU.is_lt, ALU.mult).then_inc(fl, 1)
                    for g in range(G):
                        last = dve.bn_stats(STS[0][:, bass.ds(c * (G * 6) + g * 6, 6)], SR[b][:, g, 0:F])
                    if l == 1:
                        dve.wait_ge(fl, c + 1)
                        last = dve.tensor_tensor(IDX2[:, bass.ds(c * G, G)], IT[:, 0:4], SR[b][:, :, F], ALU.add)
                    last.then_inc(s_st, 1)

                chunks(dve, body, 2 if ph == 0 else 1)

            @block.scalar
            def _(act):
                def body(k, j):
                    b, q = half(j, k)
                    c = k * 4 + j
                    if logits:
                        act.wait_ge(d_tr, c + 1)
                        at_least(act, d_cen, c)
                        act.activation(XTD, BK[1][:, :], ACT.Copy).then_inc(d_xt, 1)
                    act.wait_ge(s_tr, c + 1)
                    at_least(act, s_cen, c)
                    act.activation(XTS, BK[0][:, :], ACT.Copy).then_inc(s_xt, 1)
                    if l == 1:
                        act.wait_ge(e_tr, c + 1)
                        at_least(act, lg_pe, c)
                        act.activation(EAT, BK[1][0:EF, :], ACT.Copy).then_inc(e_xt, 1)
                    if ph is not None:
                        dense_act(act, ph, j, k)
                    act.wait_ge(s_cen, c + 1)
                    act.activation(HT[:, bass.ds(c * CH, CH)], BK[2][:, :], ACT.Relu).then_inc(s_u, 1)
                    if logits:
                        act.wait_ge(d_cen, c + 1)
                        at_least(act, lg_pe, c - 1)
                        if l == 3:
                            at_least(act, st_hd[b], q * 16)
                        act.activation(UDT[b], BK[2][:, :], ACT.Relu).then_inc(d_u_, 1)
                        act.wait_ge(lg_pe, c + 1)
                        at_least(act, st_lg[b], q * 16)
                        act.activation(LGS[b], BK[3][0:12, :], ACT.Copy).then_inc(lg_ev, 1)

                chunks(act, body, 2 if ph == 0 else 1)

            @block.tensor
            def _(te):
                def body(k, j):
                    b, q = half(j, k)
                    c = k * 4 + j
                    if logits:
                        te.wait_ge(d_ldr[b], (q + 1) * (64 if l == 0 else 16))
                        at_least(te, d_xt, c)
                        if l == 1:
                            at_least(te, e_xt, c)
                        for g in range(G):
                            last = te.transpose(BK[1][:, g * P:(g + 1) * P], DR[b][:, g, 0:F], ident[:, :])
                        last.then_inc(d_tr, 1)
                    te.wait_ge(s_ld[b], (q + 1) * 64)
                    at_least(te, s_xt, c)
                    for g in range(G):
                        last = te.transpose(BK[0][:, g * P:(g + 1) * P], SR[b][:, g, 0:F], ident[:, :])
                    last.then_inc(s_tr, 1)
                    if l == 1:
                        te.wait_ge(e_ld[b], (q + 1) * 16 if not (isinstance(c, int) and c == NCH - 1) else q * 16 + 48)
                        te.wait_ge(d_xt, c + 1)
                        gate(te, "tensor", c)
                        for g in range(G):
                            last = te.transpose(BK[1][0:EF, g * P:(g + 1) * P], EA[b][:, g, :], ident[:, :])
                        last.then_inc(e_tr, 1)
                    if ph is not None:
                        dense_pe_q(te, ph, j, k)
                    te.wait_ge(s_xt, c + 1)
                    if logits:
                        at_least(te, d_u_, c)
                    else:
                        at_least(te, s_u, c)
                    te.matmul(BK[2][:, :], CEN, XTS, start=True, stop=True).then_inc(s_cen, 1)
                    if ph is not None:
                        dense_pe_t(te, ph, j, k)
                    if logits:
                        te.wait_ge(d_xt, c + 1)
                        te.wait_ge(s_u, c + 1)
                        te.matmul(BK[2][:, :], CEN, XTD, start=True, stop=True).then_inc(d_cen, 1)
                        te.wait_ge(d_u_, c + 1)
                        at_least(te, lg_ev, c)
                        te.matmul(BK[3][0:12, :], LS[:, l, :], HT[:, bass.ds(c * CH, CH)], start=True, stop=False)
                        if l == 1:
                            te.wait_ge(e_xt, c + 1)
                            gate(te, "tensor", c)
                            te.matmul(BK[3][0:12, :], LE[:, :], EAT, start=False, stop=False)
                        te.matmul(BK[3][0:12, :], LD[:, l, :], UDT[b], start=False, stop=True).then_inc(lg_pe, 1)

                chunks(te, body, 2 if ph == 0 else 1)

    phase_a(0, None)
    end_phase()
    if stop <= 1:
        return

    BT = [ARENA[:, i * PL:(i + 1) * PL] for i in range(13)]
    BU, BNX, PF, PFN, PB, NEGU = BT[0:6]
    t = BT[6:12]
    ROW = BT[12]
    rU, rN, rB = (ROW[0:1, i * P:(i + 1) * P] for i in range(3))
    roww = ROW[0:1, 3 * P:4 * P + 1]
    KCOL = ROW[:, 720:721]
    BMR = dram("BMR", (1, 3 * P))
    STAT = [ARENA[:, 10 * PL + i * NT:10 * PL + (i + 1) * NT] for i in range(2)]
    SROW = ARENA[0:98, 11 * PL:11 * PL + 2 * P]

    def by_part(row):
        return row.rearrange("a (c n) -> (a c) n", n=PL)

    class Scans:

        def __init__(self, dve, name):
            self.dve, self.n, self.i = dve, 0, 0
            self.steps, self.part_ready, self.row_out, self.row_ready, self.col_out = SEMS[name]

        def link(self, ins):
            self.n += 1
            ins.then_inc(self.steps, 1)
            self.dve.wait_ge(self.steps, self.n)

        def tt(self, o, a, b, op):
            self.link(self.dve.tensor_tensor(o, a, b, op))

        def ts(self, o, a, s1, s2, op0, op1=None):
            self.link(self.dve.tensor_scalar(o, a, s1, s2, op0) if op1 is None
                      else self.dve.tensor_scalar(o, a, s1, s2, op0, op1))

        def stt(self, o, a, s, b, op0, op1):
            self.link(self.dve.scalar_tensor_tensor(o, a, s, b, op0, op1))

        def carry(self, tile, mask, mrow, fwd, op0, op1):
            dve, i = self.dve, self.i
            self.i += 1
            self.link(dve.memset(roww[:, 0:1] if fwd else roww[:, P:P + 1], 0.0))
            dve.nop().then_inc(self.part_ready, 1)
            dve.wait_ge(self.row_out, i + 1)
            if fwd:
                self.link(dve.tensor_tensor_scan(roww[:, 1:P + 1], mrow, BK[0][0:1, 0:P], 0.0, op0, op1))
            else:
                self.link(dve.tensor_tensor_scan(roww[:, 0:P][:, ::-1], mrow[:, ::-1], BK[0][0:1, 0:P][:, ::-1], 0.0, op0, op1))
            dve.nop().then_inc(self.row_ready, 1)
            dve.wait_ge(self.col_out, i + 1)
            self.link(dve.tensor_copy(KCOL, BK[1][:, 0:1]))
            self.stt(tile, mask, KCOL, tile, op0, op1)

        def run_sum(self, tile):
            self.link(self.dve.tensor_tensor_scan(tile, BU, tile, 0.0, ALU.mult, ALU.add))
            self.carry(tile, PF, rU, True, ALU.mult, ALU.add)

        def run_max(self, tile):
            self.link(self.dve.tensor_tensor_scan(tile, NEGU, tile, -BIG, ALU.add, ALU.max))
            self.carry(tile, PFN, rN, True, ALU.add, ALU.max)

        def spread(self, tile):
            self.stt(t[5], BNX, -1.0, tile, ALU.mult, ALU.mult)
            self.tt(tile, tile, t[5], ALU.add)
            self.link(self.dve.tensor_tensor_scan(tile[:, ::-1], BNX[:, ::-1], tile[:, ::-1], 0.0, ALU.mult, ALU.add))
            self.carry(tile, PB, rB, False, ALU.mult, ALU.add)

    SEMS = {}

    def scan_sems(name):
        SEMS[name] = [sem(f"{name}_{s}") for s in ("steps", "part_ready", "row_out", "row_ready", "col_out")]
        return SEMS[name]

    def carries_on_tensor(te, name, tiles):
        _, part_ready, row_out, row_ready, col_out = SEMS[name]
        for i, (tile, fwd) in enumerate(tiles):
            col = PL - 1 if fwd else 0
            te.wait_ge(part_ready, i + 1)
            te.matmul(BK[0][0:1, 0:P], tile[:, col:col + 1], ident[:, :], start=True, stop=True).then_inc(row_out, 1)
            te.wait_ge(row_ready, i + 1)
            te.matmul(BK[1][:, 0:1], roww[:, 0:P] if fwd else roww[:, 1:P + 1], onesr[0:1, 0:1],
                      start=True, stop=True).then_inc(col_out, 1)

    def masks():
        scan_sems("masks")
        ld, st, rows, made = (sem(f"masks_{n}") for n in ("loaded", "stored", "rows", "made"))
        with nc.Block() as block:
            @block.sync
            def _(sp):
                for h in range(H):
                    sp.dma_start(BU[h * PARTS:(h + 1) * PARTS, :], by_part(CUR)).then_inc(ld, 16)
                    sp.dma_start(BNX[h * PARTS:(h + 1) * PARTS, :], by_part(CNR)).then_inc(ld, 16)
                sp.wait_ge(made, 1)
                sp.dma_start(BM[0:6 * P, :].rearrange("(i p) n -> p i n", p=P),
                             ARENA[:, 0:6 * PL].rearrange("p (i n) -> p i n", n=PL)).then_inc(st, 16)
                sp.dma_start(BMR, ROW[0:1, 0:3 * P]).then_inc(st, 16)
                sp.wait_ge(made, 2)
                sp.dma_start(BM[6 * P:7 * P, :], t[0]).then_inc(st, 16)
                sp.wait_ge(st, 48)

            @block.vector
            def _(dve):
                s = Scans(dve, "masks")
                dve.wait_ge(ld, 128)
                s.link(dve.tensor_tensor_scan(PF, BU, BU, 1.0, ALU.mult, ALU.min))
                s.link(dve.tensor_tensor_scan(PB[:, ::-1], BNX[:, ::-1], BNX[:, ::-1], 1.0, ALU.mult, ALU.min))
                s.ts(PFN, PF, -1.0, BIG, ALU.add, ALU.mult)
                s.ts(NEGU, BU, -1.0, BIG, ALU.add, ALU.mult)
                dve.nop().then_inc(rows, 1)
                dve.wait_ge(rows, 4)
                for i, row in enumerate((rU, rN, rB)):
                    s.link(dve.tensor_copy(row, BK[2][0:1, i * P:(i + 1) * P]))
                dve.nop().then_inc(made, 1)
                s.link(dve.memset(t[0], 1.0))
                s.run_sum(t[0])
                s.spread(t[0])
                s.ts(t[0], t[0], -1.0, float(E), ALU.mult, ALU.add)
                dve.nop().then_inc(made, 1)

            @block.tensor
            def _(te):
                te.wait_ge(rows, 1)
                for i, (tile, col) in enumerate(((PF, PL - 1), (PFN, PL - 1), (PB, 0))):
                    te.matmul(BK[2][0:1, i * P:(i + 1) * P], tile[:, col:col + 1], ident[:, :],
                              start=True, stop=True).then_inc(rows, 1)
                carries_on_tensor(te, "masks", [(t[0], True), (t[0], False)])

    def stats(l):
        steps, std_in, std_out, col_in, col_out, row_in, st, ld = (sem(f"stats{l}_{n}") for n in
            ("steps", "var_ready", "std_ready", "rstd_ready", "turned", "row_ready", "stored", "loaded"))
        with nc.Block() as block:
            @block.vector
            def _(dve):
                n = [0]

                def link(ins):
                    n[0] += 1
                    ins.then_inc(steps, 1)
                    dve.wait_ge(steps, n[0])

                for side in range(2):
                    s6 = STS[side][:, :].rearrange("p (t k) -> p t k", k=6)
                    a, b = STAT
                    link(dve.tensor_tensor(a, s6[:, :, 1], s6[:, :, 4], ALU.subtract))
                    link(dve.tensor_tensor(b, s6[:, :, 2], s6[:, :, 5], ALU.add))
                    link(dve.scalar_tensor_tensor(a, a, 0.25, a, ALU.mult, ALU.mult))
                    link(dve.scalar_tensor_tensor(b, b, 1.0 / F, a, ALU.mult, ALU.add))
                    dve.nop().then_inc(std_in, 1)
                    dve.wait_ge(std_out, side + 1)
                    link(dve.reciprocal(RSD[:, :], b))
                    dve.nop().then_inc(col_in, 1)
                    dve.wait_ge(col_out, side + 1)
                    if side:
                        dve.wait_ge(st, 32)
                    link(dve.tensor_copy(SROW, BK[1][0:98, 0:2 * P]))
                    dve.nop().then_inc(row_in, 1)
                if l in (2, 3):
                    link(dve.tensor_tensor(MEAN[:, :], s6[:, :, 1], s6[:, :, 4], ALU.add))
                    link(dve.scalar_tensor_tensor(NMR[:, :], MEAN[:, :], -0.5, RSD[:, :], ALU.mult, ALU.mult))
                if l == 0:
                    link(dve.tensor_scalar(STAT[0], SRCF[:, :], -1.0, None, ALU.add))
                    link(dve.tensor_copy(SRC[:, :], STAT[0]))

            @block.scalar
            def _(act):
                for side in range(2):
                    act.wait_ge(std_in, side + 1)
                    act.activation(STAT[1], STAT[1], ACT.Sqrt, bias=epsc[:, 0:1]).then_inc(std_out, 1)

            @block.tensor
            def _(te):
                for side in range(2):
                    te.wait_ge(col_in, side + 1)
                    te.transpose(BK[1][0:98, 0:P], RSD[:, 0:98], ident[:, :])
                    te.transpose(BK[1][0:98, P:2 * P], RSD[:, 98:196], ident[:, :]).then_inc(col_out, 1)

            @block.sync
            def _(sp):
                if l != 2:
                    sp.dma_start(ARENA[:, 0:6 * PL].rearrange("p (i n) -> p i n", n=PL),
                                 BM[0:6 * P, :].rearrange("(i p) n -> p i n", p=P)).then_inc(ld, 16)
                    sp.dma_start(ROW[0:1, 0:3 * P], BMR).then_inc(ld, 16)
                    for i, tile in enumerate((t[0], t[3])):
                        sp.dma_start(tile, LG[4 * i:4 * i + 4, :].rearrange("h (c n) -> (h c) n", n=PL)).then_inc(ld, 16)
                for side in range(2):
                    sp.wait_ge(row_in, side + 1)
                    for hf in range(2):
                        sp.dma_start(RSR[side:side + 1, hf * 98 * P:(hf + 1) * 98 * P].rearrange("a (q p) -> (a q) p", p=P),
                                     SROW[:, hf * P:(hf + 1) * P]).then_inc(st, 16)
                sp.wait_ge(st, 64)
                if l != 2:
                    sp.wait_ge(ld, 64)

    def softmax(l):
        steps = scan_sems(f"soft{l}")[0]
        ld, exp_in, exp_out, le_used, deg_ld, made, st = (sem(f"soft{l}_{n}") for n in
            ("loaded", "exp_asked", "exp_done", "edge_part_used", "degree_loaded", "weights_made", "stored"))
        att, rs, rd, dl, el = t[0], t[1], t[2], t[3], t[4]
        carries = {0: [(rd, True), (rd, False)] * 2,
                   1: [(dl, False), (rd, True), (rd, False), (dl, True), (dl, False)],
                   3: [(dl, False), (el, False), (dl, True), (dl, False), (dl, True), (dl, False)]}[l]
        with nc.Block() as block:
            @block.sync
            def _(sp):
                for side, tile in enumerate((rs, rd)):
                    for h in range(H):
                        sp.dma_start(tile[h * PARTS:(h + 1) * PARTS, :], by_part(RSR[side:side + 1, :])).then_inc(ld, 16)
                if l in (1, 3):
                    sp.dma_start(el, LG[8:12, :].rearrange("h (c n) -> (h c) n", n=PL)).then_inc(ld, 16)
                if l == 1:
                    sp.wait_ge(le_used, 1)
                    sp.dma_start(el, BM[6 * P:7 * P, :]).then_inc(deg_ld, 16)
                sp.wait_ge(made, 1)
                sp.dma_start(AL[0:4, :].rearrange("h (c n) -> (h c) n", n=PL), att).then_inc(st, 16)
                if l == 3:
                    sp.dma_start(AL[4:8, :].rearrange("h (c n) -> (h c) n", n=PL), el).then_inc(st, 16)
                sp.wait_ge(st, 32 if l == 3 else 16)

            @block.tensor
            def _(te):
                carries_on_tensor(te, f"soft{l}", carries)

            @block.scalar
            def _(act):
                act.wait_ge(exp_in, 1)
                act.activation(att, att, ACT.Exp).then_inc(exp_out, 1)
                if l == 1:
                    act.activation(rd, rd, ACT.Exp, scale=-1.0).then_inc(exp_out, 1)
                if l == 3:
                    act.activation(el, el, ACT.Exp).then_inc(exp_out, 1)

            @block.vector
            def _(dve):
                s = Scans(dve, f"soft{l}")
                dve.wait_ge(ld, 128 if l == 0 else 144)
                s.tt(att, att, rs, ALU.mult)
                s.tt(dl, dl, rd, ALU.mult)
                if l == 0:
                    s.tt(att, att, dl, ALU.add)
                    s.stt(att, att, 0.2, att, ALU.mult, ALU.max)
                    s.link(dve.tensor_copy(rd, att))
                    s.run_max(rd)
                    s.spread(rd)
                    s.tt(att, att, rd, ALU.subtract)
                    dve.nop().then_inc(exp_in, 1)
                    dve.wait_ge(exp_out, 1)
                    s.link(dve.tensor_copy(rd, att))
                    s.run_sum(rd)
                    s.spread(rd)
                    s.ts(rd, rd, 1e-16, None, ALU.add)
                    s.link(dve.reciprocal(rd, rd))
                    s.tt(att, att, rd, ALU.mult)
                if l == 1:
                    s.spread(dl)
                    s.tt(att, att, dl, ALU.add)
                    s.tt(att, att, el, ALU.add)
                    dve.nop().then_inc(le_used, 1)
                    s.stt(att, att, 0.2, att, ALU.mult, ALU.max)
                    s.link(dve.tensor_copy(rd, att))
                    s.run_max(rd)
                    s.spread(rd)
                    s.ts(rd, rd, 0.0, None, ALU.max)
                    s.tt(att, att, rd, ALU.subtract)
                    dve.nop().then_inc(exp_in, 1)
                    dve.wait_ge(exp_out, 2)
                    s.link(dve.tensor_copy(dl, att))
                    s.run_sum(dl)
                    s.spread(dl)
                    dve.wait_ge(deg_ld, 16)
                    s.tt(rd, rd, el, ALU.mult)
                    s.tt(dl, dl, rd, ALU.add)
                    s.link(dve.reciprocal(dl, dl))
                    s.tt(att, att, dl, ALU.mult)
                if l == 3:
                    s.tt(el, el, rd, ALU.mult)
                    s.spread(dl)
                    s.spread(el)
                    s.tt(att, att, dl, ALU.add)
                    s.tt(el, el, dl, ALU.add)
                    s.stt(att, att, 0.2, att, ALU.mult, ALU.max)
                    s.stt(el, el, 0.2, el, ALU.mult, ALU.max)
                    s.tt(dl, att, el, ALU.max)
                    s.run_max(dl)
                    s.spread(dl)
                    s.tt(att, att, dl, ALU.subtract)
                    s.tt(el, el, dl, ALU.subtract)
                    dve.nop().then_inc(exp_in, 1)
                    dve.wait_ge(exp_out, 2)
                    s.link(dve.tensor_copy(dl, att))
                    s.run_sum(dl)
                    s.spread(dl)
                    s.tt(dl, dl, el, ALU.add)
                    s.link(dve.reciprocal(dl, dl))
                    s.ts(dl, dl, 1.0 / H, None, ALU.mult)
                    s.tt(att, att, dl, ALU.mult)
                    s.tt(el, el, dl, ALU.mult)
                    s.tt(el, el, rd, ALU.mult)
                s.tt(att, att, rs, ALU.mult)
                dve.nop().then_inc(made, 1)

    masks()
    end_phase()
    stats(0)
    end_phase()
    softmax(0)
    end_phase()
    if stop <= 2:
        return

    def phase_c(l, ph):
        a = [0]

        def take(cols):
            v = ARENA[:, a[0]:a[0] + cols]
            a[0] += cols
            return v

        AB = [take(CH) for _ in range(2)]
        CU = [take(CH // 2).bitcast(BF16) for _ in range(2)]
        OLDW = F if l == 0 else F + 1
        OLD = [take(G * OLDW).rearrange("p (g f) -> p g f", f=OLDW) for _ in range(2)]
        NEW = [take(G * (F + 1)).rearrange("p (g f) -> p g f", f=F + 1) for _ in range(2)]
        MS = [take(CH) for _ in range(2)]
        AG = [take(CH) for _ in range(2)]
        if l == 0:
            ZM, ZE, ZR = ([take(CH) for _ in range(2)] for _ in range(3))
        assert a[0] <= 10240
        old_rows, new_rows = {0: (D0, T2), 1: (T2, T2)}[l]
        weights = {0: W0s, 1: W1T}[l]
        ab_ld, cu_ld, old_ld, new_st, sc = (
            [sem(f"c{l}_{n}{i}") for i in range(2)] for n in
            ("weights_loaded", "mask_loaded", "rows_loaded", "rows_stored", "rows_scattered"))
        (hp, ms, ag, zm, ze, zr, el, tp, nw, ic, fl) = (sem(f"c{l}_{n}") for n in
            ("projected", "messages", "summed", "below_zero", "exp", "above_zero", "elu", "turned", "rows_new",
             "index_columns", "slot_column"))

        with nc.Block() as block:
            @block.sync
            def _(sp):
                def loads(n, k):
                    b, q = half(n, k)
                    c = k * 4 + n
                    cols = bass.ds(c * CH, CH)
                    sync_wait(sp, ag, c - 1)
                    for h in range(H):
                        sp.dma_start(AB[b][h * HC:(h + 1) * HC, :], AL[h:h + 1, cols].broadcast_to([HC, CH])).then_inc(ab_ld[b], 16)
                    sp.dma_start(CU[b], CUB[0:1, cols].broadcast_to([P, CH])).then_inc(cu_ld[b], 16)

                def old_load(n, k):
                    b, q = half(n, k)
                    c = k * 4 + n
                    sync_wait(sp, nw, c - 1)
                    sp.dma_start(OLD[b][:, :, :], old_rows[bass.ds(c * CH, CH), :].rearrange("(g p) f -> p g f", p=P)).then_inc(old_ld[b], 16)

                def store(n, k):
                    b, q = half(n, k)
                    c = k * 4 + n
                    sync_wait(sp, nw, c + 1)
                    sp.dma_start(new_rows[bass.ds(c * CH, CH), :].rearrange("(g p) f -> p g f", p=P), NEW[b][:, :, :]).then_inc(new_st[b], 16)

                def body(k, j):
                    c = known(j, k)
                    if c == 0:
                        loads(0, 0)
                    if c != NCH - 1:
                        loads(j + 1, k)
                    if ph is not None:
                        dense_sp(sp, ph, j, k)
                    if c not in (0, 1):
                        store(j - 2, k)
                    old_load(j, k)

                chunks(sp, body, 2 if ph == 0 else 1)
                store(-1, NCH // U)
                store(0, NCH // U)
                sp.wait_ge(new_st[0], 16 * ((NCH + 1) // 2))
                sp.wait_ge(new_st[1], 16 * (NCH // 2))

            @block.tensor
            def _(te):
                def turn(n, k):
                    b, q = half(n, k)
                    c = k * 4 + n
                    te.wait_ge(el if l == 0 else ag, c + 1)
                    at_least(te, nw, c - 1)
                    for g in range(G):
                        last = te.transpose(BK[2 + b][:, g * P:(g + 1) * P], (MS if l == 0 else AG)[b][:, g * P:(g + 1) * P], ident[:, :])
                    last.then_inc(tp, 1)

                def body(k, j):
                    b, q = half(j, k)
                    c = k * 4 + j
                    at_least(te, ms, c - 1)
                    te.matmul(BK[b][:, :], weights[:, :], HT[:, bass.ds(c * CH, CH)], start=True, stop=True).then_inc(hp, 1)
                    if ph is not None:
                        dense_pe_q(te, ph, j, k)
                        dense_pe_t(te, ph, j, k)
                    if known(j, k) != 0:
                        turn(j - 1, k)

                chunks(te, body, 2 if ph == 0 else 1)
                turn(0, NCH // U)

            @block.scalar
            def _(act):
                def body(k, j):
                    b, q = half(j, k)
                    c = k * 4 + j
                    if ph is not None:
                        dense_act(act, ph, j, k)
                    if l == 0:
                        act.wait_ge(zm, c + 1)
                        at_least(act, el, c - 1)
                        act.activation(ZE[b], ZM[b], ACT.Exp).then_inc(ze, 1)
                        act.activation(ZR[b], AG[b], ACT.Relu, bias=b0c[:, 0:1]).then_inc(zr, 1)

                if l == 0 or ph is not None:
                    chunks(act, body, 2 if ph == 0 else 1)

            @block.vector
            def _(dve):
                def finish(n, k):
                    b, q = half(n, k)
                    c = k * 4 + n
                    dve.wait_ge(tp, c + 1)
                    dve.wait_ge(old_ld[b], q * 16 + 16)
                    at_least(dve, new_st[b], q * 16)
                    if l == 0:
                        at_least(dve, sc[b], q * 64)
                    dve.tensor_copy(NEW[b][:, :, F], SLOTF[:, bass.ds(c * G, G)]).then_inc(fl, 1)
                    dve.tensor_tensor(NEW[b][:, :, 0:F], BK[2 + b][:, :].rearrange("p (g f) -> p g f", g=G),
                                      OLD[b][:, :, 0:F], ALU.add).then_inc(nw, 1)

                def elu(n, k):
                    b, q = half(n, k)
                    c = k * 4 + n
                    dve.wait_ge(ze, c + 1)
                    dve.wait_ge(zr, c + 1)
                    dve.scalar_tensor_tensor(MS[b], ZE[b], -1.0, ZR[b], ALU.add, ALU.add).then_inc(el, 1)

                def body(k, j):
                    b, q = half(j, k)
                    c = k * 4 + j
                    first = known(j, k) == 0
                    if l == 0 and not first:
                        elu(j - 1, k)
                    dve.wait_ge(hp, c + 1)
                    dve.wait_ge(ab_ld[b], q * 64 + 64)
                    if l == 0:
                        at_least(dve, tp, c - 1)
                    dve.tensor_tensor(MS[b], BK[b][:, :], AB[b], ALU.mult).then_inc(ms, 1)
                    if l == 0 and not first:
                        pass
                    if ph is not None:
                        dense_dve(dve, ph, j, k)
                    dve.wait_ge(ms, c + 1)
                    dve.wait_ge(cu_ld[b], q * 16 + 16)
                    if l == 0:
                        at_least(dve, zr, c - 1)
                    else:
                        at_least(dve, tp, c - 1)
                    if not first:
                        dve.wait_ge(ag, c)
                    dve.tensor_tensor_scan(AG[b], CU[b], MS[b], 0.0 if first else AG[1 - b][:, CH - 1:CH],
                                           ALU.mult, ALU.add).then_inc(ag, 1)
                    if l == 0:
                        dve.wait_ge(ag, c + 1)
                        at_least(dve, ze, c - 1)
                        dve.tensor_scalar(ZM[b], AG[b], b0c[:, 0:1], 0.0, ALU.add, ALU.min).then_inc(zm, 1)
                    if not first:
                        finish(j - 1, k)

                chunks(dve, body, 2 if ph == 0 else 1)
                if l == 0:
                    elu(0, NCH // U)
                finish(0, NCH // U)

            if l == 0:
                @block.gpsimd
                def _(pool):
                    def body(k, j):
                        b, q = half(j, k)
                        c = k * 4 + j
                        at_least(pool, sc[b], q * 64)
                        pool.tensor_copy(IC[b][:, 0:4], ENDN[:, bass.ds(c * G, G)]).then_inc(ic, 1)
                        pool.wait_ge(ic, c + 1)
                        pool.wait_ge(nw, c + 1)
                        settle(pool, turns["pool"])
                        for g in range(G):
                            pool.indirect_dma_start(
                                out=T2[:, :], out_offset=bass.IndirectOffsetOnAxis(ap=IC[b][:, g:g + 1], axis=0),
                                in_=NEW[b][:, g, :], in_offset=None, bounds_check=EP + N - 1, oob_is_err=False).then_inc(sc[b], 16)

                    chunks(pool, body, 2 if ph == 0 else 1)
                    pool.wait_ge(sc[0], 64 * ((NCH + 1) // 2))
                    pool.wait_ge(sc[1], 64 * (NCH // 2))

            else:
                @block.gpsimd
                def _(pool):
                    chunks(pool, lambda k, j: dense_pool(pool, ph, j, k), 2 if ph == 0 else 1)

    phase_c(0, None)
    end_phase()
    if stop <= 3:
        return
    phase_a(1, 0)
    end_phase()
    stats(1)
    end_phase()
    softmax(1)
    end_phase()
    if stop <= 4:
        return
    phase_c(1, 1)
    end_phase()
    if stop <= 5:
        return
    phase_a(2, 2)
    end_phase()
    stats(2)
    end_phase()
    if stop <= 6:
        return

    def phase_relations(ph):
        a = [0]

        def take(cols, parts=P):
            v = ARENA[0:parts, a[0]:a[0] + cols]
            a[0] += cols
            return v

        TY = [take(CH) for _ in range(2)]
        RS = [take(CH) for _ in range(2)]
        CU = [take(CH // 2).bitcast(BF16) for _ in range(2)]
        OLD = [take(G * (F + 1)).rearrange("p (g f) -> p g f", f=F + 1) for _ in range(2)]
        PICK = [take(CH) for _ in range(3)]
        PICKP = [take(CH) for _ in range(2)]
        ONE = take(CH, R)
        AG = [take(CH) for _ in range(2)]
        HD = [take(CH).rearrange("p (g f) -> p g f", f=F) for _ in range(2)]
        NEW = [take(CH).rearrange("p (g f) -> p g f", f=F) for _ in range(2)]
        assert a[0] <= 10240, a[0]
        BY_DVE, BY_POOL = (0, 1, 2, 3, 4), (5, 6, 7)
        ORDER = (0, 1, 5, 2, 6, 3, 4, 7)
        ND, NP = len(BY_DVE), len(BY_POOL)
        BNZ = BN["z"]
        MVZ = MV["z"]
        SD = ERT[:, 0:8]
        RZ = ERT[:, 8:16]
        row_ld, cu_ld, old_ld, new_st = ([sem(f"r_{n}{i}") for i in range(2)] for n in
            ("rows_over_edges_loaded", "mask_loaded", "old_loaded", "new_stored"))
        mask = sem("r_pool_mask")
        (hs, pk, pkp, pu, pup, on, ag, tp, hd, z, bz, az, sd, rz, zt, xb, nw) = (sem(f"r_{n}") for n in
            ("h_ready", "picked", "picked_by_pool", "pick_used", "pool_pick_used", "one_hot", "summed", "turned", "h_dst", "z", "z_stats",
             "z_moments", "z_std", "z_rstd", "z_scaled", "x_beta", "rows_new"))

        with nc.Block() as block:
            @block.sync
            def _(sp):
                def loads(n, k):
                    b, q = half(n, k)
                    c = k * 4 + n
                    cols = bass.ds(c * CH, CH)
                    sync_wait(sp, ag, c - 1)
                    sp.dma_start(TY[b], TYR[0:1, cols].broadcast_to([P, CH])).then_inc(row_ld[b], 16)
                    sp.dma_start(RS[b], RSR[0:1, cols].broadcast_to([P, CH])).then_inc(row_ld[b], 16)
                    sp.dma_start(CU[b], CUB[0:1, cols].broadcast_to([P, CH])).then_inc(cu_ld[b], 16)

                def old_load(n, k):
                    b, q = half(n, k)
                    c = k * 4 + n
                    sync_wait(sp, nw, c - 1)
                    sp.dma_start(OLD[b], T2[bass.ds(c * CH, CH), :].rearrange("(g p) f -> p g f", p=P)).then_inc(old_ld[b], 16)

                def store(n, k):
                    b, q = half(n, k)
                    c = k * 4 + n
                    sync_wait(sp, nw, c + 1)
                    sp.dma_start(T3[bass.ds(c * CH, CH), :].rearrange("(g p) f -> p g f", p=P), NEW[b]).then_inc(new_st[b], 16)

                def body(k, j):
                    c = known(j, k)
                    if c == 0:
                        loads(0, 0)
                    old_load(j, k)
                    if c != NCH - 1:
                        loads(j + 1, k)
                    dense_sp(sp, ph, j, k)
                    if c not in (0, 1):
                        store(j - 2, k)

                chunks(sp, body)
                store(-1, NCH // U)
                store(0, NCH // U)
                for m in range(1, LAG + 3):
                    dense_sp(sp, ph, m, NCH // U)
                sp.wait_ge(new_st[0], 16 * ((NCH + 1) // 2))
                sp.wait_ge(new_st[1], 16 * (NCH // 2))
                for i in range(4):
                    sp.wait_ge(d_x3st[i], 16 * (NDC // 4))
                for i in range(2):
                    sp.wait_ge(d_ost[i], 16 * (NDC // 2))

            @block.tensor
            def _(te):
                def turn(n, k):
                    b, q = half(n, k)
                    c = k * 4 + n
                    te.wait_ge(ag, c + 1)
                    at_least(te, z, c - 1)
                    for g in range(G):
                        last = te.transpose(BK[2 + b][:, g * P:(g + 1) * P], AG[b][:, g * P:(g + 1) * P], ident[:, :])
                    last.then_inc(tp, 1)

                def body(k, j):
                    b, q = half(j, k)
                    c = k * 4 + j
                    if known(j, k) != 0:
                        turn(j - 1, k)
                    at_least(te, ag, c - 1)
                    te.wait_ge(on, c + 1)
                    te.matmul(BK[b][:, :], b2s[:, :], ONE, start=True, stop=False)
                    for i, r in enumerate(ORDER):
                        if r in BY_DVE:
                            te.wait_ge(pk, c * ND + (r + 1))
                            te.matmul(BK[b][:, :], W2T[:, r, :], PICK[r % 3], start=False, stop=i == R - 1).then_inc(pu, 1)
                        else:
                            n = r - ND
                            te.wait_ge(pkp, c * NP + (n + 1))
                            te.matmul(BK[b][:, :], W2T[:, r, :], PICKP[n % 2], start=False, stop=i == R - 1).then_inc(pup, 1)
                    dense_pe_q(te, ph, j, k)
                    dense_pe_t(te, ph, j, k)

                chunks(te, body)
                turn(0, NCH // U)
                for m in range(1, LAG + 3):
                    dense_pe_q(te, ph, m, NCH // U)
                    dense_pe_t(te, ph, m, NCH // U)

            @block.scalar
            def _(act):
                def body(k, j):
                    b, q = half(j, k)
                    c = k * 4 + j
                    act.wait_ge(old_ld[b], q * 16 + 16)
                    at_least(act, nw, c - 1)
                    for g in range(G):
                        col = bass.ds(c * G + g, 1)
                        last = act.activation(HD[b][:, g, :], OLD[b][:, g, 0:F], ACT.Relu, bias=NMR[:, col], scale=RSD[:, col])
                    last.then_inc(hd, 1)
                    if known(j, k) != 0:
                        root(j - 1, k)
                    dense_act(act, ph, j, k)

                def root(n, k):
                    c = k * 4 + n
                    act.wait_ge(az, c + 1)
                    act.activation(SD[:, 0:4], MVZ[:, 0, :, 1], ACT.Sqrt, bias=epsc[:, 0:1]).then_inc(sd, 1)

                chunks(act, body)
                root(0, NCH // U)
                for m in range(1, LAG + 3):
                    dense_act(act, ph, m, NCH // U)

            @block.vector
            def _(dve):
                def measure(n, k):
                    b, q = half(n, k)
                    c = k * 4 + n
                    dve.wait_ge(tp, c + 1)
                    dve.wait_ge(hd, c + 1)
                    dve.tensor_tensor(HD[b], BK[2 + b][:, :].rearrange("p (g f) -> p g f", g=G), HD[b], ALU.add).then_inc(z, 1)
                    dve.wait_ge(z, c + 1)
                    for g in range(G):
                        last = dve.bn_stats(BNZ[:, 0, g, :], HD[b][:, g, :])
                    last.then_inc(bz, 1)
                    dve.wait_ge(bz, c + 1)
                    gate(dve, "vector", c)
                    for g in range(G):
                        last = dve.bn_aggr(MVZ[:, 0, g, :], BNZ[:, 0, g, :])
                    last.then_inc(az, 1)

                def finish(n, k):
                    b, q = half(n, k)
                    c = k * 4 + n
                    dve.wait_ge(az, c + 1)
                    for g in range(G):
                        last = dve.scalar_tensor_tensor(HD[b][:, g, :], HD[b][:, g, :], MVZ[:, 0, g, 0:1], g2b[:, :],
                                                        ALU.subtract, ALU.mult)
                    last.then_inc(zt, 1)
                    dve.wait_ge(sd, c + 1)
                    dve.reciprocal(RZ[:, 0:4], SD[:, 0:4]).then_inc(rz, 1)
                    at_least(dve, new_st[b], q * 16)
                    dve.wait_ge(zt, c + 1)
                    dve.wait_ge(xb, c + 1)
                    dve.wait_ge(rz, c + 1)
                    for g in range(G):
                        last = dve.scalar_tensor_tensor(NEW[b][:, g, :], HD[b][:, g, :], RZ[:, g:g + 1],
                                                        OLD[b][:, g, 0:F], ALU.mult, ALU.add)
                    last.then_inc(nw, 1)

                def body(k, j):
                    b, q = half(j, k)
                    c = k * 4 + j
                    first = known(j, k) == 0
                    dve.wait_ge(row_ld[b], q * 32 + 32)
                    dve.tensor_tensor(RS[b], HT[:, bass.ds(c * CH, CH)], RS[b], ALU.mult).then_inc(hs, 1)
                    at_least(dve, pu, c * ND)
                    dve.tensor_scalar(ONE, TY[b][0:R, :], ridx[0:R, 0:1], None, ALU.is_equal).then_inc(on, 1)
                    dve.wait_ge(hs, c + 1)
                    for r in BY_DVE:
                        if r == 3 and not first:
                            measure(j - 1, k)
                        at_least(dve, pu, c * ND + (r - 2))
                        dve.scalar_tensor_tensor(PICK[r % 3], TY[b], float(r), RS[b], ALU.is_equal, ALU.mult).then_inc(pk, 1)
                    dense_dve(dve, ph, j, k)
                    if not first:
                        finish(j - 1, k)
                    dve.wait_ge(pup, c * NP + NP)
                    dve.wait_ge(pu, c * ND + ND)
                    dve.wait_ge(cu_ld[b], q * 16 + 16)
                    at_least(dve, tp, c - 1)
                    if not first:
                        dve.wait_ge(ag, c)
                    dve.tensor_tensor_scan(AG[b], CU[b], BK[b][:, :], 0.0 if first else AG[1 - b][:, CH - 1:CH],
                                           ALU.mult, ALU.add).then_inc(ag, 1)

                chunks(dve, body)
                measure(0, NCH // U)
                finish(0, NCH // U)
                for m in range(1, LAG + 3):
                    dense_dve(dve, ph, m, NCH // U)

            @block.gpsimd
            def _(pool):
                def body(k, j):
                    b, q = half(j, k)
                    c = k * 4 + j
                    pool.wait_ge(hs, c + 1)
                    for r in BY_POOL:
                        n = r - ND
                        at_least(pool, pup, c * NP + max(n - 1, 0))
                        gate(pool, "pool", c)
                        pool.tensor_scalar(PICKP[n % 2], TY[b], float(r), None, ALU.is_equal).then_inc(mask, 1)
                        pool.wait_ge(mask, c * NP + (n + 1))
                        pool.tensor_tensor(PICKP[n % 2], PICKP[n % 2], RS[b], ALU.mult).then_inc(pkp, 1)
                    pool.wait_ge(hd, c + 1)
                    pool.tensor_tensor(OLD[b][:, :, 0:F], OLD[b][:, :, 0:F],
                                       be2b[:, :].unsqueeze(1).broadcast_to([P, G, F]), ALU.add).then_inc(xb, 1)
                    dense_pool(pool, ph, j, k)

                chunks(pool, body)
                for m in range(1, LAG + 3):
                    dense_pool(pool, ph, m, NCH // U)

    phase_relations(3)
    end_phase()
    if stop <= 7:
        return
    phase_a(3, None)
    end_phase()
    stats(3)
    end_phase()
    softmax(3)
    end_phase()
    if stop <= 8:
        return

    def phase_last():
        a = [0]

        def take(cols):
            v = ARENA[:, a[0]:a[0] + cols]
            a[0] += cols
            return v

        AB = [take(H * CH).rearrange("p (h n) -> p h n", h=H) for _ in range(2)]
        flat = "p g f -> p (g f)"
        SB = [[take(CH) for _ in range(H)], [X3[h][:, :, :].rearrange(flat) for h in range(H)]]
        UD = [take(CH), UU[2][:, :, :].rearrange(flat)]
        OLD = [take(CH).rearrange("p (g f) -> p g f", f=F) for _ in range(2)]
        CU = [take(CH // 2).bitcast(BF16) for _ in range(2)]
        AG = [take(CH) for _ in range(2)]
        NEW = [take(CH).rearrange("p (g f) -> p g f", f=F) for _ in range(2)]
        assert a[0] <= 10240, a[0]
        SO = U3T
        HD = [UU[i][:, :, :] for i in range(2)]
        ab_ld, cu_ld, old_ld, sc = ([sem(f"l_{n}{i}") for i in range(2)] for n in
            ("weights_loaded", "mask_loaded", "rows_loaded", "rows_scattered"))
        sb_ld = [sem(f"l_self_loaded{i}") for i in range(2)]
        (hd, xh, sm, gs, gd, mp, sp_, so, ag, qq, bz, az, sd, rz, o, nw, ic) = (sem(f"l_{n}") for n in
            ("h_dst", "x_plus_h", "both_summed", "s_weighted", "d_weighted", "messages", "self_message", "self_evacuated", "summed",
             "centred", "stats", "moments", "std", "rstd", "scaled", "rows_new", "index_columns"))
        BNZ, MVZ, SD, RZ = BN["z"], MV["z"], ERT[:, 0:8], ERT[:, 8:16]

        with nc.Block() as block:
            @block.sync
            def _(sp):
                def loads(n, k):
                    b, q = half(n, k)
                    c = k * 4 + n
                    cols = bass.ds(c * CH, CH)
                    sync_wait(sp, mp, c - 1)
                    for h in range(H):
                        sp.dma_start(AB[b][:, h, :], AL[h:h + 1, cols].broadcast_to([P, CH])).then_inc(ab_ld[b], 16)
                    sync_wait(sp, ag, c - 1)
                    sp.dma_start(CU[b], CUB[0:1, cols].broadcast_to([P, CH])).then_inc(cu_ld[b], 16)

                def old_load(n, k):
                    b, q = half(n, k)
                    c = k * 4 + n
                    sync_wait(sp, nw, c - 1)
                    sp.dma_start(OLD[b], T3[bass.ds(c * CH, CH), :].rearrange("(g p) f -> p g f", p=P)).then_inc(old_ld[b], 16)

                def self_loads(n, k):
                    b, q = half(n, k)
                    c = k * 4 + n
                    cols = bass.ds(c * CH, CH)
                    sync_wait(sp, sp_, c - 1)
                    for h in range(H):
                        sp.dma_start(SB[b][h], AL[4 + h:5 + h, cols].broadcast_to([P, CH])).then_inc(sb_ld[b], 16)
                    sp.dma_start(UD[b], HDT[bass.ds(c * P, P), :]).then_inc(sb_ld[b], 16)

                def body(k, j):
                    c = known(j, k)
                    if c == 0:
                        loads(0, 0)
                        self_loads(0, 0)
                    old_load(j, k)
                    if c != NCH - 1:
                        loads(j + 1, k)
                        self_loads(j + 1, k)

                chunks(sp, body)

            @block.tensor
            def _(te):
                def out_rows(n, k):
                    b, q = half(n, k)
                    c = k * 4 + n
                    te.wait_ge(sm, c + 1)
                    at_least(te, o, c)
                    bias_rows(te, Q)
                    for g in range(G):
                        sl = slice(g * P, (g + 1) * P)
                        last = te.matmul(Q[:, g, :], SO[b][:, sl], CC[:, :], start=False, stop=g % 2 == 1)
                    last.then_inc(qq, 1)

                def body(k, j):
                    b, q = half(j, k)
                    c = k * 4 + j
                    at_least(te, ag, c - 1)
                    for h in range(H):
                        te.wait_ge(gs, c * H + (h + 1))
                        last = te.matmul(BK[b][:, :], W3s[:, h, :], AB[b][:, h, :], start=h == 0, stop=h == H - 1)
                    last.then_inc(mp, 1)
                    at_least(te, so, c - 1)
                    for h in range(H):
                        te.wait_ge(gd, c * H + (h + 1))
                        last = te.matmul(BK[2 + b][:, :], W3s[:, h, :], SB[b][h], start=h == 0, stop=h == H - 1)
                    last.then_inc(sp_, 1)
                    if known(j, k) != 0:
                        out_rows(j - 1, k)

                chunks(te, body)
                out_rows(0, NCH // U)

            @block.scalar
            def _(act):
                def root(n, k):
                    c = k * 4 + n
                    act.wait_ge(az, c + 1)
                    act.activation(SD[:, 0:4], MVZ[:, 0, :, 1], ACT.Sqrt, bias=epsc[:, 0:1]).then_inc(sd, 1)

                def body(k, j):
                    b, q = half(j, k)
                    c = k * 4 + j
                    act.wait_ge(sp_, c + 1)
                    at_least(act, qq, c - 1)
                    act.activation(SO[b][:, :], BK[2 + b][:, :], ACT.Copy).then_inc(so, 1)
                    act.wait_ge(old_ld[b], q * 16 + 16)
                    at_least(act, xh, c - 1)
                    for g in range(G):
                        col = bass.ds(c * G + g, 1)
                        last = act.activation(HD[b][:, g, :], OLD[b][:, g, :], ACT.Relu, bias=NMR[:, col], scale=RSD[:, col])
                    last.then_inc(hd, 1)
                    if known(j, k) != 0:
                        root(j - 1, k)

                chunks(act, body)
                root(0, NCH // U)

            @block.vector
            def _(dve):
                def finish(n, k):
                    b, q = half(n, k)
                    c = k * 4 + n
                    dve.wait_ge(qq, c + 1)
                    for g in range(G):
                        last = dve.bn_stats(BNZ[:, 0, g, :], Q[:, g, 0:F])
                    last.then_inc(bz, 1)
                    dve.wait_ge(bz, c + 1)
                    gate(dve, "vector", c)
                    for g in range(G):
                        last = dve.bn_aggr(MVZ[:, 0, g, :], BNZ[:, 0, g, :])
                    last.then_inc(az, 1)
                    dve.wait_ge(sd, c + 1)
                    dve.reciprocal(RZ[:, 0:4], SD[:, 0:4]).then_inc(rz, 1)
                    at_least(dve, sc[b], q * 64)
                    dve.wait_ge(rz, c + 1)
                    for g in range(G):
                        last = dve.scalar_tensor_tensor(NEW[b][:, g, :], Q[:, g, F:2 * F], RZ[:, g:g + 1],
                                                        be3b[:, :], ALU.mult, ALU.add)
                    last.then_inc(o, 1)
                    dve.wait_ge(o, c + 1)
                    dve.wait_ge(xh, c + 1)
                    dve.scalar_tensor_tensor(NEW[b], NEW[b], 0.0, OLD[b], ALU.max, ALU.add).then_inc(nw, 1)

                def body(k, j):
                    b, q = half(j, k)
                    c = k * 4 + j
                    first = known(j, k) == 0
                    dve.wait_ge(ab_ld[b], q * 64 + 64)
                    for h in range(H):
                        dve.tensor_tensor(AB[b][:, h, :], AB[b][:, h, :], HT[:, bass.ds(c * CH, CH)], ALU.mult).then_inc(gs, 1)
                    dve.wait_ge(sb_ld[b], q * 80 + 80)
                    for h in range(H):
                        dve.tensor_tensor(SB[b][h], SB[b][h], UD[b], ALU.mult).then_inc(gd, 1)
                    dve.wait_ge(mp, c + 1)
                    dve.wait_ge(cu_ld[b], q * 16 + 16)
                    at_least(dve, sm, c - 1)
                    if not first:
                        dve.wait_ge(ag, c)
                    dve.tensor_tensor_scan(AG[b], CU[b], BK[b][:, :], 0.0 if first else AG[1 - b][:, CH - 1:CH],
                                           ALU.mult, ALU.add).then_inc(ag, 1)
                    if not first:
                        finish(j - 1, k)

                chunks(dve, body)
                finish(0, NCH // U)

            @block.gpsimd
            def _(pool):
                def scatter(n, k):
                    b, q = half(n, k)
                    c = k * 4 + n
                    at_least(pool, sc[b], q * 64)
                    pool.tensor_copy(IC[b][:, 0:4], ENDO[:, bass.ds(c * G, G)]).then_inc(ic, 1)
                    pool.wait_ge(ic, c + 1)
                    pool.wait_ge(nw, c + 1)
                    settle(pool, turns["pool"])
                    for g in range(G):
                        pool.indirect_dma_start(
                            out=out, out_offset=bass.IndirectOffsetOnAxis(ap=IC[b][:, g:g + 1], axis=0),
                            in_=NEW[b][:, g, :], in_offset=None, bounds_check=N - 1, oob_is_err=False).then_inc(sc[b], 16)

                def add(n, k):
                    b, q = half(n, k)
                    c = k * 4 + n
                    pool.wait_ge(hd, c + 1)
                    pool.tensor_tensor(OLD[b], OLD[b], HD[b], ALU.add).then_inc(xh, 1)
                    pool.wait_ge(so, c + 1)
                    pool.wait_ge(ag, c + 1)
                    pool.tensor_tensor(SO[b][:, :], SO[b][:, :], AG[b], ALU.add).then_inc(sm, 1)

                def body(k, j):
                    add(j, k)
                    if known(j, k) != 0:
                        scatter(j - 1, k)

                chunks(pool, body)
                scatter(0, NCH // U)
                pool.wait_ge(sc[0], 64 * ((NCH + 1) // 2))
                pool.wait_ge(sc[1], 64 * (NCH // 2))

    phase_last()


_INS = ['x', 'src', 'dst', 'edge_attr_64', 'edge_type_8', 'L0_gnn_W', 'L0_gnn_att_src', 'L0_gnn_att_dst',
        'L0_gnn_bias', 'L1_gnn_W_node', 'L1_gnn_W_edge', 'L1_gnn_a', 'L2_gnn_W', 'L2_gnn_b', 'L2_gnn_gamma',
        'L2_gnn_beta', 'L3_gnn_W', 'L3_gnn_att_src', 'L3_gnn_att_dst', 'L3_gnn_bias', 'L3_gnn_ln_gamma',
        'L3_gnn_ln_beta']


def kernel(**inputs):
    import numpy as _np
    import concourse.bacc as _bacc
    from concourse import mybir as _mybir
    from concourse.bass_utils import run_bass_kernel_spmd as _run

    nc = _bacc.Bacc("TRN2", target_bir_lowering=False, num_devices=1)
    arrays, args = {}, []
    for name in _INS:
        a = _np.ascontiguousarray(inputs[name])
        arrays[f"in_{name}_dram"] = a
        args.append(nc.dram_tensor(f"in_{name}_dram", a.shape, _mybir.dt.from_np(a.dtype), kind="ExternalInput").ap())
    out = nc.dram_tensor("out_0_dram", (N, F), _mybir.dt.float32, kind="ExternalOutput").ap()
    program(nc, *args, out)
    r = _run(nc, [arrays], core_ids=[0])
    return r.results[0]["out_0_dram"]
```

```python
import numpy as np
import concourse.bass as bass
from concourse import mybir

F32, I32, BF16 = mybir.dt.float32, mybir.dt.int32, mybir.dt.bfloat16
ALU, ACT = mybir.AluOpType, mybir.ActivationFunctionType

N, E, F = 100000, 25000, 128
P = 128
H, HC = 4, 32
EF = 64
R = 8
EPS = 1e-5
CH = 512
G = CH // P
NCH = -(-E // CH)
EP = NCH * CH
NT = EP // P
PARTS = 32
PL = EP // PARTS
FAR = 200000
BIG = 1.0e30
NDC = -(-N // CH)
U = 4
LAG = 6


def at_least(eng, sem, value):
    if isinstance(value, int) and value <= 0:
        return
    eng.wait_ge(sem, value)


def settle(eng, turns):
    eng.sem_inc(turns, 1)


def program(nc, x, src, dst, eattr, etype, W0, as0, ad0, b0, W1n, W1e, a1, W2, b2, g2, be2,
            W3, as3, ad3, b3, g3, be3, out, stop=99):
    def dram(name, shape, dt=F32):
        return nc.dram_tensor(name, shape, dt, kind="Internal").ap()

    D0 = dram("D0", (EP, F))
    T2 = dram("T2", (EP + NDC * CH, F + 1))
    T3 = dram("T3", (EP + NDC * CH, F))
    LG = dram("LG", (16, EP))
    AL = dram("AL", (8, EP))
    RSR = dram("RSR", (2, EP))
    CUB = dram("CUB", (1, EP), BF16)
    CUR = dram("CUR", (1, EP))
    CNR = dram("CNR", (1, EP))
    TYR = dram("TYR", (1, EP))
    MKB = dram("MKB", (R, EP), BF16)
    HDT = dram("HDT", (NCH * P, CH))
    BM = dram("BM", (7 * P, PL))

    sb = nc.alloc_sbuf_tensor
    pb = nc.alloc_psum_tensor

    phase_sems = []

    def lasting(name):
        return nc.alloc_semaphore(name)

    def sem(name):
        phase_sems.append(nc.alloc_semaphore(name))
        return phase_sems[-1]

    def end_phase():
        nc.clear_and_free_semaphores(list(phase_sems))
        phase_sems.clear()
        nc.all_engine_barrier()

    turns = {name: lasting(f"turns_{name}") for name in ("pool", "sync", "vector", "tensor")}

    HT = sb("HT", [P, EP], F32)
    ARENA = sb("ARENA", [P, 10240], F32)
    X = [sb(f"X{i}", [P, G, F + 1], F32) for i in range(4)]
    UU = [sb(f"UU{i}", [P, G, F], F32) for i in range(4)]
    X3 = [sb(f"X3_{i}", [P, G, F], F32) for i in range(4)]
    U3 = [sb(f"U3_{i}", [P, G, F], F32) for i in range(2)]
    U3T = [sb(f"U3T{i}", [P, CH], F32) for i in range(2)]
    O = [sb(f"O{i}", [P, G, F], F32) for i in range(2)]

    ident = sb("ident", [P, P], F32)
    CC = sb("CC", [P, 2 * F], F32)
    CEN, g3c = CC[:, 0:F], CC[:, F:2 * F]
    W0s = sb("W0s", [P, F], F32)
    W1T = sb("W1T", [P, F], F32)
    W2T = sb("W2T", [P, R, F], F32)
    W3s = sb("W3s", [P, H, F], F32)
    WW3 = sb("WW3", [P, 2 * F], F32)
    LS = sb("LS", [P, 4, 12], F32)
    LD = sb("LD", [P, 4, 12], F32)
    LE = sb("LE", [EF, 12], F32)
    b2p = sb("b2p", [3 * R, F], BF16)
    b0c = sb("b0c", [P, 1], F32)
    b3c = sb("b3c", [P, 1], F32)
    bc3 = sb("bc3", [3, 4 * F], BF16)
    ones3 = sb("ones3", [3, P], BF16)
    onesr = sb("onesr", [1, P], F32)
    c0b = sb("c0b", [P, F], F32)
    g2b = sb("g2b", [P, F], F32)
    be2b = sb("be2b", [P, F], F32)
    be3b = sb("be3b", [P, F], F32)
    epsc = sb("epsc", [P, 2], F32)
    STS = [sb(f"STS{i}", [P, NT * 6], F32) for i in range(2)]
    MEAN = sb("MEAN", [P, NT], F32)
    RSD = sb("RSD", [P, NT], F32)
    NMR = sb("NMR", [P, NT], F32)
    SRC = sb("SRC", [P, NT], I32)
    SRCF = sb("SRCF", [P, NT], F32)
    GDST = sb("GDST", [P, NT], I32)
    ENDN = sb("ENDN", [P, NT], I32)
    ENDO = sb("ENDO", [P, NT], I32)
    SLOTF = sb("SLOTF", [P, NT], F32)
    IDX2 = sb("IDX2", [P, NT], I32)
    IC = [sb(f"IC{i}", [P, 8], I32) for i in range(2)]
    IT = sb("IT", [P, 8], F32)
    MV = {n: sb(f"MV{n}", [P, 4, G, 2], F32) for n in "xu3z"}
    BN = {n: sb(f"BN{n}", [P, 2, G, 6], F32) for n in "xu3z"}
    SM = {n: sb(f"SM{n}", [P, 4, G], F32) for n in ("nm1", "s2", "sd2", "r2", "nm3", "sg", "r3", "sd5", "r5", "ss5", "nm2")}
    ERT = sb("ERT", [P, 64], F32)

    BK = [pb(f"BK{i}", [P, CH], F32) for i in range(6)]
    Q = pb("Q", [P, G, 2 * F], F32)

    AR = ARENA[:, :]
    D_flat = AR[0:98, 0:256].bitcast(I32)
    Dn_flat = AR[0:98, 256:512].bitcast(I32)
    Dp_flat = AR[0:98, 512:768].bitcast(I32)
    S_flat = AR[0:98, 768:1024].bitcast(I32)
    Ty_flat = AR[0:98, 1024:1280].bitcast(I32)
    fD, fDn, fDp = AR[0:98, 1280:1536], AR[0:98, 1536:1792], AR[0:98, 1792:2048]
    fS, fTy, cU, cN = (AR[0:98, 2048 + 256 * i:2304 + 256 * i] for i in range(4))
    fG, fO = AR[0:98, 3072:3328], AR[0:98, 3328:3584]
    cUb = AR[0:98, 3584:3712].bitcast(BF16)
    W1ns, W1es = AR[:, 3712:3840], AR[:, 3840:3904]
    W2s = AR[:, 4096:4096 + R * F].rearrange("p (r f) -> p r f", r=R)
    W3T = AR[:, 5120:5120 + H * F].rearrange("p (h f) -> p h f", h=H)
    BK0 = AR[:, 5632:5640]
    BK1 = AR[:, 5640:5652]
    A3c = AR[:, 5652:5660]
    W0T = AR[:, 5660:5788]
    Wm = AR[:, 5788:5916]
    WmT = AR[:, 5916:6044]
    g3b = AR[:, 6044:6172]
    tA, tB = AR[:, 6300:6428], AR[:, 6428:6556]
    SLI = AR[:, 6556:6556 + NT].bitcast(I32)
    FT = AR[:, 6800:6800 + NT]
    brow, bback = AR[0:1, 7168:7680], AR[0:1, 7680:8192]
    type_masks = [AR[0:98, 9000 + 128 * i:9128 + 128 * i].bitcast(BF16) for i in range(R)]
    b2r, b2back = AR[0:R, 8968 - 256:8968 - 128], AR[0:R, 8968 - 128:8968]
    b2parts = [AR[0:R, 10024 + 64 * i:10088 + 64 * i].bitcast(BF16) for i in range(3)]
    bparts = [AR[0:1, 8192 + 256 * i:8448 + 256 * i].bitcast(BF16) for i in range(3)]

    wloads = sem("set_weight_loads")
    loads, mem, v, pe, ac, pl, st0 = (sem(n) for n in
        ("set_loads", "set_memset", "set_dve", "set_pe", "set_act", "set_pool", "set_stores"))
    FULLQ = E // 256
    REST = E - FULLQ * 256
    with nc.Block() as block:
        nload = [0]

        @block.sync
        def _(sp):
            def load(dst_ap, src_ap):
                sp.dma_start(dst_ap, src_ap).then_inc(loads if nload[0] < 16 * 11 else wloads, 16)
                nload[0] += 16

            sp.wait_ge(mem, 1)
            load(D_flat[0:FULLQ, :], dst[0:FULLQ * 256].rearrange("(q j) -> q j", j=256))
            load(D_flat[FULLQ:FULLQ + 1, 0:REST], dst[FULLQ * 256:E].rearrange("(q j) -> q j", q=1))
            load(S_flat[0:FULLQ, :], src[0:FULLQ * 256].rearrange("(q j) -> q j", j=256))
            load(S_flat[FULLQ:FULLQ + 1, 0:REST], src[FULLQ * 256:E].rearrange("(q j) -> q j", q=1))
            load(Ty_flat[0:FULLQ, :], etype[0:FULLQ * 256].rearrange("(q j) -> q j", j=256))
            load(Ty_flat[FULLQ:FULLQ + 1, 0:REST], etype[FULLQ * 256:E].rearrange("(q j) -> q j", q=1))
            load(Dn_flat[0:FULLQ, :], dst[1:1 + FULLQ * 256].rearrange("(q j) -> q j", j=256))
            load(Dn_flat[FULLQ:FULLQ + 1, 0:REST - 1], dst[FULLQ * 256 + 1:E].rearrange("(q j) -> q j", q=1))
            load(Dp_flat[0:1, 1:256], dst[0:255].rearrange("(q j) -> q j", q=1))
            load(Dp_flat[1:FULLQ, :], dst[255:FULLQ * 256 - 1].rearrange("(q j) -> q j", j=256))
            load(Dp_flat[FULLQ:FULLQ + 1, 0:REST + 1], dst[FULLQ * 256 - 1:E].rearrange("(q j) -> q j", q=1))
            load(W0s[:, :], W0)
            load(W1ns, W1n)
            load(W1es, W1e)
            load(W2s, W2.rearrange("r h d -> h r d"))
            load(W3s[:, :, :], W3.rearrange("f (h c) -> f h c", h=H))
            load(b2r, b2)
            for h in range(H):
                hp = slice(h * HC, (h + 1) * HC)
                load(BK0[hp, h:h + 1], as0[h, :].rearrange("(c a) -> c a", a=1))
                load(BK0[hp, 4 + h:5 + h], ad0[h, :].rearrange("(c a) -> c a", a=1))
                for part in range(3):
                    load(BK1[hp, 4 * part + h:4 * part + h + 1],
                         a1[h, part * HC:(part + 1) * HC].rearrange("(c a) -> c a", a=1))
                load(A3c[:, h:h + 1], as3[h, :].rearrange("(c a) -> c a", a=1))
                load(A3c[:, 4 + h:5 + h], ad3[h, :].rearrange("(c a) -> c a", a=1))
            for col, row in ((b0c, b0), (b3c, b3)):
                load(col[:, :], row.rearrange("(c a) -> c a", a=1))
            for wide, row in ((c0b[:, :], b0), (g2b[:, :], g2), (be2b[:, :], be2), (be3b[:, :], be3), (g3b, g3)):
                load(wide, row.rearrange("(a c) -> a c", a=1).broadcast_to([P, F]))
            nload.append(nload[0])
            sp.wait_ge(v, 1)
            for row, tile in ((CUB, cUb), (CUR, cU), (CNR, cN), (TYR, fTy)):
                sp.dma_start(row.rearrange("a (q j) -> (a q) j", j=256), tile).then_inc(st0, 16)
            for i, tile in enumerate(type_masks):
                sp.dma_start(MKB[i:i + 1, :].rearrange("a (q j) -> (a q) j", j=256), tile).then_inc(st0, 16)
            for part in range(3):
                sp.dma_start(b2p[part * R:(part + 1) * R, :], b2parts[part]).then_inc(st0, 16)
            sp.wait_ge(v, 8)
            for part in range(3):
                sp.dma_start(bc3[part:part + 1, :], bparts[part]).then_inc(st0, 16)
            sp.wait_ge(st0, 16 * (4 + R + 3 + 3))

        @block.gpsimd
        def _(pool):
            pool.memset(ident[:, :], 0.0).then_inc(pl, 1)
            pool.wait_ge(pl, 1)
            pool.affine_select(out=ident[:, :], in_=ident[:, :], compare_op=ALU.not_equal, fill=1.0,
                               base=0, pattern=[[-1, P]], channel_multiplier=1).then_inc(pl, 1)
            pool.iota(SLI, pattern=[[P, NT]], base=0, channel_multiplier=1).then_inc(pl, 1)

        total_loads = 16 * (11 + 6 + H * 7 + 2 + 5)

        @block.vector
        def _(dve):
            n = [0]

            def link(ins):
                n[0] += 1
                ins.then_inc(chain, 1)
                dve.wait_ge(chain, n[0])

            chain = sem("set_chain")
            for tile, value in ((D_flat, N), (Dn_flat, N), (Dp_flat, N), (S_flat, 0), (Ty_flat, 0)):
                link(dve.memset(tile, value))
            link(dve.memset(AR[0:1, 512:513].bitcast(I32), -1))
            link(dve.memset(Dn_flat[96:98, 255:256], -1))
            link(dve.memset(AR[:, 5632:5660], 0.0))
            link(dve.memset(LS[:, :, :], 0.0))
            link(dve.memset(LD[:, :, :], 0.0))
            link(dve.memset(LE[:, :], 0.0))
            link(dve.memset(onesr[:, :], 1.0))
            link(dve.memset(ones3[:, :], 1.0))
            link(dve.memset(epsc[:, 0:1], EPS))
            link(dve.memset(epsc[:, 1:2], EPS * EPS))
            for i in range(4):
                link(dve.memset(X[i][:, :, F:F + 1], -1.0))
            dve.nop().then_inc(mem, 1)
            dve.wait_ge(loads, 16 * 11)
            for f, i in ((fD, D_flat), (fDn, Dn_flat), (fDp, Dp_flat), (fS, S_flat), (fTy, Ty_flat)):
                link(dve.tensor_copy(f, i))
            link(dve.tensor_tensor(cU, fD, fDp, ALU.is_equal))
            link(dve.tensor_tensor(cN, fD, fDn, ALU.is_equal))
            link(dve.tensor_copy(cUb, cU))
            dve.wait_ge(wloads, total_loads - 16 * 11)
            for r, tile in enumerate(type_masks):
                link(dve.tensor_scalar(tile, fTy, float(r), None, ALU.is_equal))
            for part in range(3):
                link(dve.tensor_copy(b2parts[part], b2r))
                if part < 2:
                    link(dve.tensor_copy(b2back, b2parts[part]))
                    link(dve.tensor_tensor(b2r, b2r, b2back, ALU.subtract))
            dve.nop().then_inc(v, 1)
            link(dve.tensor_scalar(fG, fD, float(N - 1), None, ALU.min))
            link(dve.scalar_tensor_tensor(fO, cN, float(FAR), fD, ALU.mult, ALU.add))
            link(dve.tensor_scalar(tA, c0b[:, :], 0.0, None, ALU.min))
            dve.nop().then_inc(v, 1)
            link(dve.tensor_scalar(tB, c0b[:, :], 0.0, -1.0, ALU.max, ALU.add))
            dve.wait_ge(ac, 1)
            link(dve.tensor_tensor(c0b[:, :], tA, tB, ALU.add))
            dve.wait_ge(pl, 3)
            link(dve.tensor_scalar(CEN, ident[:, :], -1.0 / F, None, ALU.add))
            link(dve.tensor_copy(g3c, g3b))
            link(dve.tensor_copy(SLOTF[:, :], SLI))
            link(dve.tensor_tensor(Wm, W3s[:, 0, :], W3s[:, 1, :], ALU.add))
            link(dve.tensor_tensor(Wm, Wm, W3s[:, 2, :], ALU.add))
            link(dve.tensor_tensor(Wm, Wm, W3s[:, 3, :], ALU.add))
            link(dve.tensor_scalar(Wm, Wm, 1.0 / H, None, ALU.mult))
            dve.nop().then_inc(v, 1)
            dve.wait_ge(pe, 1)
            link(dve.tensor_copy(W0T, BK[0][:, 0:P]))
            link(dve.tensor_copy(W1T[:, :], BK[0][:, P:2 * P]))
            link(dve.tensor_copy(WmT, BK[0][:, 2 * P:3 * P]))
            link(dve.tensor_copy(W3T, BK[1][:, :].rearrange("p (h f) -> p h f", h=H)))
            link(dve.tensor_copy(W2T[:, 0:4, :], BK[2][:, :].rearrange("p (h f) -> p h f", h=4)))
            link(dve.tensor_copy(W2T[:, 4:8, :], BK[3][:, :].rearrange("p (h f) -> p h f", h=4)))
            dve.nop().then_inc(v, 1)
            for k, (f, ints, shift) in enumerate(((fS, SRC, 0), (fG, GDST, 0), (fO, ENDO, 0))):
                dve.wait_ge(pe, 2 + k)
                link(dve.tensor_copy(FT.rearrange("p (q two) -> p two q", two=2),
                                     BK[4][:, 0:NT].rearrange("p (two q) -> p two q", two=2)))
                link(dve.tensor_copy(ints[:, :], FT))
                if k == 0:
                    link(dve.tensor_scalar(SRCF[:, :], FT, float(EP + 1), None, ALU.add))
                if k == 2:
                    link(dve.tensor_scalar(FT, FT, float(EP), None, ALU.add))
                    link(dve.tensor_copy(ENDN[:, :], FT))
                dve.nop().then_inc(v, 1)
            dve.wait_ge(pe, 5)
            ps = BK[5]
            link(dve.tensor_copy(LS[:, 0, 0:4], ps[:, 0:4]))
            link(dve.tensor_copy(LD[:, 0, 4:8], ps[:, 4:8]))
            link(dve.tensor_copy(LS[:, 1, 0:4], ps[:, 8:12]))
            link(dve.tensor_copy(LD[:, 1, 4:8], ps[:, 12:16]))
            link(dve.tensor_copy(LE[:, 8:12], ps[0:EF, 16:20]))
            link(dve.tensor_copy(LS[:, 3, 0:4], ps[:, 24:28]))
            link(dve.tensor_copy(LD[:, 3, 8:12], ps[:, 24:28]))
            link(dve.tensor_copy(LD[:, 3, 4:8], ps[:, 28:32]))
            link(dve.tensor_copy(WW3[:, 0:F], ps[:, P:2 * P]))
            link(dve.tensor_tensor(WW3[:, F:2 * F], WW3[:, 0:F], g3b, ALU.mult))
            for i in (0, 2):
                link(dve.tensor_copy(brow[:, i * F:(i + 1) * F], ps[0:1, 2 * P:3 * P]))
                link(dve.tensor_tensor(brow[:, (i + 1) * F:(i + 2) * F], brow[:, i * F:(i + 1) * F], g3b[0:1, :], ALU.mult))
            for part in range(3):
                link(dve.tensor_copy(bparts[part], brow))
                if part < 2:
                    link(dve.tensor_copy(bback, bparts[part]))
                    link(dve.tensor_tensor(brow, brow, bback, ALU.subtract))
            dve.nop().then_inc(v, 1)

        @block.scalar
        def _(act):
            act.wait_ge(v, 2)
            act.activation(tA, tA, ACT.Exp).then_inc(ac, 1)

        @block.tensor
        def _(te):
            te.wait_ge(v, 3)
            te.transpose(BK[0][:, 0:P], W0s[:, :], ident[:, :])
            te.transpose(BK[0][:, P:2 * P], W1ns, ident[:, :])
            te.transpose(BK[0][:, 2 * P:3 * P], Wm, ident[:, :])
            for h in range(H):
                te.transpose(BK[1][:, h * P:(h + 1) * P], W3s[:, h, :], ident[:, :])
            for r in range(R):
                last = te.transpose(BK[2 + r // 4][:, (r % 4) * P:(r % 4 + 1) * P], W2s[:, r, :], ident[:, :])
            last.then_inc(pe, 1)
            te.wait_ge(v, 4)
            for k, f in enumerate((fS, fG, fO)):
                if k:
                    te.wait_ge(v, 4 + k)
                te.transpose(BK[4][:, 0:98], f[:, 0:128], ident[0:98, 0:98])
                te.transpose(BK[4][:, 98:196], f[:, 128:256], ident[0:98, 0:98]).then_inc(pe, 1)
            ps = BK[5]
            te.matmul(ps[:, 0:8], W0T, BK0, start=True, stop=True)
            te.matmul(ps[:, 8:16], W1ns, BK1[:, 0:8], start=True, stop=True)
            te.matmul(ps[0:EF, 16:20], W1es, BK1[:, 8:12], start=True, stop=True)
            for h in range(H):
                te.matmul(ps[:, 24 + h:25 + h], W3T[:, h, :], A3c[:, h:h + 1], start=True, stop=True)
                te.matmul(ps[:, 28 + h:29 + h], W3T[:, h, :], A3c[:, 4 + h:5 + h], start=True, stop=True)
            te.matmul(ps[:, P:2 * P], WmT, CEN, start=True, stop=True)
            te.matmul(ps[0:1, 2 * P:3 * P], b3c[:, :], CEN, start=True, stop=True).then_inc(pe, 1)

    assert nload[1] == total_loads
    end_phase()
    if stop <= 0:
        return

    def chunks(eng, body, peel=1):
        for k in range(peel):
            for j in range(U):
                body(k, j)
        with eng.Fori(peel, NCH // U - 1) as k:
            for j in range(U):
                body(k, j)
        for j in range(U):
            body(NCH // U - 1, j)
        body(NCH // U, 0)

    def sync_wait(sp, sem, value):
        at_least(sp, sem, value)
        if not isinstance(value, int):
            settle(sp, turns["sync"])

    def gate(eng, name, count):
        if not isinstance(count, int):
            settle(eng, turns[name])

    def half(n, k):
        return n % 2, k * 2 + n // 2

    def known(n, k):
        return 4 * k + n if isinstance(k, int) else None

    d_ld = [lasting(f"dense_x_loaded{i}") for i in range(4)]
    (d_bn, d_sq, d_qe, d_agx, d_agu, d_ag3, d_nm1, d_u, d_s2, d_sd2, d_r2, d_t, d_xb, d_x3,
     d_nm3, d_u3, d_sg, d_pt, d_ut, d_q, d_r3, d_xh, d_sd5, d_r5, d_o, d_out) = (lasting(f"dense_{n}") for n in
        ("stats", "q_squares", "q_evacuated", "x_moments", "u_moments", "x3_moments",
         "neg_mean1", "u", "var2", "std2", "rstd2", "t", "xb", "x3", "neg_mean3", "u3", "std3", "transposed",
         "evacuated", "q", "rstd3", "x3_plus_h", "std5", "rstd5", "o", "out"))
    d_x3st = [lasting(f"dense_x3_stored{i}") for i in range(4)]
    d_ost = [lasting(f"dense_out_stored{i}") for i in range(2)]

    def at(ph, j, lag, k):
        n = NCH * ph + j - lag
        if isinstance(k, int):
            d = 4 * k + n
            return 0 <= d < NDC, d, d % 4, d // 4
        return True, k * 4 + n, n % 4, k + n // 4

    def dense_sp(sp, ph, j, k):
        ok, d, s, q = at(ph, j, LAG + 1, k)
        if ok:
            sync_wait(sp, d_out, d + 1)
            if isinstance(d, int) and d == NDC - 1:
                rows = N - d * CH
                sp.dma_start(out[d * CH:N, :].rearrange("(p g) f -> p g f", g=G),
                             O[s % 2][0:rows // G, :, :]).then_inc(d_ost[s % 2], 16)
            else:
                sp.dma_start(out[bass.ds(d * CH, CH), :].rearrange("(p g) f -> p g f", g=G),
                             O[s % 2][:, :, :]).then_inc(d_ost[s % 2], 16)
        ok, d, s, q = at(ph, j, 3, k)
        if ok:
            sync_wait(sp, d_x3, d + 1)
            sp.dma_start(T3[bass.ds(d * CH + EP, CH), :].rearrange("(p g) f -> p g f", g=G), X3[s][:, :, :]).then_inc(d_x3st[s], 16)
        first = isinstance(k, int) and 4 * k + NCH * ph + j == 0
        for lag in ((0, -1) if first else (-1,)):
            ok, d, s, q = at(ph, j, lag, k)
            if ok:
                sync_wait(sp, d_x3, d - 3)
                sp.dma_start(X[s][:, :, :].rearrange("p g f -> p (g f)"),
                             T2[bass.ds(d * CH + EP, CH), :].rearrange("(p g) f -> p (g f)", g=G)).then_inc(d_ld[s], 16)

    def shared(ph):
        return ph in (1, 3)

    def scaled_by_act(ph):
        return ph in (1, 2, 3)

    d_nm2, d_v, d_clip = {}, {}, {}

    def shared_sems(ph):
        d_nm2[ph], d_v[ph], d_clip[ph] = (sem(f"dense{ph}_{n}") for n in ("neg_mean2", "v", "clipped"))

    def since(ph, lag, d):
        return d - max(NCH * ph - lag, 0) + 1

    def dense_dve(dve, ph, j, k):
        dense_dve_first(dve, ph, j, k)
        dense_dve_x3(dve, ph, j, k)

    def dense_dve_first(dve, ph, j, k):
        ok6, d6, s6, q6 = at(ph, j, LAG, k)
        ok0, d0, s0, q0 = at(ph, j, 0, k)
        ok1, d1, s1, q1 = at(ph, j, 1, k)
        ok2, d2, s2, q2 = at(ph, j, 2, k)
        ok3, d3, s3, q3 = at(ph, j, 3, k)
        ok4, d4, s4, q4 = at(ph, j, 4, k)

        def rstd2():
            dve.wait_ge(d_sd2, d2 + 1)
            dve.reciprocal(SM["r2"][:, s2, :], SM["sd2"][:, s2, :]).then_inc(d_r2, 1)

        def rstd5():
            dve.wait_ge(d_sd5, d6 + 1)
            dve.reciprocal(SM["r5"][:, s6, :], SM["sd5"][:, s6, :]).then_inc(d_r5, 1)

        def scale5():
            o = O[s6 % 2]
            dve.wait_ge(d_r5, d6 + 1)
            for g in range(G):
                last = dve.scalar_tensor_tensor(o[:, g, :], o[:, g, :], SM["r5"][:, s6, g:g + 1],
                                                be3b[:, :], ALU.mult, ALU.add)
            last.then_inc(d_o, 1)

        if ok1:
            dve.wait_ge(d_u, d1 + 1)
            for g in range(G):
                last = dve.bn_stats(BN["u"][:, s1 % 2, g, :], UU[s1][:, g, :])
        if ok0:
            dve.wait_ge(d_ld[s0], q0 * 16 + 16)
            for g in range(G):
                last = dve.bn_stats(BN["x"][:, s0 % 2, g, :], X[s0][:, g, 0:F])
        if scaled_by_act(ph) and ok2:
            rstd2()
        if ok4:
            dve.wait_ge(d_sg, d4 + 1)
            dve.reciprocal(SM["r3"][:, s4, :], SM["sg"][:, s4, :]).then_inc(d_r3, 1)
        if shared(ph) and ok6:
            rstd5()
        if scaled_by_act(ph) and ok2:
            dve.wait_ge(d_r2, d2 + 1)
            dve.scalar_tensor_tensor(SM["nm2"][:, s2, :], MV["u"][:, s2, :, 0], -1.0, SM["r2"][:, s2, :],
                                     ALU.mult, ALU.mult).then_inc(d_nm2[ph], 1)
        if ok3:
            dve.wait_ge(d_x3, d3 + 1)
            for g in range(G):
                last = dve.bn_stats(BN["3"][:, s3 % 2, g, :], X3[s3][:, g, :])
        if ok0 or ok1 or ok3:
            last.then_inc(d_bn, 1)
        if ok4:
            dve.wait_ge(d_r3, d4 + 1)
            dve.scalar_tensor_tensor(SM["nm3"][:, s4, :], MV["3"][:, s4, :, 0], -1.0, SM["r3"][:, s4, :],
                                     ALU.mult, ALU.mult).then_inc(d_nm3, 1)
        if shared(ph) and ok6:
            scale5()
        if not scaled_by_act(ph) and ok2:
            for g in range(G):
                last = dve.scalar_tensor_tensor(UU[s2][:, g, :], UU[s2][:, g, :], MV["u"][:, s2, g, 0:1],
                                                g2b[:, :], ALU.subtract, ALU.mult)
            last.then_inc(d_t, 1)
        if ok0 or ok1 or ok3:
            dve.wait_ge(d_bn, d0 + 1)
            gate(dve, "vector", d0)
        if ok0:
            for g in range(G):
                last = dve.bn_aggr(MV["x"][:, s0, g, :], BN["x"][:, s0 % 2, g, :])
            last.then_inc(d_agx, 1)
        if ok1:
            for g in range(G):
                last = dve.bn_aggr(MV["u"][:, s1, g, :], BN["u"][:, s1 % 2, g, :])
            last.then_inc(d_agu, 1)
        if ok3:
            for g in range(G):
                last = dve.bn_aggr(MV["3"][:, s3, g, :], BN["3"][:, s3 % 2, g, :])
            last.then_inc(d_ag3, 1)
        if ok0:
            dve.wait_ge(d_agx, d0 + 1)
            dve.tensor_scalar(SM["nm1"][:, s0, :], MV["x"][:, s0, :, 0], -1.0, None, ALU.mult).then_inc(d_nm1, 1)
        if not scaled_by_act(ph) and ok2:
            rstd2()
        if not shared(ph) and ok6:
            rstd5()
        if ok1:
            dve.wait_ge(d_agu, d1 + 1)
            dve.scalar_tensor_tensor(SM["s2"][:, s1, :], MV["x"][:, s1, :, 1], EPS, MV["u"][:, s1, :, 1],
                                     ALU.mult, ALU.add).then_inc(d_s2, 1)
        if not shared(ph) and ok6:
            scale5()
        if scaled_by_act(ph) and not shared(ph) and ok2:
            dve.wait_ge(d_v[ph], since(ph, 2, d2))
            u = UU[s2][:, :, :]
            dve.tensor_tensor(u, u, g2b[:, :].unsqueeze(1).broadcast_to([P, G, F]), ALU.mult).then_inc(d_t, 1)

    def dense_dve_x3(dve, ph, j, k):
        ok6, d6, s6, q6 = at(ph, j, LAG, k)
        ok2, d2, s2, q2 = at(ph, j, 2, k)
        if not shared(ph) and ok6:
            dve.wait_ge(d_o, d6 + 1)
            dve.wait_ge(d_xh, d6 + 1)
            o = O[s6 % 2][:, :, :]
            dve.scalar_tensor_tensor(o, o, 0.0, X3[s6][:, :, :], ALU.max, ALU.add).then_inc(d_out, 1)
        if ok2:
            at_least(dve, d_x3st[s2], q2 * 16)
            at_least(dve, d_out, d2 - 3)
            dve.wait_ge(d_t, d2 + 1)
            dve.wait_ge(d_xb, d2 + 1)
            if scaled_by_act(ph):
                dve.tensor_tensor(X3[s2][:, :, :], UU[s2][:, :, :], X[s2][:, :, 0:F], ALU.add).then_inc(d_x3, 1)
            else:
                dve.wait_ge(d_r2, d2 + 1)
                for g in range(G):
                    last = dve.scalar_tensor_tensor(X3[s2][:, g, :], UU[s2][:, g, :], SM["r2"][:, s2, g:g + 1],
                                                    X[s2][:, g, 0:F], ALU.mult, ALU.add)
                last.then_inc(d_x3, 1)

    def dense_pool(pool, ph, j, k):
        dense_pool_adds(pool, ph, j, k)
        dense_pool_shared(pool, ph, j, k)

    def dense_pool_adds(pool, ph, j, k):
        ok1, d1, s1, q1 = at(ph, j, 1, k)
        ok5, d5, s5, q5 = at(ph, j, 5, k)
        if ok1:
            pool.wait_ge(d_u, d1 + 1)
            x = X[s1][:, :, 0:F]
            pool.tensor_tensor(x, x, be2b[:, :].unsqueeze(1).broadcast_to([P, G, F]), ALU.add).then_inc(d_xb, 1)
        if ok5:
            pool.wait_ge(d_x3st[s5], q5 * 16 + 16)
            pool.wait_ge(d_u3, d5 + 1)
            x3 = X3[s5][:, :, :]
            pool.tensor_tensor(x3, x3, U3[s5 % 2][:, :, :], ALU.add).then_inc(d_xh, 1)

    def dense_pool_shared(pool, ph, j, k):
        if shared(ph):
            ok2, d2, s2, q2 = at(ph, j, 2, k)
            ok6, d6, s6, q6 = at(ph, j, LAG, k)
            if ok2:
                pool.wait_ge(d_v[ph], since(ph, 2, d2))
                u = UU[s2][:, :, :]
                pool.tensor_tensor(u, u, g2b[:, :].unsqueeze(1).broadcast_to([P, G, F]), ALU.mult).then_inc(d_t, 1)
            if ok6:
                pool.wait_ge(d_clip[ph], since(ph, LAG, d6))
                pool.wait_ge(d_xh, d6 + 1)
                o = O[s6 % 2][:, :, :]
                pool.tensor_tensor(o, o, X3[s6][:, :, :], ALU.add).then_inc(d_out, 1)

    def dense_act_turned(act, ph, j, k):
        ok5, d5, s5, q5 = at(ph, j, 5, k)
        if ok5:
            at_least(act, d_q, d5 - 1)
            act.wait_ge(d_pt, d5 + 1)
            act.activation(U3T[s5 % 2][:, :], BK[5][:, :], ACT.Copy).then_inc(d_ut, 1)

    def dense_act_h(act, ph, j, k):
        ok4, d4, s4, q4 = at(ph, j, 4, k)
        if ok4:
            act.wait_ge(d_nm3, d4 + 1)
            at_least(act, d_xh, d4 - 1)
            at_least(act, d_pt, d4 - 1)
            for g in range(G):
                last = act.activation(U3[s4 % 2][:, g, :], X3[s4][:, g, :], ACT.Relu, bias=SM["nm3"][:, s4, g:g + 1],
                                      scale=SM["r3"][:, s4, g:g + 1])
            last.then_inc(d_u3, 1)

    def dense_act_shared(act, ph, j, k):
        ok2, d2, s2, q2 = at(ph, j, 2, k)
        ok6, d6, s6, q6 = at(ph, j, LAG, k)
        if scaled_by_act(ph) and ok2:
            act.wait_ge(d_nm2[ph], since(ph, 2, d2))
            for g in range(G):
                last = act.activation(UU[s2][:, g, :], UU[s2][:, g, :], ACT.Identity, bias=SM["nm2"][:, s2, g:g + 1],
                                      scale=SM["r2"][:, s2, g:g + 1])
            last.then_inc(d_v[ph], 1)
        if shared(ph) and ok6:
            act.wait_ge(d_o, d6 + 1)
            act.activation(O[s6 % 2][:, :, :], O[s6 % 2][:, :, :], ACT.Relu).then_inc(d_clip[ph], 1)

    def dense_act(act, ph, j, k):
        dense_act_turned(act, ph, j, k)
        dense_act_shared(act, ph, j, k)
        dense_act_h(act, ph, j, k)
        dense_act_rest(act, ph, j, k)

    def dense_act_rest(act, ph, j, k):
        ok5, d5, s5, q5 = at(ph, j, 5, k)
        ok0, d0, s0, q0 = at(ph, j, 0, k)
        ok1, d1, s1, q1 = at(ph, j, 1, k)
        ok3, d3, s3, q3 = at(ph, j, 3, k)
        if ok0:
            act.wait_ge(d_nm1, d0 + 1)
            at_least(act, d_x3, d0 - 3)
            for g in range(G):
                last = act.activation(UU[s0][:, g, :], X[s0][:, g, 0:F], ACT.Relu, bias=SM["nm1"][:, s0, g:g + 1])
            last.then_inc(d_u, 1)
        if ok3:
            act.wait_ge(d_ag3, d3 + 1)
            act.activation(SM["sg"][:, s3, :], MV["3"][:, s3, :, 1], ACT.Sqrt, bias=epsc[:, 0:1]).then_inc(d_sg, 1)
        if ok5:
            act.wait_ge(d_q, d5 + 1)
            for g in range(G):
                last = act.activation(Q[:, g, 0:F], Q[:, g, 0:F], ACT.Square, accum_out=SM["ss5"][:, s5, g:g + 1])
            last.then_inc(d_sq, 1)
            at_least(act, d_ost[s5 % 2], ((d5 // 2) if isinstance(d5, int) else q5 * 2 + s5 // 2) * 16)
            act.activation(O[s5 % 2][:, :, :], Q[:, :, F:2 * F], ACT.Copy).then_inc(d_qe, 1)
        if ok1:
            act.wait_ge(d_s2, d1 + 1)
            act.activation(SM["sd2"][:, s1, :], SM["s2"][:, s1, :], ACT.Sqrt, bias=epsc[:, 1:2]).then_inc(d_sd2, 1)
        if ok5:
            act.wait_ge(d_sq, d5 + 1)
            act.activation(SM["sd5"][:, s5, :], SM["ss5"][:, s5, :], ACT.Sqrt, bias=epsc[:, 0:1],
                           scale=1.0 / F).then_inc(d_sd5, 1)

    def bias_rows(te, q):
        for half_q in range(2):
            te.matmul(q[:, 2 * half_q:2 * half_q + 2, :], ones3[:, :], bc3[:, :], start=True, stop=False)

    def dense_pe_q(te, ph, j, k):
        ok5, d5, s5, q5 = at(ph, j, 5, k)
        if ok5:
            te.wait_ge(d_ut, d5 + 1)
            at_least(te, d_qe, d5)
            bias_rows(te, Q)
            for g in range(G):
                last = te.matmul(Q[:, g, :], U3T[s5 % 2][:, g * P:(g + 1) * P], WW3[:, :], start=False, stop=g % 2 == 1)
            last.then_inc(d_q, 1)

    def dense_pe_t(te, ph, j, k):
        ok4, d4, s4, q4 = at(ph, j, 4, k)
        if ok4:
            te.wait_ge(d_u3, d4 + 1)
            at_least(te, d_ut, d4)
            for g in range(G):
                last = te.transpose(BK[5][:, g * P:(g + 1) * P], U3[s4 % 2][:, g, :], ident[:, :])
            last.then_inc(d_pt, 1)

    def phase_a(l, ph):
        if ph is not None and scaled_by_act(ph):
            shared_sems(ph)
        a = [0]

        def take(cols, parts=P):
            v = ARENA[0:parts, a[0]:a[0] + cols]
            a[0] += cols
            return v

        SW = F + 1 if l in (1, 2) else F
        SR = [take(G * SW).rearrange("p (g f) -> p g f", f=SW) for _ in range(2)]
        DR = [take(G * SW).rearrange("p (g f) -> p g f", f=SW) for _ in range(2)]
        XTS, XTD = take(CH), take(CH)
        UDT = [take(CH) for _ in range(2)]
        LGS = [take(CH, 12) for _ in range(2)]
        if l == 1:
            EA = [take(G * EF).rearrange("p (g f) -> p g f", f=EF) for _ in range(2)]
            EAT = take(CH, EF)
        assert a[0] <= 10240
        logits = l != 2

        def pair(name):
            return [sem(f"a{l}_{name}{i}") for i in range(2)]

        s_ld, d_ldr, st_d0, st_lg, st_hd, e_ld = (pair(n) for n in
            ("s_rows", "d_rows", "d0_stored", "logits_stored", "ud_stored", "edges_loaded"))
        (s_tr, d_tr, e_tr, s_xt, d_xt, e_xt, s_cen, d_cen, s_u, d_u_, lg_pe, lg_ev, s_st, d_st, ic, fl) = (
            sem(f"a{l}_{n}") for n in ("s_transposed", "d_transposed", "e_transposed", "s_evacuated", "d_evacuated",
                "e_evacuated", "s_centred", "d_centred", "s_u", "d_u", "logits", "logits_evacuated", "s_stats",
                "d_stats", "index_columns", "flag_bias"))
        x_ld = [sem(f"a{l}_x_loaded{i}") for i in range(4)]
        x_st = [sem(f"a{l}_x_stored{i}") for i in range(4)]
        x_add = sem(f"a{l}_x_added")
        source = {0: x, 1: T2, 2: T2, 3: T3}[l]
        index = {0: SRC, 1: SRC, 2: IDX2, 3: IDX2}[l]
        dsrc = {1: T2, 2: T2, 3: T3}.get(l)

        with nc.Block() as block:
            @block.gpsimd
            def _(pool):
                def body(k, j):
                    b, q = half(j, k)
                    c = k * 4 + j
                    at_least(pool, s_tr, c - 1)
                    at_least(pool, s_st, c - 1)
                    if l == 0:
                        at_least(pool, d_tr, c - 1)
                        at_least(pool, d_st, c - 1)
                        at_least(pool, st_d0[b], q * 16)
                    pool.tensor_copy(IC[b][:, 0:4], index[:, bass.ds(c * G, G)]).then_inc(ic, 1)
                    if l == 0:
                        pool.tensor_copy(IC[b][:, 4:8], GDST[:, bass.ds(c * G, G)]).then_inc(ic, 1)
                    pool.wait_ge(ic, (c + 1) * (2 if l == 0 else 1))
                    settle(pool, turns["pool"])
                    for g in range(G):
                        pool.indirect_dma_start(
                            out=SR[b][:, g, :], out_offset=None, in_=source,
                            in_offset=bass.IndirectOffsetOnAxis(ap=IC[b][:, g:g + 1], axis=0),
                            element_offset=0).then_inc(s_ld[b], 16)
                    if l == 0:
                        for g in range(G):
                            pool.indirect_dma_start(
                                out=DR[b][:, g, :], out_offset=None, in_=source,
                                in_offset=bass.IndirectOffsetOnAxis(ap=IC[b][:, 4 + g:5 + g], axis=0)).then_inc(d_ldr[b], 16)
                    if ph is not None:
                        dense_pool(pool, ph, j, k)

                chunks(pool, body, 2 if ph == 0 else 1)

            @block.sync
            def _(sp):
                def loads(n, k):
                    b, q = half(n, k)
                    c = k * 4 + n
                    if l:
                        if logits:
                            sync_wait(sp, d_tr, c - 1)
                        sync_wait(sp, d_st, c - 1)
                        sp.dma_start(DR[b][:, :, :], dsrc[bass.ds(c * CH, CH), :].rearrange("(g p) f -> p g f", p=P)).then_inc(d_ldr[b], 16)
                    if l == 1:
                        sync_wait(sp, e_tr, c - 1)
                        if isinstance(c, int) and c == NCH - 1:
                            rest = E - c * CH
                            full = rest // P
                            sp.dma_start(EA[b][:, 0:full, :], eattr[c * CH:c * CH + full * P, :].rearrange("(g p) f -> p g f", p=P)).then_inc(e_ld[b], 16)
                            sp.dma_start(EA[b][:, full:G, :], eattr[0:(G - full) * P, :].rearrange("(g p) f -> p g f", p=P)).then_inc(e_ld[b], 16)
                            sync_wait(sp, e_ld[b], q * 16 + 32)
                            sp.dma_start(EA[b][0:rest - full * P, full, :], eattr[c * CH + full * P:E, :]).then_inc(e_ld[b], 16)
                        else:
                            sp.dma_start(EA[b][:, :, :], eattr[bass.ds(c * CH, CH), :].rearrange("(g p) f -> p g f", p=P)).then_inc(e_ld[b], 16)

                def body(k, j):
                    b, q = half(j, k)
                    c = k * 4 + j
                    first = isinstance(c, int) and c == 0
                    last = isinstance(c, int) and c == NCH - 1
                    if first:
                        loads(0, 0)
                    if not last:
                        loads(j + 1, k)
                    if l == 0:
                        if first:
                            for i in range(3):
                                sp.dma_start(X[i][:, :, 0:F], x[i * CH:(i + 1) * CH, :].rearrange("(p g) f -> p g f", g=G)).then_inc(x_ld[i], 16)
                        sync_wait(sp, x_st[3], c * 16)
                        if last:
                            row = (NDC - 1) * CH
                            sp.dma_start(X[3][0:(N - row) // G, :, 0:F], x[row:N, :].rearrange("(p g) f -> p g f", g=G)).then_inc(x_ld[3], 16)
                        else:
                            sp.dma_start(X[3][:, :, 0:F], x[bass.ds((c * 4 + 3) * CH, CH), :].rearrange("(p g) f -> p g f", g=G)).then_inc(x_ld[3], 16)
                        for i in range(4):
                            sync_wait(sp, x_add, c * 4 + (i + 1))
                            sp.dma_start(T2[bass.ds((c * 4 + i) * CH + EP, CH), :].rearrange("(p g) f -> p (g f)", g=G),
                                         X[i][:, :, :].rearrange("p g f -> p (g f)")).then_inc(x_st[i], 16)
                        sync_wait(sp, d_ldr[b], (q + 1) * 64)
                        sp.dma_start(D0[bass.ds(c * CH, CH), :].rearrange("(g p) f -> p g f", p=P), DR[b][:, :, :]).then_inc(st_d0[b], 16)
                        if not last:
                            for i in range(3):
                                sync_wait(sp, x_st[i], c * 16 + 16)
                                sp.dma_start(X[i][:, :, 0:F], x[bass.ds((c * 4 + 4 + i) * CH, CH), :].rearrange("(p g) f -> p g f", g=G)).then_inc(x_ld[i], 16)
                    if ph is not None:
                        dense_sp(sp, ph, j, k)
                    if l == 3 and not first:
                        store_side(j - 1, k)
                    if logits and known(j, k) not in (0, 1):
                        store(j - 2, k)

                def store(n, k):
                    b, q = half(n, k)
                    c = k * 4 + n
                    sync_wait(sp, lg_ev, c + 1)
                    sp.dma_start(LG[0:12, bass.ds(c * CH, CH)], LGS[b][:, :]).then_inc(st_lg[b], 16)

                def store_side(n, k):
                    b, q = half(n, k)
                    c = k * 4 + n
                    sync_wait(sp, d_u_, c + 1)
                    sp.dma_start(HDT[bass.ds(c * P, P), :], UDT[b][:, :]).then_inc(st_hd[b], 16)

                chunks(sp, body, 2 if ph == 0 else 1)
                if l == 3:
                    store_side(0, NCH // U)
                if logits:
                    store(-1, NCH // U)
                    store(0, NCH // U)
                n0, n1 = (NCH + 1) // 2, NCH // 2
                for sems, used in ((st_d0, l == 0), (st_lg, logits), (st_hd, l == 3)):
                    if used:
                        sync_wait(sp, sems[0], 16 * n0)
                        sync_wait(sp, sems[1], 16 * n1)
                if l == 0:
                    for i in range(4):
                        sync_wait(sp, x_st[i], 16 * NCH)

            @block.vector
            def _(dve):
                def body(k, j):
                    b, q = half(j, k)
                    c = k * 4 + j
                    if l == 0:
                        for i in range(4):
                            dve.wait_ge(x_ld[i], c * 16 + 16)
                            dve.tensor_tensor(X[i][:, :, 0:F], X[i][:, :, 0:F],
                                              c0b[:, :].unsqueeze(1).broadcast_to([P, G, F]), ALU.add).then_inc(x_add, 1)
                    dve.wait_ge(d_ldr[b], (q + 1) * (64 if l == 0 else 16))
                    for g in range(G):
                        last = dve.bn_stats(STS[1][:, bass.ds(c * (G * 6) + g * 6, 6)], DR[b][:, g, 0:F])
                    last.then_inc(d_st, 1)
                    if ph is not None:
                        dense_dve(dve, ph, j, k)
                    dve.wait_ge(s_ld[b], (q + 1) * 64)
                    if l == 1:
                        dve.scalar_tensor_tensor(IT[:, 0:4], SR[b][:, :, F], 0.0, SRCF[:, bass.ds(c * G, G)],
                                                 ALU.is_lt, ALU.mult).then_inc(fl, 1)
                    for g in range(G):
                        last = dve.bn_stats(STS[0][:, bass.ds(c * (G * 6) + g * 6, 6)], SR[b][:, g, 0:F])
                    if l == 1:
                        dve.wait_ge(fl, c + 1)
                        last = dve.tensor_tensor(IDX2[:, bass.ds(c * G, G)], IT[:, 0:4], SR[b][:, :, F], ALU.add)
                    last.then_inc(s_st, 1)

                chunks(dve, body, 2 if ph == 0 else 1)

            @block.scalar
            def _(act):
                def body(k, j):
                    b, q = half(j, k)
                    c = k * 4 + j
                    if ph is not None:
                        dense_act_turned(act, ph, j, k)
                    if logits:
                        act.wait_ge(d_tr, c + 1)
                        at_least(act, d_cen, c)
                        act.activation(XTD, BK[1][:, :], ACT.Copy).then_inc(d_xt, 1)
                    act.wait_ge(s_tr, c + 1)
                    at_least(act, s_cen, c)
                    act.activation(XTS, BK[0][:, :], ACT.Copy).then_inc(s_xt, 1)
                    if logits and known(j, k) != 0:
                        store_logits(j - 1, k)
                    if l == 1:
                        act.wait_ge(e_tr, c + 1)
                        at_least(act, lg_pe, c)
                        act.activation(EAT, BK[1][0:EF, :], ACT.Copy).then_inc(e_xt, 1)
                    if ph is not None:
                        dense_act_shared(act, ph, j, k)
                        dense_act_h(act, ph, j, k)
                    act.wait_ge(s_cen, c + 1)
                    act.activation(HT[:, bass.ds(c * CH, CH)], BK[2][:, :], ACT.Relu).then_inc(s_u, 1)
                    if logits:
                        act.wait_ge(d_cen, c + 1)
                        at_least(act, lg_pe, c - 1)
                        if l == 3:
                            at_least(act, st_hd[b], q * 16)
                        act.activation(UDT[b], BK[4][:, :], ACT.Relu).then_inc(d_u_, 1)
                    if ph is not None:
                        dense_act_rest(act, ph, j, k)

                def store_logits(n, k):
                    b, q = half(n, k)
                    c = k * 4 + n
                    act.wait_ge(lg_pe, c + 1)
                    at_least(act, st_lg[b], q * 16)
                    act.activation(LGS[b], BK[3][0:12, :], ACT.Copy).then_inc(lg_ev, 1)

                chunks(act, body, 2 if ph == 0 else 1)
                if logits:
                    store_logits(0, NCH // U)

            @block.tensor
            def _(te):
                def body(k, j):
                    b, q = half(j, k)
                    c = k * 4 + j
                    if logits:
                        te.wait_ge(d_ldr[b], (q + 1) * (64 if l == 0 else 16))
                        at_least(te, d_xt, c)
                        if l == 1:
                            at_least(te, e_xt, c)
                        for g in range(G):
                            last = te.transpose(BK[1][:, g * P:(g + 1) * P], DR[b][:, g, 0:F], ident[:, :])
                        last.then_inc(d_tr, 1)
                    te.wait_ge(s_ld[b], (q + 1) * 64)
                    at_least(te, s_xt, c)
                    for g in range(G):
                        last = te.transpose(BK[0][:, g * P:(g + 1) * P], SR[b][:, g, 0:F], ident[:, :])
                    last.then_inc(s_tr, 1)
                    if logits and known(j, k) != 0:
                        project(j - 1, k)
                    if l == 1:
                        te.wait_ge(e_ld[b], (q + 1) * 16 if not (isinstance(c, int) and c == NCH - 1) else q * 16 + 48)
                        te.wait_ge(d_xt, c + 1)
                        gate(te, "tensor", c)
                        for g in range(G):
                            last = te.transpose(BK[1][0:EF, g * P:(g + 1) * P], EA[b][:, g, :], ident[:, :])
                        last.then_inc(e_tr, 1)
                    te.wait_ge(s_xt, c + 1)
                    at_least(te, s_u, c)
                    te.matmul(BK[2][:, :], CEN, XTS, start=True, stop=True).then_inc(s_cen, 1)
                    if logits:
                        te.wait_ge(d_xt, c + 1)
                        at_least(te, d_u_, c)
                        te.matmul(BK[4][:, :], CEN, XTD, start=True, stop=True).then_inc(d_cen, 1)
                    if ph is not None:
                        dense_pe_q(te, ph, j, k)
                        dense_pe_t(te, ph, j, k)

                def project(n, k):
                    b, q = half(n, k)
                    c = k * 4 + n
                    te.wait_ge(s_u, c + 1)
                    te.wait_ge(d_u_, c + 1)
                    at_least(te, lg_ev, c)
                    te.matmul(BK[3][0:12, :], LS[:, l, :], HT[:, bass.ds(c * CH, CH)], start=True, stop=False)
                    if l == 1:
                        te.wait_ge(e_xt, c + 1)
                        gate(te, "tensor", c)
                        te.matmul(BK[3][0:12, :], LE[:, :], EAT, start=False, stop=False)
                    te.matmul(BK[3][0:12, :], LD[:, l, :], UDT[b], start=False, stop=True).then_inc(lg_pe, 1)

                chunks(te, body, 2 if ph == 0 else 1)
                if logits:
                    project(0, NCH // U)

    phase_a(0, None)
    end_phase()
    if stop <= 1:
        return

    BT = [ARENA[:, i * PL:(i + 1) * PL] for i in range(13)]
    BU, BNX, PF, PFN, PB, NEGU = BT[0:6]
    t = BT[6:12]
    ROW = BT[12]
    rU, rN, rB = (ROW[0:1, i * P:(i + 1) * P] for i in range(3))
    roww = ROW[0:1, 3 * P:4 * P + 1]
    KCOL = ROW[:, 720:721]
    BMR = dram("BMR", (1, 3 * P))
    STAT = [ARENA[:, 10 * PL + i * NT:10 * PL + (i + 1) * NT] for i in range(2)]
    SROW = ARENA[0:98, 11 * PL:11 * PL + 2 * P]

    def by_part(row):
        return row.rearrange("a (c n) -> (a c) n", n=PL)

    class Scans:

        def __init__(self, dve, name):
            self.dve, self.n, self.i = dve, 0, 0
            self.steps, self.part_ready, self.row_out, self.row_ready, self.col_out = SEMS[name]

        def link(self, ins):
            self.n += 1
            ins.then_inc(self.steps, 1)
            self.dve.wait_ge(self.steps, self.n)

        def tt(self, o, a, b, op):
            self.link(self.dve.tensor_tensor(o, a, b, op))

        def ts(self, o, a, s1, s2, op0, op1=None):
            self.link(self.dve.tensor_scalar(o, a, s1, s2, op0) if op1 is None
                      else self.dve.tensor_scalar(o, a, s1, s2, op0, op1))

        def stt(self, o, a, s, b, op0, op1):
            self.link(self.dve.scalar_tensor_tensor(o, a, s, b, op0, op1))

        def carry(self, tile, mask, mrow, fwd, op0, op1):
            dve, i = self.dve, self.i
            self.i += 1
            self.link(dve.memset(roww[:, 0:1] if fwd else roww[:, P:P + 1], 0.0))
            dve.nop().then_inc(self.part_ready, 1)
            dve.wait_ge(self.row_out, i + 1)
            if fwd:
                self.link(dve.tensor_tensor_scan(roww[:, 1:P + 1], mrow, BK[0][0:1, 0:P], 0.0, op0, op1))
            else:
                self.link(dve.tensor_tensor_scan(roww[:, 0:P][:, ::-1], mrow[:, ::-1], BK[0][0:1, 0:P][:, ::-1], 0.0, op0, op1))
            dve.nop().then_inc(self.row_ready, 1)
            dve.wait_ge(self.col_out, i + 1)
            self.link(dve.tensor_copy(KCOL, BK[1][:, 0:1]))
            self.stt(tile, mask, KCOL, tile, op0, op1)

        def run_sum(self, tile):
            self.link(self.dve.tensor_tensor_scan(tile, BU, tile, 0.0, ALU.mult, ALU.add))
            self.carry(tile, PF, rU, True, ALU.mult, ALU.add)

        def run_max(self, tile):
            self.link(self.dve.tensor_tensor_scan(tile, NEGU, tile, -BIG, ALU.add, ALU.max))
            self.carry(tile, PFN, rN, True, ALU.add, ALU.max)

        def spread(self, tile):
            self.stt(t[5], BNX, -1.0, tile, ALU.add, ALU.mult)
            self.link(self.dve.tensor_tensor_scan(tile[:, ::-1], BNX[:, ::-1], t[5][:, ::-1], 0.0, ALU.mult, ALU.subtract))
            self.carry(tile, PB, rB, False, ALU.mult, ALU.add)

    SEMS = {}

    def scan_sems(name):
        SEMS[name] = [sem(f"{name}_{s}") for s in ("steps", "part_ready", "row_out", "row_ready", "col_out")]
        return SEMS[name]

    def carries_on_tensor(te, name, tiles):
        _, part_ready, row_out, row_ready, col_out = SEMS[name]
        for i, (tile, fwd) in enumerate(tiles):
            col = PL - 1 if fwd else 0
            te.wait_ge(part_ready, i + 1)
            te.matmul(BK[0][0:1, 0:P], tile[:, col:col + 1], ident[:, :], start=True, stop=True).then_inc(row_out, 1)
            te.wait_ge(row_ready, i + 1)
            te.matmul(BK[1][:, 0:1], roww[:, 0:P] if fwd else roww[:, 1:P + 1], onesr[0:1, 0:1],
                      start=True, stop=True).then_inc(col_out, 1)

    def masks():
        scan_sems("masks")
        ld, st, rows, made = (sem(f"masks_{n}") for n in ("loaded", "stored", "rows", "made"))
        with nc.Block() as block:
            @block.sync
            def _(sp):
                for h in range(H):
                    sp.dma_start(BU[h * PARTS:(h + 1) * PARTS, :], by_part(CUR)).then_inc(ld, 16)
                    sp.dma_start(BNX[h * PARTS:(h + 1) * PARTS, :], by_part(CNR)).then_inc(ld, 16)
                sp.wait_ge(made, 1)
                sp.dma_start(BM[0:6 * P, :].rearrange("(i p) n -> p i n", p=P),
                             ARENA[:, 0:6 * PL].rearrange("p (i n) -> p i n", n=PL)).then_inc(st, 16)
                sp.dma_start(BMR, ROW[0:1, 0:3 * P]).then_inc(st, 16)
                sp.wait_ge(made, 2)
                sp.dma_start(BM[6 * P:7 * P, :], t[0]).then_inc(st, 16)
                sp.wait_ge(st, 48)

            @block.vector
            def _(dve):
                s = Scans(dve, "masks")
                dve.wait_ge(ld, 128)
                s.link(dve.tensor_tensor_scan(PF, BU, BU, 1.0, ALU.mult, ALU.min))
                s.link(dve.tensor_tensor_scan(PB[:, ::-1], BNX[:, ::-1], BNX[:, ::-1], 1.0, ALU.mult, ALU.min))
                s.ts(PFN, PF, -1.0, BIG, ALU.add, ALU.mult)
                s.ts(NEGU, BU, -1.0, BIG, ALU.add, ALU.mult)
                dve.nop().then_inc(rows, 1)
                dve.wait_ge(rows, 4)
                for i, row in enumerate((rU, rN, rB)):
                    s.link(dve.tensor_copy(row, BK[2][0:1, i * P:(i + 1) * P]))
                dve.nop().then_inc(made, 1)
                s.link(dve.memset(t[0], 1.0))
                s.run_sum(t[0])
                s.spread(t[0])
                s.ts(t[0], t[0], -1.0, float(E), ALU.mult, ALU.add)
                dve.nop().then_inc(made, 1)

            @block.tensor
            def _(te):
                te.wait_ge(rows, 1)
                for i, (tile, col) in enumerate(((PF, PL - 1), (PFN, PL - 1), (PB, 0))):
                    te.matmul(BK[2][0:1, i * P:(i + 1) * P], tile[:, col:col + 1], ident[:, :],
                              start=True, stop=True).then_inc(rows, 1)
                carries_on_tensor(te, "masks", [(t[0], True), (t[0], False)])

    def stats(l):
        steps, std_in, std_out, col_in, col_out, row_in, st, ld = (sem(f"stats{l}_{n}") for n in
            ("steps", "var_ready", "std_ready", "rstd_ready", "turned", "row_ready", "stored", "loaded"))
        with nc.Block() as block:
            @block.vector
            def _(dve):
                n = [0]

                def link(ins):
                    n[0] += 1
                    ins.then_inc(steps, 1)
                    dve.wait_ge(steps, n[0])

                for side in range(2):
                    s6 = STS[side][:, :].rearrange("p (t k) -> p t k", k=6)
                    a, b = STAT
                    link(dve.tensor_tensor(a, s6[:, :, 1], s6[:, :, 4], ALU.subtract))
                    link(dve.tensor_tensor(b, s6[:, :, 2], s6[:, :, 5], ALU.add))
                    link(dve.scalar_tensor_tensor(a, a, 0.25, a, ALU.mult, ALU.mult))
                    link(dve.scalar_tensor_tensor(b, b, 1.0 / F, a, ALU.mult, ALU.add))
                    dve.nop().then_inc(std_in, 1)
                    dve.wait_ge(std_out, side + 1)
                    link(dve.reciprocal(RSD[:, :], b))
                    dve.nop().then_inc(col_in, 1)
                    dve.wait_ge(col_out, side + 1)
                    if side:
                        dve.wait_ge(st, 32)
                    link(dve.tensor_copy(SROW, BK[1][0:98, 0:2 * P]))
                    dve.nop().then_inc(row_in, 1)
                if l in (2, 3):
                    link(dve.tensor_tensor(MEAN[:, :], s6[:, :, 1], s6[:, :, 4], ALU.add))
                    link(dve.scalar_tensor_tensor(NMR[:, :], MEAN[:, :], -0.5, RSD[:, :], ALU.mult, ALU.mult))
                if l == 0:
                    link(dve.tensor_scalar(STAT[0], SRCF[:, :], -1.0, None, ALU.add))
                    link(dve.tensor_copy(SRC[:, :], STAT[0]))

            @block.scalar
            def _(act):
                for side in range(2):
                    act.wait_ge(std_in, side + 1)
                    act.activation(STAT[1], STAT[1], ACT.Sqrt, bias=epsc[:, 0:1]).then_inc(std_out, 1)

            @block.tensor
            def _(te):
                for side in range(2):
                    te.wait_ge(col_in, side + 1)
                    te.transpose(BK[1][0:98, 0:P], RSD[:, 0:98], ident[:, :])
                    te.transpose(BK[1][0:98, P:2 * P], RSD[:, 98:196], ident[:, :]).then_inc(col_out, 1)

            @block.sync
            def _(sp):
                if l != 2:
                    sp.dma_start(ARENA[:, 0:6 * PL].rearrange("p (i n) -> p i n", n=PL),
                                 BM[0:6 * P, :].rearrange("(i p) n -> p i n", p=P)).then_inc(ld, 16)
                    sp.dma_start(ROW[0:1, 0:3 * P], BMR).then_inc(ld, 16)
                    for i, tile in enumerate((t[0], t[3])):
                        sp.dma_start(tile, LG[4 * i:4 * i + 4, :].rearrange("h (c n) -> (h c) n", n=PL)).then_inc(ld, 16)
                for side in range(2):
                    sp.wait_ge(row_in, side + 1)
                    for hf in range(2):
                        sp.dma_start(RSR[side:side + 1, hf * 98 * P:(hf + 1) * 98 * P].rearrange("a (q p) -> (a q) p", p=P),
                                     SROW[:, hf * P:(hf + 1) * P]).then_inc(st, 16)
                sp.wait_ge(st, 64)
                if l != 2:
                    sp.wait_ge(ld, 64)

    def softmax(l):
        steps = scan_sems(f"soft{l}")[0]
        ld, exp_in, exp_out, le_used, deg_ld, made, st = (sem(f"soft{l}_{n}") for n in
            ("loaded", "exp_asked", "exp_done", "edge_part_used", "degree_loaded", "weights_made", "stored"))
        att, rs, rd, dl, el = t[0], t[1], t[2], t[3], t[4]
        carries = {0: [(rd, True), (rd, False)] * 2,
                   1: [(dl, False), (rd, True), (rd, False), (dl, True), (dl, False)],
                   3: [(dl, False), (el, False), (dl, True), (dl, False), (dl, True), (dl, False)]}[l]
        with nc.Block() as block:
            @block.sync
            def _(sp):
                for side, tile in enumerate((rs, rd)):
                    for h in range(H):
                        sp.dma_start(tile[h * PARTS:(h + 1) * PARTS, :], by_part(RSR[side:side + 1, :])).then_inc(ld, 16)
                if l in (1, 3):
                    sp.dma_start(el, LG[8:12, :].rearrange("h (c n) -> (h c) n", n=PL)).then_inc(ld, 16)
                if l == 1:
                    sp.wait_ge(le_used, 1)
                    sp.dma_start(el, BM[6 * P:7 * P, :]).then_inc(deg_ld, 16)
                sp.wait_ge(made, 1)
                sp.dma_start(AL[0:4, :].rearrange("h (c n) -> (h c) n", n=PL), att).then_inc(st, 16)
                if l == 3:
                    sp.dma_start(AL[4:8, :].rearrange("h (c n) -> (h c) n", n=PL), el).then_inc(st, 16)
                sp.wait_ge(st, 32 if l == 3 else 16)

            @block.tensor
            def _(te):
                carries_on_tensor(te, f"soft{l}", carries)

            @block.scalar
            def _(act):
                act.wait_ge(exp_in, 1)
                act.activation(att, att, ACT.Exp).then_inc(exp_out, 1)
                if l == 1:
                    act.activation(rd, rd, ACT.Exp, scale=-1.0).then_inc(exp_out, 1)
                if l == 3:
                    act.activation(el, el, ACT.Exp).then_inc(exp_out, 1)

            @block.vector
            def _(dve):
                s = Scans(dve, f"soft{l}")
                dve.wait_ge(ld, 128 if l == 0 else 144)
                s.tt(att, att, rs, ALU.mult)
                s.tt(dl, dl, rd, ALU.mult)
                if l == 0:
                    s.tt(att, att, dl, ALU.add)
                    s.stt(att, att, 0.2, att, ALU.mult, ALU.max)
                    s.link(dve.tensor_copy(rd, att))
                    s.run_max(rd)
                    s.spread(rd)
                    s.tt(att, att, rd, ALU.subtract)
                    dve.nop().then_inc(exp_in, 1)
                    dve.wait_ge(exp_out, 1)
                    s.link(dve.tensor_copy(rd, att))
                    s.run_sum(rd)
                    s.spread(rd)
                    s.ts(rd, rd, 1e-16, None, ALU.add)
                    s.link(dve.reciprocal(rd, rd))
                    s.tt(att, att, rd, ALU.mult)
                if l == 1:
                    s.spread(dl)
                    s.tt(att, att, dl, ALU.add)
                    s.tt(att, att, el, ALU.add)
                    dve.nop().then_inc(le_used, 1)
                    s.stt(att, att, 0.2, att, ALU.mult, ALU.max)
                    s.link(dve.tensor_copy(rd, att))
                    s.run_max(rd)
                    s.spread(rd)
                    s.ts(rd, rd, 0.0, None, ALU.max)
                    s.tt(att, att, rd, ALU.subtract)
                    dve.nop().then_inc(exp_in, 1)
                    dve.wait_ge(exp_out, 2)
                    s.link(dve.tensor_copy(dl, att))
                    s.run_sum(dl)
                    s.spread(dl)
                    dve.wait_ge(deg_ld, 16)
                    s.tt(rd, rd, el, ALU.mult)
                    s.tt(dl, dl, rd, ALU.add)
                    s.link(dve.reciprocal(dl, dl))
                    s.tt(att, att, dl, ALU.mult)
                if l == 3:
                    s.tt(el, el, rd, ALU.mult)
                    s.spread(dl)
                    s.spread(el)
                    s.tt(att, att, dl, ALU.add)
                    s.tt(el, el, dl, ALU.add)
                    s.stt(att, att, 0.2, att, ALU.mult, ALU.max)
                    s.stt(el, el, 0.2, el, ALU.mult, ALU.max)
                    s.tt(dl, att, el, ALU.max)
                    s.run_max(dl)
                    s.spread(dl)
                    s.tt(att, att, dl, ALU.subtract)
                    s.tt(el, el, dl, ALU.subtract)
                    dve.nop().then_inc(exp_in, 1)
                    dve.wait_ge(exp_out, 2)
                    s.link(dve.tensor_copy(dl, att))
                    s.run_sum(dl)
                    s.spread(dl)
                    s.tt(dl, dl, el, ALU.add)
                    s.link(dve.reciprocal(dl, dl))
                    s.ts(dl, dl, 1.0 / H, None, ALU.mult)
                    s.tt(att, att, dl, ALU.mult)
                    s.tt(el, el, dl, ALU.mult)
                    s.tt(el, el, rd, ALU.mult)
                s.tt(att, att, rs, ALU.mult)
                dve.nop().then_inc(made, 1)

    masks()
    end_phase()
    stats(0)
    end_phase()
    softmax(0)
    end_phase()
    if stop <= 2:
        return

    def phase_c(l, ph):
        if ph is not None:
            shared_sems(ph)
        a = [0]

        def take(cols):
            v = ARENA[:, a[0]:a[0] + cols]
            a[0] += cols
            return v

        AB = [take(CH) for _ in range(2)]
        CU = [take(CH // 2).bitcast(BF16) for _ in range(2)]
        OLDW = F if l == 0 else F + 1
        OLD = [take(G * OLDW).rearrange("p (g f) -> p g f", f=OLDW) for _ in range(2)]
        NEW = [take(G * (F + 1)).rearrange("p (g f) -> p g f", f=F + 1) for _ in range(2)]
        MS = [take(CH) for _ in range(2)]
        AG = [take(CH) for _ in range(2)]
        if l == 0:
            ZM, ZE, ZR = ([take(CH) for _ in range(2)] for _ in range(3))
        assert a[0] <= 10240
        old_rows, new_rows = {0: (D0, T2), 1: (T2, T2)}[l]
        weights = {0: W0s, 1: W1T}[l]
        ab_ld, cu_ld, old_ld, new_st, sc = (
            [sem(f"c{l}_{n}{i}") for i in range(2)] for n in
            ("weights_loaded", "mask_loaded", "rows_loaded", "rows_stored", "rows_scattered"))
        (hp, ms, ag, zm, ze, zr, el, tp, nw, ic, fl) = (sem(f"c{l}_{n}") for n in
            ("projected", "messages", "summed", "below_zero", "exp", "above_zero", "elu", "turned", "rows_new",
             "index_columns", "slot_column"))

        with nc.Block() as block:
            @block.sync
            def _(sp):
                def loads(n, k):
                    b, q = half(n, k)
                    c = k * 4 + n
                    cols = bass.ds(c * CH, CH)
                    sync_wait(sp, ag, c - 1)
                    for h in range(H):
                        sp.dma_start(AB[b][h * HC:(h + 1) * HC, :], AL[h:h + 1, cols].broadcast_to([HC, CH])).then_inc(ab_ld[b], 16)
                    sp.dma_start(CU[b], CUB[0:1, cols].broadcast_to([P, CH])).then_inc(cu_ld[b], 16)

                def old_load(n, k):
                    b, q = half(n, k)
                    c = k * 4 + n
                    sync_wait(sp, nw, c - 1)
                    sp.dma_start(OLD[b][:, :, :], old_rows[bass.ds(c * CH, CH), :].rearrange("(g p) f -> p g f", p=P)).then_inc(old_ld[b], 16)

                def store(n, k):
                    b, q = half(n, k)
                    c = k * 4 + n
                    sync_wait(sp, nw, c + 1)
                    sp.dma_start(new_rows[bass.ds(c * CH, CH), :].rearrange("(g p) f -> p g f", p=P), NEW[b][:, :, :]).then_inc(new_st[b], 16)

                def body(k, j):
                    c = known(j, k)
                    if c == 0:
                        loads(0, 0)
                    if c != NCH - 1:
                        loads(j + 1, k)
                    if ph is not None:
                        dense_sp(sp, ph, j, k)
                    if c not in (0, 1):
                        store(j - 2, k)
                    old_load(j, k)

                chunks(sp, body, 2 if ph == 0 else 1)
                store(-1, NCH // U)
                store(0, NCH // U)
                sp.wait_ge(new_st[0], 16 * ((NCH + 1) // 2))
                sp.wait_ge(new_st[1], 16 * (NCH // 2))

            @block.tensor
            def _(te):
                def turn(n, k):
                    b, q = half(n, k)
                    c = k * 4 + n
                    te.wait_ge(el if l == 0 else ag, c + 1)
                    at_least(te, nw, c - 1)
                    for g in range(G):
                        last = te.transpose(BK[2 + b][:, g * P:(g + 1) * P], (MS if l == 0 else AG)[b][:, g * P:(g + 1) * P], ident[:, :])
                    last.then_inc(tp, 1)

                def project(n, k):
                    b, q = half(n, k)
                    c = k * 4 + n
                    at_least(te, ms, c - 1)
                    te.matmul(BK[b][:, :], weights[:, :], HT[:, bass.ds(c * CH, CH)], start=True, stop=True).then_inc(hp, 1)

                def body(k, j):
                    if known(j, k) == 0:
                        project(0, k)
                    if known(j, k) != NCH - 1:
                        project(j + 1, k)
                    if known(j, k) != 0:
                        turn(j - 1, k)
                    if ph is not None:
                        dense_pe_q(te, ph, j, k)
                        dense_pe_t(te, ph, j, k)

                chunks(te, body, 2 if ph == 0 else 1)
                turn(0, NCH // U)

            @block.scalar
            def _(act):
                def body(k, j):
                    b, q = half(j, k)
                    c = k * 4 + j
                    if ph is not None:
                        dense_act(act, ph, j, k)
                    if l == 0:
                        act.wait_ge(zm, c + 1)
                        at_least(act, el, c - 1)
                        act.activation(ZE[b], ZM[b], ACT.Exp).then_inc(ze, 1)
                        act.activation(ZR[b], AG[b], ACT.Relu, bias=b0c[:, 0:1]).then_inc(zr, 1)

                if l == 0 or ph is not None:
                    chunks(act, body, 2 if ph == 0 else 1)

            @block.vector
            def _(dve):
                def finish(n, k):
                    b, q = half(n, k)
                    c = k * 4 + n
                    dve.wait_ge(tp, c + 1)
                    dve.wait_ge(old_ld[b], q * 16 + 16)
                    at_least(dve, new_st[b], q * 16)
                    if l == 0:
                        at_least(dve, sc[b], q * 64)
                    dve.tensor_copy(NEW[b][:, :, F], SLOTF[:, bass.ds(c * G, G)]).then_inc(fl, 1)
                    dve.tensor_tensor(NEW[b][:, :, 0:F], BK[2 + b][:, :].rearrange("p (g f) -> p g f", g=G),
                                      OLD[b][:, :, 0:F], ALU.add).then_inc(nw, 1)

                def elu(n, k):
                    b, q = half(n, k)
                    c = k * 4 + n
                    dve.wait_ge(ze, c + 1)
                    dve.wait_ge(zr, c + 1)
                    dve.scalar_tensor_tensor(MS[b], ZE[b], -1.0, ZR[b], ALU.add, ALU.add).then_inc(el, 1)

                def body(k, j):
                    b, q = half(j, k)
                    c = k * 4 + j
                    first = known(j, k) == 0
                    if l == 0 and not first:
                        elu(j - 1, k)
                    dve.wait_ge(hp, c + 1)
                    dve.wait_ge(ab_ld[b], q * 64 + 64)
                    if l == 0:
                        at_least(dve, tp, c - 1)
                    dve.tensor_tensor(MS[b], BK[b][:, :], AB[b], ALU.mult).then_inc(ms, 1)
                    if ph is not None:
                        dense_dve_first(dve, ph, j, k)
                    dve.wait_ge(ms, c + 1)
                    dve.wait_ge(cu_ld[b], q * 16 + 16)
                    if l == 0:
                        at_least(dve, zr, c - 1)
                    else:
                        at_least(dve, tp, c - 1)
                    if not first:
                        dve.wait_ge(ag, c)
                    dve.tensor_tensor_scan(AG[b], CU[b], MS[b], 0.0 if first else AG[1 - b][:, CH - 1:CH],
                                           ALU.mult, ALU.add).then_inc(ag, 1)
                    if l == 0:
                        dve.wait_ge(ag, c + 1)
                        at_least(dve, ze, c - 1)
                        dve.tensor_scalar(ZM[b], AG[b], b0c[:, 0:1], 0.0, ALU.add, ALU.min).then_inc(zm, 1)
                    if not first:
                        finish(j - 1, k)
                    if ph is not None:
                        dense_dve_x3(dve, ph, j, k)

                chunks(dve, body, 2 if ph == 0 else 1)
                if l == 0:
                    elu(0, NCH // U)
                finish(0, NCH // U)

            if l == 0:
                @block.gpsimd
                def _(pool):
                    def body(k, j):
                        b, q = half(j, k)
                        c = k * 4 + j
                        at_least(pool, sc[b], q * 64)
                        pool.tensor_copy(IC[b][:, 0:4], ENDN[:, bass.ds(c * G, G)]).then_inc(ic, 1)
                        pool.wait_ge(ic, c + 1)
                        pool.wait_ge(nw, c + 1)
                        settle(pool, turns["pool"])
                        for g in range(G):
                            pool.indirect_dma_start(
                                out=T2[:, :], out_offset=bass.IndirectOffsetOnAxis(ap=IC[b][:, g:g + 1], axis=0),
                                in_=NEW[b][:, g, :], in_offset=None, bounds_check=EP + N - 1, oob_is_err=False).then_inc(sc[b], 16)

                    chunks(pool, body, 2 if ph == 0 else 1)
                    pool.wait_ge(sc[0], 64 * ((NCH + 1) // 2))
                    pool.wait_ge(sc[1], 64 * (NCH // 2))

            else:
                @block.gpsimd
                def _(pool):
                    chunks(pool, lambda k, j: dense_pool(pool, ph, j, k), 2 if ph == 0 else 1)

    phase_c(0, None)
    end_phase()
    if stop <= 3:
        return
    phase_a(1, 0)
    end_phase()
    stats(1)
    end_phase()
    softmax(1)
    end_phase()
    if stop <= 4:
        return
    phase_c(1, 1)
    end_phase()
    if stop <= 5:
        return
    phase_a(2, 2)
    end_phase()
    stats(2)
    end_phase()
    if stop <= 6:
        return

    def phase_relations(ph):
        shared_sems(ph)
        a = [0]

        def take(cols, parts=P):
            v = ARENA[0:parts, a[0]:a[0] + cols]
            a[0] += cols
            return v

        TY = [take(CH) for _ in range(2)]
        RS = [take(CH) for _ in range(2)]
        CU = [take(CH // 2).bitcast(BF16) for _ in range(2)]
        OLD = [take(G * (F + 1)).rearrange("p (g f) -> p g f", f=F + 1) for _ in range(2)]
        PICK = [take(CH) for _ in range(3)]
        PICKP = [take(CH) for _ in range(2)] + [STS[1][:, i * CH:(i + 1) * CH] for i in range(2)]
        ONE = [take(CH // 2, 3 * R).bitcast(BF16) for _ in range(2)]
        AG = [take(CH) for _ in range(2)]
        HD = [take(CH).rearrange("p (g f) -> p g f", f=F) for _ in range(2)]
        NEW = [take(CH).rearrange("p (g f) -> p g f", f=F) for _ in range(2)]
        assert a[0] <= 10240, a[0]
        BY_DVE, BY_POOL = (0, 1, 2, 3), (4, 5, 6, 7)
        ORDER = (0, 1, 4, 2, 5, 3, 6, 7)
        ND, NP = len(BY_DVE), len(BY_POOL)
        BNZ = BN["z"]
        MVZ = MV["z"]
        SD = ERT[:, 0:8]
        RZ = ERT[:, 8:16]
        NZ = ERT[:, 16:20]
        vz, nz = sem("r_z_scaled_by_std"), sem("r_neg_mean_z")
        row_ld, cu_ld, old_ld, new_st = ([sem(f"r_{n}{i}") for i in range(2)] for n in
            ("rows_over_edges_loaded", "mask_loaded", "old_loaded", "new_stored"))
        MASKS = STS[0][:, 0:2 * CH].bitcast(BF16).rearrange("p (r n) -> p r n", r=NP)
        mk_ld = sem("r_masks_loaded")
        on = [sem(f"r_one_hot_loaded{i}") for i in range(2)]
        (hs, pk, pkp, pu, pup, ag, tp, hd, z, bz, az, sd, rz, zt, xb, nw) = (sem(f"r_{n}") for n in
            ("h_ready", "picked", "picked_by_pool", "pick_used", "pool_pick_used", "summed", "turned", "h_dst", "z", "z_stats",
             "z_moments", "z_std", "z_rstd", "z_scaled", "x_beta", "rows_new"))

        with nc.Block() as block:
            @block.sync
            def _(sp):
                def loads(n, k):
                    b, q = half(n, k)
                    c = k * 4 + n
                    cols = bass.ds(c * CH, CH)
                    sync_wait(sp, ag, c - 1)
                    sp.dma_start(TY[b], TYR[0:1, cols].broadcast_to([P, CH])).then_inc(row_ld[b], 16)
                    sp.dma_start(RS[b], RSR[0:1, cols].broadcast_to([P, CH])).then_inc(row_ld[b], 16)
                    for part in range(3):
                        sp.dma_start(ONE[b][part * R:(part + 1) * R, :], MKB[:, cols]).then_inc(on[b], 16)
                    sp.dma_start(CU[b], CUB[0:1, cols].broadcast_to([P, CH])).then_inc(cu_ld[b], 16)

                def masks_load(n, k):
                    c = k * 4 + n
                    sync_wait(sp, pkp, c * NP)
                    sp.dma_start(MASKS, MKB[R - NP:R, bass.ds(c * CH, CH)].unsqueeze(0).broadcast_to([P, NP, CH])).then_inc(mk_ld, 16)

                def old_load(n, k):
                    b, q = half(n, k)
                    c = k * 4 + n
                    sync_wait(sp, nw, c - 1)
                    sp.dma_start(OLD[b], T2[bass.ds(c * CH, CH), :].rearrange("(g p) f -> p g f", p=P)).then_inc(old_ld[b], 16)

                def store(n, k):
                    b, q = half(n, k)
                    c = k * 4 + n
                    sync_wait(sp, nw, c + 1)
                    sp.dma_start(T3[bass.ds(c * CH, CH), :].rearrange("(g p) f -> p g f", p=P), NEW[b]).then_inc(new_st[b], 16)

                def body(k, j):
                    c = known(j, k)
                    if c == 0:
                        loads(0, 0)
                        masks_load(0, 0)
                    if c != 0:
                        old_load(j - 1, k)
                    dense_sp(sp, ph, j, k)
                    if c != NCH - 1:
                        loads(j + 1, k)
                        masks_load(j + 1, k)
                    if c not in (0, 1, 2):
                        store(j - 3, k)

                chunks(sp, body)
                old_load(0, NCH // U)
                store(-2, NCH // U)
                store(-1, NCH // U)
                store(0, NCH // U)
                for m in range(1, LAG + 3):
                    dense_sp(sp, ph, m, NCH // U)
                sp.wait_ge(new_st[0], 16 * ((NCH + 1) // 2))
                sp.wait_ge(new_st[1], 16 * (NCH // 2))
                for i in range(4):
                    sp.wait_ge(d_x3st[i], 16 * (NDC // 4))
                for i in range(2):
                    sp.wait_ge(d_ost[i], 16 * (NDC // 2))

            @block.tensor
            def _(te):
                def turn(n, k):
                    b, q = half(n, k)
                    c = k * 4 + n
                    te.wait_ge(ag, c + 1)
                    at_least(te, z, c - 1)
                    for g in range(G):
                        last = te.transpose(BK[2 + b][:, g * P:(g + 1) * P], AG[b][:, g * P:(g + 1) * P], ident[:, :])
                    last.then_inc(tp, 1)

                def body(k, j):
                    b, q = half(j, k)
                    c = k * 4 + j
                    at_least(te, ag, c - 1)
                    te.wait_ge(on[b], q * 48 + 48)
                    te.matmul(BK[b][:, :], b2p[:, :], ONE[b], start=True, stop=False)
                    for i, r in enumerate(ORDER):
                        if r in BY_DVE:
                            te.wait_ge(pk, c * ND + (r + 1))
                            te.matmul(BK[b][:, :], W2T[:, r, :], PICK[r % 3], start=False, stop=i == R - 1).then_inc(pu, 1)
                        else:
                            n = r - ND
                            te.wait_ge(pkp, c * NP + (n + 1))
                            te.matmul(BK[b][:, :], W2T[:, r, :], PICKP[n], start=False, stop=i == R - 1).then_inc(pup, 1)
                    if known(j, k) != 0:
                        turn(j - 1, k)
                    dense_pe_q(te, ph, j, k)
                    dense_pe_t(te, ph, j, k)

                chunks(te, body)
                turn(0, NCH // U)
                for m in range(1, LAG + 3):
                    dense_pe_q(te, ph, m, NCH // U)
                    dense_pe_t(te, ph, m, NCH // U)

            @block.scalar
            def _(act):
                def h_dst(n, k):
                    b, q = half(n, k)
                    c = k * 4 + n
                    act.wait_ge(old_ld[b], q * 16 + 16)
                    at_least(act, nw, c - 1)
                    for g in range(G):
                        col = bass.ds(c * G + g, 1)
                        last = act.activation(HD[b][:, g, :], OLD[b][:, g, 0:F], ACT.Relu, bias=NMR[:, col], scale=RSD[:, col])
                    last.then_inc(hd, 1)

                def body(k, j):
                    dense_act_turned(act, ph, j, k)
                    if known(j, k) != 0:
                        h_dst(j - 1, k)
                    if known(j, k) not in (0, 1):
                        root(j - 2, k)
                        scale(j - 2, k)
                    dense_act_shared(act, ph, j, k)
                    dense_act_h(act, ph, j, k)
                    dense_act_rest(act, ph, j, k)

                def root(n, k):
                    c = k * 4 + n
                    act.wait_ge(az, c + 1)
                    act.activation(SD[:, 0:4], MVZ[:, 0, :, 1], ACT.Sqrt, bias=epsc[:, 0:1]).then_inc(sd, 1)

                def scale(n, k):
                    b, q = half(n, k)
                    c = k * 4 + n
                    act.wait_ge(nz, c + 1)
                    for g in range(G):
                        last = act.activation(HD[b][:, g, :], HD[b][:, g, :], ACT.Identity, bias=NZ[:, g:g + 1], scale=RZ[:, g:g + 1])
                    last.then_inc(vz, 1)

                chunks(act, body)
                root(-1, NCH // U)
                scale(-1, NCH // U)
                h_dst(0, NCH // U)
                root(0, NCH // U)
                scale(0, NCH // U)
                for m in range(1, LAG + 3):
                    dense_act(act, ph, m, NCH // U)

            @block.vector
            def _(dve):
                def measure(n, k):
                    b, q = half(n, k)
                    c = k * 4 + n
                    dve.wait_ge(tp, c + 1)
                    dve.wait_ge(hd, c + 1)
                    dve.tensor_tensor(HD[b], BK[2 + b][:, :].rearrange("p (g f) -> p g f", g=G), HD[b], ALU.add).then_inc(z, 1)
                    dve.wait_ge(z, c + 1)
                    for g in range(G):
                        last = dve.bn_stats(BNZ[:, 0, g, :], HD[b][:, g, :])
                    last.then_inc(bz, 1)
                    dve.wait_ge(bz, c + 1)
                    gate(dve, "vector", c)
                    for g in range(G):
                        last = dve.bn_aggr(MVZ[:, 0, g, :], BNZ[:, 0, g, :])
                    last.then_inc(az, 1)

                def scale_factors(n, k):
                    c = k * 4 + n
                    dve.wait_ge(sd, c + 1)
                    at_least(dve, vz, c)
                    dve.reciprocal(RZ[:, 0:4], SD[:, 0:4]).then_inc(rz, 1)
                    dve.wait_ge(rz, c + 1)
                    dve.scalar_tensor_tensor(NZ, MVZ[:, 0, :, 0], -1.0, RZ[:, 0:4], ALU.mult, ALU.mult).then_inc(nz, 1)

                def finish(n, k):
                    b, q = half(n, k)
                    c = k * 4 + n
                    dve.wait_ge(vz, c + 1)
                    dve.tensor_tensor(HD[b], HD[b], g2b[:, :].unsqueeze(1).broadcast_to([P, G, F]), ALU.mult).then_inc(zt, 1)
                    at_least(dve, new_st[b], q * 16)
                    dve.wait_ge(zt, c + 1)
                    dve.wait_ge(xb, c + 1)
                    dve.tensor_tensor(NEW[b], HD[b], OLD[b][:, :, 0:F], ALU.add).then_inc(nw, 1)

                def body(k, j):
                    b, q = half(j, k)
                    c = k * 4 + j
                    first = known(j, k) == 0
                    dve.wait_ge(row_ld[b], q * 32 + 32)
                    dve.tensor_tensor(RS[b], HT[:, bass.ds(c * CH, CH)], RS[b], ALU.mult).then_inc(hs, 1)
                    if not first:
                        scan(j - 1, k)
                    dve.wait_ge(hs, c + 1)
                    for r in BY_DVE:
                        if r == 2 and known(j, k) not in (0, 1):
                            measure(j - 2, k)
                        at_least(dve, pu, c * ND + (r - 2))
                        dve.scalar_tensor_tensor(PICK[r % 3], TY[b], float(r), RS[b], ALU.is_equal, ALU.mult).then_inc(pk, 1)
                    if known(j, k) not in (0, 1):
                        scale_factors(j - 2, k)
                    dense_dve_first(dve, ph, j, k)
                    if known(j, k) not in (0, 1):
                        finish(j - 2, k)
                    dense_dve_x3(dve, ph, j, k)

                def scan(n, k):
                    b, q = half(n, k)
                    c = k * 4 + n
                    first = known(n, k) == 0
                    dve.wait_ge(pup, c * NP + NP)
                    dve.wait_ge(pu, c * ND + ND)
                    dve.wait_ge(cu_ld[b], q * 16 + 16)
                    at_least(dve, tp, c - 1)
                    if not first:
                        dve.wait_ge(ag, c)
                    dve.tensor_tensor_scan(AG[b], CU[b], BK[b][:, :], 0.0 if first else AG[1 - b][:, CH - 1:CH],
                                           ALU.mult, ALU.add).then_inc(ag, 1)

                chunks(dve, body)
                scan(0, NCH // U)
                for n in (-1, 0):
                    measure(n, NCH // U)
                    scale_factors(n, NCH // U)
                    finish(n, NCH // U)
                for m in range(1, LAG + 3):
                    dense_dve(dve, ph, m, NCH // U)

            @block.gpsimd
            def _(pool):
                def body(k, j):
                    b, q = half(j, k)
                    c = k * 4 + j
                    pool.wait_ge(hs, c + 1)
                    pool.wait_ge(mk_ld, c * 16 + 16)
                    for n in range(NP):
                        at_least(pool, pup, c * NP - (NP - 1 - n))
                        pool.tensor_tensor(PICKP[n], MASKS[:, n, :], RS[b], ALU.mult).then_inc(pkp, 1)
                    dense_pool_adds(pool, ph, j, k)
                    if known(j, k) != 0:
                        add_beta(j - 1, k)
                    dense_pool_shared(pool, ph, j, k)

                def add_beta(n, k):
                    b, q = half(n, k)
                    c = k * 4 + n
                    pool.wait_ge(hd, c + 1)
                    pool.tensor_tensor(OLD[b][:, :, 0:F], OLD[b][:, :, 0:F],
                                       be2b[:, :].unsqueeze(1).broadcast_to([P, G, F]), ALU.add).then_inc(xb, 1)

                chunks(pool, body)
                add_beta(0, NCH // U)
                for m in range(1, LAG + 3):
                    dense_pool(pool, ph, m, NCH // U)

    phase_relations(3)
    end_phase()
    if stop <= 7:
        return
    phase_a(3, None)
    end_phase()
    stats(3)
    end_phase()
    softmax(3)
    end_phase()
    if stop <= 8:
        return

    def phase_last():
        a = [0]

        def take(cols):
            v = ARENA[:, a[0]:a[0] + cols]
            a[0] += cols
            return v

        AB = [take(H * CH).rearrange("p (h n) -> p h n", h=H) for _ in range(2)]
        flat = "p g f -> p (g f)"
        SB = [[take(CH) for _ in range(H)], [X3[h][:, :, :].rearrange(flat) for h in range(H)]]
        UD = [take(CH), UU[2][:, :, :].rearrange(flat)]
        OLD = [take(CH).rearrange("p (g f) -> p g f", f=F) for _ in range(2)]
        CU = [take(CH // 2).bitcast(BF16) for _ in range(2)]
        AG = [take(CH) for _ in range(2)]
        NEW = [take(CH).rearrange("p (g f) -> p g f", f=F) for _ in range(2)]
        assert a[0] <= 10240, a[0]
        SO = U3T
        HD = [UU[i][:, :, :] for i in range(2)]
        ab_ld, cu_ld, old_ld, sc = ([sem(f"l_{n}{i}") for i in range(2)] for n in
            ("weights_loaded", "mask_loaded", "rows_loaded", "rows_scattered"))
        sb_ld = [sem(f"l_self_loaded{i}") for i in range(2)]
        sq, nb = sem("l_squares"), sem("l_plus_beta")
        (hd, xh, sm, gs, gd, mp, sp_, so, ag, qq, sd, rz, o, nw, ic) = (sem(f"l_{n}") for n in
            ("h_dst", "x_plus_h", "both_summed", "s_weighted", "d_weighted", "messages", "self_message", "self_evacuated", "summed",
             "centred", "std", "rstd", "scaled", "rows_new", "index_columns"))
        QL = [Q[:, 2 * i:2 * i + 2, :].rearrange("p a (b f) -> p (a b) f", b=2) for i in range(2)]
        SQ = UU[3]
        SD, RZ, SS = ERT[:, 0:8], ERT[:, 8:16], ERT[:, 16:20]

        with nc.Block() as block:
            @block.sync
            def _(sp):
                def loads(n, k):
                    b, q = half(n, k)
                    c = k * 4 + n
                    cols = bass.ds(c * CH, CH)
                    sync_wait(sp, mp, c - 1)
                    for h in range(H):
                        sp.dma_start(AB[b][:, h, :], AL[h:h + 1, cols].broadcast_to([P, CH])).then_inc(ab_ld[b], 16)

                def mask_load(n, k):
                    b, q = half(n, k)
                    c = k * 4 + n
                    cols = bass.ds(c * CH, CH)
                    sync_wait(sp, ag, c - 1)
                    sp.dma_start(CU[b], CUB[0:1, cols].broadcast_to([P, CH])).then_inc(cu_ld[b], 16)

                def old_load(n, k):
                    b, q = half(n, k)
                    c = k * 4 + n
                    sync_wait(sp, nw, c - 1)
                    sp.dma_start(OLD[b], T3[bass.ds(c * CH, CH), :].rearrange("(g p) f -> p g f", p=P)).then_inc(old_ld[b], 16)

                def self_loads(n, k):
                    b, q = half(n, k)
                    c = k * 4 + n
                    cols = bass.ds(c * CH, CH)
                    sync_wait(sp, sp_, c - 1)
                    for h in range(H):
                        sp.dma_start(SB[b][h], AL[4 + h:5 + h, cols].broadcast_to([P, CH])).then_inc(sb_ld[b], 16)
                    sp.dma_start(UD[b], HDT[bass.ds(c * P, P), :]).then_inc(sb_ld[b], 16)

                def body(k, j):
                    c = known(j, k)
                    if c == 0:
                        loads(0, 0)
                        self_loads(0, 0)
                        mask_load(0, 0)
                    else:
                        old_load(j - 1, k)
                    if c != NCH - 1:
                        loads(j + 1, k)
                        self_loads(j + 1, k)
                        mask_load(j + 1, k)

                chunks(sp, body)
                old_load(0, NCH // U)

            @block.tensor
            def _(te):
                def out_rows(n, k):
                    b, q = half(n, k)
                    c = k * 4 + n
                    te.wait_ge(sm, c + 1)
                    at_least(te, o, c - 1)
                    te.matmul(QL[b], ones3[:, :], bc3[:, 0:F].unsqueeze(1).broadcast_to([3, G, F]), start=True, stop=False)
                    for g in range(G):
                        sl = slice(g * P, (g + 1) * P)
                        last = te.matmul(QL[b][:, g, :], SO[b][:, sl], CEN, start=False, stop=g == G - 1)
                    last.then_inc(qq, 1)

                def body(k, j):
                    b, q = half(j, k)
                    c = k * 4 + j
                    at_least(te, ag, c - 1)
                    for h in range(H):
                        te.wait_ge(gs, c * H + (h + 1))
                        last = te.matmul(BK[b][:, :], W3s[:, h, :], AB[b][:, h, :], start=h == 0, stop=h == H - 1)
                    last.then_inc(mp, 1)
                    at_least(te, so, c - 1)
                    for h in range(H):
                        te.wait_ge(gd, c * H + (h + 1))
                        last = te.matmul(BK[2 + b][:, :], W3s[:, h, :], SB[b][h], start=h == 0, stop=h == H - 1)
                    last.then_inc(sp_, 1)
                    if known(j, k) != 0:
                        out_rows(j - 1, k)

                chunks(te, body)
                out_rows(0, NCH // U)

            @block.scalar
            def _(act):
                def h_dst(n, k):
                    b, q = half(n, k)
                    c = k * 4 + n
                    act.wait_ge(old_ld[b], q * 16 + 16)
                    at_least(act, xh, c - 1)
                    for g in range(G):
                        col = bass.ds(c * G + g, 1)
                        last = act.activation(HD[b][:, g, :], OLD[b][:, g, :], ACT.Relu, bias=NMR[:, col], scale=RSD[:, col])
                    last.then_inc(hd, 1)

                def root(n, k):
                    b, q = half(n, k)
                    c = k * 4 + n
                    act.wait_ge(qq, c + 1)
                    at_least(act, sd, c)
                    for g in range(G):
                        last = act.activation(SQ[:, g, :], QL[b][:, g, :], ACT.Square, accum_out=SS[:, g:g + 1])
                    last.then_inc(sq, 1)
                    at_least(act, rz, c)
                    act.wait_ge(sq, c + 1)
                    act.activation(SD[:, 0:4], SS, ACT.Sqrt, bias=epsc[:, 0:1], scale=1.0 / F).then_inc(sd, 1)

                def body(k, j):
                    b, q = half(j, k)
                    c = k * 4 + j
                    if known(j, k) != 0:
                        h_dst(j - 1, k)
                    act.wait_ge(sp_, c + 1)
                    at_least(act, qq, c - 1)
                    act.activation(SO[b][:, :], BK[2 + b][:, :], ACT.Copy).then_inc(so, 1)
                    if known(j, k) != 0:
                        root(j - 1, k)

                chunks(act, body)
                h_dst(0, NCH // U)
                root(0, NCH // U)

            @block.vector
            def _(dve):
                def scan(n, k):
                    b, q = half(n, k)
                    c = k * 4 + n
                    first = known(n, k) == 0
                    dve.wait_ge(mp, c + 1)
                    dve.wait_ge(cu_ld[b], q * 16 + 16)
                    at_least(dve, sm, c - 1)
                    if not first:
                        dve.wait_ge(ag, c)
                    dve.tensor_tensor_scan(AG[b], CU[b], BK[b][:, :], 0.0 if first else AG[1 - b][:, CH - 1:CH],
                                           ALU.mult, ALU.add).then_inc(ag, 1)

                def scale(n, k):
                    b, q = half(n, k)
                    c = k * 4 + n
                    dve.wait_ge(sd, c + 1)
                    dve.reciprocal(RZ[:, 0:4], SD[:, 0:4]).then_inc(rz, 1)
                    at_least(dve, sc[b], q * 64)
                    dve.wait_ge(rz, c + 1)
                    for g in range(G):
                        last = dve.scalar_tensor_tensor(NEW[b][:, g, :], QL[b][:, g, :], RZ[:, g:g + 1],
                                                        g3c, ALU.mult, ALU.mult)
                    last.then_inc(o, 1)

                def finish(n, k):
                    b, q = half(n, k)
                    c = k * 4 + n
                    dve.wait_ge(o, c + 1)
                    dve.tensor_tensor(NEW[b], NEW[b], be3b[:, :].unsqueeze(1).broadcast_to([P, G, F]), ALU.add).then_inc(nb, 1)
                    dve.wait_ge(nb, c + 1)
                    dve.wait_ge(xh, c + 1)
                    dve.scalar_tensor_tensor(NEW[b], NEW[b], 0.0, OLD[b], ALU.max, ALU.add).then_inc(nw, 1)

                def body(k, j):
                    b, q = half(j, k)
                    c = k * 4 + j
                    late = known(j, k) not in (0, 1)
                    if known(j, k) != 0:
                        scan(j - 1, k)
                    dve.wait_ge(ab_ld[b], q * 64 + 64)
                    for h in range(H):
                        dve.tensor_tensor(AB[b][:, h, :], AB[b][:, h, :], HT[:, bass.ds(c * CH, CH)], ALU.mult).then_inc(gs, 1)
                    dve.wait_ge(sb_ld[b], q * 80 + 80)
                    for h in range(H):
                        dve.tensor_tensor(SB[b][h], SB[b][h], UD[b], ALU.mult).then_inc(gd, 1)
                    if late:
                        scale(j - 2, k)
                        finish(j - 2, k)

                chunks(dve, body)
                scan(0, NCH // U)
                for n in (-1, 0):
                    scale(n, NCH // U)
                    finish(n, NCH // U)

            @block.gpsimd
            def _(pool):
                def scatter(n, k):
                    b, q = half(n, k)
                    c = k * 4 + n
                    at_least(pool, sc[b], q * 64)
                    pool.tensor_copy(IC[b][:, 0:4], ENDO[:, bass.ds(c * G, G)]).then_inc(ic, 1)
                    pool.wait_ge(ic, c + 1)
                    pool.wait_ge(nw, c + 1)
                    settle(pool, turns["pool"])
                    for g in range(G):
                        pool.indirect_dma_start(
                            out=out, out_offset=bass.IndirectOffsetOnAxis(ap=IC[b][:, g:g + 1], axis=0),
                            in_=NEW[b][:, g, :], in_offset=None, bounds_check=N - 1, oob_is_err=False).then_inc(sc[b], 16)

                def add(n, k):
                    b, q = half(n, k)
                    c = k * 4 + n
                    pool.wait_ge(hd, c + 1)
                    pool.tensor_tensor(OLD[b], OLD[b], HD[b], ALU.add).then_inc(xh, 1)
                    pool.wait_ge(so, c + 1)
                    pool.wait_ge(ag, c + 1)
                    pool.tensor_tensor(SO[b][:, :], SO[b][:, :], AG[b], ALU.add).then_inc(sm, 1)

                def body(k, j):
                    if known(j, k) != 0:
                        add(j - 1, k)
                    if known(j, k) not in (0, 1):
                        scatter(j - 2, k)

                chunks(pool, body)
                add(0, NCH // U)
                scatter(-1, NCH // U)
                scatter(0, NCH // U)
                pool.wait_ge(sc[0], 64 * ((NCH + 1) // 2))
                pool.wait_ge(sc[1], 64 * (NCH // 2))

    phase_last()


_INS = ['x', 'src', 'dst', 'edge_attr_64', 'edge_type_8', 'L0_gnn_W', 'L0_gnn_att_src', 'L0_gnn_att_dst',
        'L0_gnn_bias', 'L1_gnn_W_node', 'L1_gnn_W_edge', 'L1_gnn_a', 'L2_gnn_W', 'L2_gnn_b', 'L2_gnn_gamma',
        'L2_gnn_beta', 'L3_gnn_W', 'L3_gnn_att_src', 'L3_gnn_att_dst', 'L3_gnn_bias', 'L3_gnn_ln_gamma',
        'L3_gnn_ln_beta']


def kernel(**inputs):
    import numpy as _np
    import concourse.bacc as _bacc
    from concourse import mybir as _mybir
    from concourse.bass_utils import run_bass_kernel_spmd as _run

    nc = _bacc.Bacc("TRN2", target_bir_lowering=False, num_devices=1)
    arrays, args = {}, []
    for name in _INS:
        a = _np.ascontiguousarray(inputs[name])
        arrays[f"in_{name}_dram"] = a
        args.append(nc.dram_tensor(f"in_{name}_dram", a.shape, _mybir.dt.from_np(a.dtype), kind="ExternalInput").ap())
    out = nc.dram_tensor("out_0_dram", (N, F), _mybir.dt.float32, kind="ExternalOutput").ap()
    program(nc, *args, out)
    r = _run(nc, [arrays], core_ids=[0])
    return r.results[0]["out_0_dram"]
```
